# Optimizing a Trainium2 kernel written in Bass

```python
import numpy as np
import jax
import jax.numpy as jnp

def _softmax(x, axis=-1):
    return jax.nn.softmax(x, axis=axis)

def _gelu(x):
    return jax.nn.gelu(x, approximate=True)

def _silu(x):
    return jax.nn.silu(x)

def _sigmoid(x):
    return jax.nn.sigmoid(x)

def _layernorm(x, axis=-1, eps=1e-05):
    m = jnp.mean(x, axis=axis, keepdims=True)
    v = jnp.var(x, axis=axis, keepdims=True)
    return (x - m) / jnp.sqrt(v + eps)

def _scatter_add(tgt, idx, src, axis=0):
    return tgt.at[idx].add(src)

def _segment_sum(src, seg, n):
    return jax.ops.segment_sum(src, seg, n)
kernel_name = 'mk_xattn_ffn_d2_seqx_r8_c592ac'

def setup_inputs(seed: int=0):
    np.random.seed(seed)
    _w = jnp.asarray

    def _rec_inputs():
        import jax
        import jax.numpy as jnp
        _rk = jax.random.key(seed)
        x = -0.0003929 + 0.9999 * jax.random.normal(jax.random.fold_in(_rk, 1), (1, 1024, 128), jnp.float32)
        _lenS = 1024 - jax.random.randint(jax.random.fold_in(_rk, 7), (1,), 0, max(1, 1024 // 4) + 1, jnp.int32)
        _lenS2 = 6404 - jax.random.randint(jax.random.fold_in(_rk, 8), (1,), 0, max(1, 6404 // 4) + 1, jnp.int32)
        _ctx_768P = jax.random.normal(jax.random.fold_in(_rk, 11), (1, 16, 96), jnp.float32)
        _ctx_768c = jax.random.dirichlet(jax.random.fold_in(_rk, 511), 0.3 * jnp.ones((16,), jnp.float32), (1, 6404))
        _ctx_768t = jnp.einsum('bsk,bkd->bsd', _ctx_768c, _ctx_768P)
        _ctx_768t = _ctx_768t * jax.lax.rsqrt(jnp.mean(jnp.square(_ctx_768t)) + 1e-12) * 0.953939
        ctx_768 = -7.36909e-05 + 0.999899 * (_ctx_768t + 0.3 * jax.random.normal(jax.random.fold_in(_rk, 611), (1, 6404, 96), jnp.float32))
        return (x, ctx_768)
    x, ctx_768 = _rec_inputs()

    def _L0_xattn_setup():
        import jax, jax.numpy as jnp
        import numpy as np
        IMG_DIM, TXT_DIM, HID = (128, 96, 128)
        B, LQ, LK = (8, 256, 256)
        key = jax.random.key(seed)
        ks = jax.random.split(key, 8)
        s_img = 1.0 / np.sqrt(IMG_DIM)
        s_txt = 1.0 / np.sqrt(TXT_DIM)
        return {'image_features': jax.random.normal(ks[0], (B, LQ, IMG_DIM), jnp.float32), 'text_features': jax.random.normal(ks[1], (B, LK, TXT_DIM), jnp.float32), 'Wq': jax.random.uniform(ks[2], (IMG_DIM, HID), jnp.float32, -s_img, s_img), 'bq': jax.random.uniform(ks[3], (HID,), jnp.float32, -s_img, s_img), 'Wk': jax.random.uniform(ks[4], (TXT_DIM, HID), jnp.float32, -s_txt, s_txt), 'bk': jax.random.uniform(ks[5], (HID,), jnp.float32, -s_txt, s_txt), 'Wv': jax.random.uniform(ks[6], (TXT_DIM, HID), jnp.float32, -s_txt, s_txt), 'bv': jax.random.uniform(ks[7], (HID,), jnp.float32, -s_txt, s_txt)}
    _L0_xattn_all = _L0_xattn_setup()
    _L0_xattn_in = {k: v for k, v in _L0_xattn_all.items() if k in ('Wq', 'bq', 'Wk', 'bk', 'Wv', 'bv')}
    del _L0_xattn_all

    def _L0_ffn_setup():
        import jax, jax.numpy as jnp
        import numpy as np
        B, T, D, E, H = (8, 256, 128, 8, 32)
        LN_EPS = 1e-05
        key = jax.random.key(seed)
        ks = jax.random.split(key, 4)
        return {'x': jax.random.normal(ks[0], (B, T, D), dtype=jnp.float32), 'Wg': jax.random.normal(ks[1], (E, D), dtype=jnp.float32) * 0.02, 'ln_scale': jnp.ones((E, D), dtype=jnp.float32), 'ln_bias': jnp.zeros((E, D), dtype=jnp.float32), 'W1': jax.random.normal(ks[2], (E, D, H), dtype=jnp.float32) * 0.02, 'b1': jnp.zeros((E, H), dtype=jnp.float32), 'W2': jax.random.normal(ks[3], (E, H, D), dtype=jnp.float32) * 0.02, 'b2': jnp.zeros((E, D), dtype=jnp.float32)}
    _L0_ffn_all = _L0_ffn_setup()
    _L0_ffn_in = {k: v for k, v in _L0_ffn_all.items() if k in ('Wg', 'ln_scale', 'ln_bias', 'W1', 'b1', 'W2', 'b2')}
    del _L0_ffn_all

    def _L1_xattn_setup():
        import jax, jax.numpy as jnp
        import numpy as np
        QUERY_DIM = 128
        CONTEXT_DIM = 96
        HEADS = 8
        DIM_HEAD = 64
        INNER = HEADS * DIM_HEAD
        key = jax.random.key(seed)
        ks = jax.random.split(key, 7)
        B, S, L = (8, 512, 77)
        x = jax.random.normal(ks[0], (B, S, QUERY_DIM), dtype=jnp.float32)
        context = jax.random.normal(ks[1], (B, L, CONTEXT_DIM), dtype=jnp.float32)
        Wq = jax.random.normal(ks[2], (QUERY_DIM, INNER), dtype=jnp.float32) * QUERY_DIM ** (-0.5)
        Wk = jax.random.normal(ks[3], (CONTEXT_DIM, INNER), dtype=jnp.float32) * CONTEXT_DIM ** (-0.5)
        Wv = jax.random.normal(ks[4], (CONTEXT_DIM, INNER), dtype=jnp.float32) * CONTEXT_DIM ** (-0.5)
        Wo = jax.random.normal(ks[5], (INNER, QUERY_DIM), dtype=jnp.float32) * INNER ** (-0.5)
        bo = jax.random.normal(ks[6], (QUERY_DIM,), dtype=jnp.float32) * 0.01
        return {'x': x, 'context': context, 'Wq': Wq, 'Wk': Wk, 'Wv': Wv, 'Wo': Wo, 'bo': bo}
    _L1_xattn_all = _L1_xattn_setup()
    _L1_xattn_in = {k: v for k, v in _L1_xattn_all.items() if k in ('Wq', 'Wk', 'Wv', 'Wo', 'bo')}
    del _L1_xattn_all

    def _L1_ffn_setup():
        import jax, jax.numpy as jnp
        import numpy as np
        DIM = 128
        INTER = 64
        E = 32
        TOPK = 4
        GROUPS = 8
        TOPK_GROUPS = 4
        SHARED_INTER = 2 * INTER
        ROUTE_SCALE = 1.0
        B, S = (8, 512)

        def _gate(xf, gw, gb):
            T = xf.shape[0]
            scores = jax.nn.softmax((xf @ gw + gb).astype(jnp.float32), axis=-1)
            original_scores = scores
            scores_g = scores.reshape(T, GROUPS, E // GROUPS)
            group_scores = jnp.sum(jax.lax.top_k(scores_g, 2)[0], axis=-1)
            gidx = jax.lax.top_k(group_scores, TOPK_GROUPS)[1]
            keep = jnp.zeros((T, GROUPS), bool).at[jnp.arange(T)[:, None], gidx].set(True)
            masked = jnp.where(keep[:, :, None], scores_g, -jnp.inf).reshape(T, E)
            indices = jax.lax.top_k(masked, TOPK)[1]
            weights = jnp.take_along_axis(original_scores, indices, axis=1) * ROUTE_SCALE
            return (weights.astype(xf.dtype), indices)
        key = jax.random.key(seed)
        ks = jax.random.split(key, 16)

        def xav(k, shape):
            fan_in, fan_out = (shape[-2], shape[-1])
            lim = np.sqrt(6.0 / (fan_in + fan_out))
            return jax.random.uniform(k, shape, jnp.float32, -lim, lim)
        return {'x': jax.random.normal(ks[0], (B, S, DIM), jnp.float32), 'gw': xav(ks[1], (DIM, E)), 'gb': jnp.zeros((E,), jnp.float32), 'w1': xav(ks[2], (E, DIM, INTER)), 'b1': jnp.zeros((E, INTER), jnp.float32), 'w3': xav(ks[3], (E, DIM, INTER)), 'b3': jnp.zeros((E, INTER), jnp.float32), 'w2': xav(ks[4], (E, INTER, DIM)), 'b2': jnp.zeros((E, DIM), jnp.float32), 'sw1': xav(ks[5], (DIM, SHARED_INTER)), 'sb1': jnp.zeros((SHARED_INTER,), jnp.float32), 'sw3': xav(ks[6], (DIM, SHARED_INTER)), 'sb3': jnp.zeros((SHARED_INTER,), jnp.float32), 'sw2': xav(ks[7], (SHARED_INTER, DIM)), 'sb2': jnp.zeros((DIM,), jnp.float32)}
    _L1_ffn_all = _L1_ffn_setup()
    _L1_ffn_in = {k: v for k, v in _L1_ffn_all.items() if k in ('gw', 'gb', 'w1', 'b1', 'w3', 'b3', 'w2', 'b2', 'sw1', 'sb1', 'sw3', 'sb3', 'sw2', 'sb2')}
    del _L1_ffn_all
    return {'x': x, 'ctx_768': ctx_768, 'L0_xattn_Wq': _L0_xattn_in['Wq'], 'L0_xattn_bq': _L0_xattn_in['bq'], 'L0_xattn_Wk': _L0_xattn_in['Wk'], 'L0_xattn_bk': _L0_xattn_in['bk'], 'L0_xattn_Wv': _L0_xattn_in['Wv'], 'L0_xattn_bv': _L0_xattn_in['bv'], 'L0_ffn_Wg': _L0_ffn_in['Wg'], 'L0_ffn_ln_scale': _L0_ffn_in['ln_scale'], 'L0_ffn_ln_bias': _L0_ffn_in['ln_bias'], 'L0_ffn_W1': _L0_ffn_in['W1'], 'L0_ffn_b1': _L0_ffn_in['b1'], 'L0_ffn_W2': _L0_ffn_in['W2'], 'L0_ffn_b2': _L0_ffn_in['b2'], 'L1_xattn_Wq': _L1_xattn_in['Wq'], 'L1_xattn_Wk': _L1_xattn_in['Wk'], 'L1_xattn_Wv': _L1_xattn_in['Wv'], 'L1_xattn_Wo': _L1_xattn_in['Wo'], 'L1_xattn_bo': _L1_xattn_in['bo'], 'L1_ffn_gw': _L1_ffn_in['gw'], 'L1_ffn_gb': _L1_ffn_in['gb'], 'L1_ffn_w1': _L1_ffn_in['w1'], 'L1_ffn_b1': _L1_ffn_in['b1'], 'L1_ffn_w3': _L1_ffn_in['w3'], 'L1_ffn_b3': _L1_ffn_in['b3'], 'L1_ffn_w2': _L1_ffn_in['w2'], 'L1_ffn_b2': _L1_ffn_in['b2'], 'L1_ffn_sw1': _L1_ffn_in['sw1'], 'L1_ffn_sb1': _L1_ffn_in['sb1'], 'L1_ffn_sw3': _L1_ffn_in['sw3'], 'L1_ffn_sb3': _L1_ffn_in['sb3'], 'L1_ffn_sw2': _L1_ffn_in['sw2'], 'L1_ffn_sb2': _L1_ffn_in['sb2']}

def reference(x, ctx_768, L0_xattn_Wq, L0_xattn_bq, L0_xattn_Wk, L0_xattn_bk, L0_xattn_Wv, L0_xattn_bv, L0_ffn_Wg, L0_ffn_ln_scale, L0_ffn_ln_bias, L0_ffn_W1, L0_ffn_b1, L0_ffn_W2, L0_ffn_b2, L1_xattn_Wq, L1_xattn_Wk, L1_xattn_Wv, L1_xattn_Wo, L1_xattn_bo, L1_ffn_gw, L1_ffn_gb, L1_ffn_w1, L1_ffn_b1, L1_ffn_w3, L1_ffn_b3, L1_ffn_w2, L1_ffn_b2, L1_ffn_sw1, L1_ffn_sb1, L1_ffn_sw3, L1_ffn_sb3, L1_ffn_sw2, L1_ffn_sb2):
    import jax
    import jax.numpy as jnp

    def _L0_xattn_ref(image_features, text_features, Wq, bq, Wk, bk, Wv, bv):
        import jax, jax.numpy as jnp
        import numpy as np
        IMG_DIM, TXT_DIM, HID = (128, 96, 128)
        B, LQ, LK = (8, 256, 256)
        query = jnp.einsum('bqi,ih->bqh', image_features, Wq) + bq
        key = jnp.einsum('bkt,th->bkh', text_features, Wk) + bk
        value = jnp.einsum('bkt,th->bkh', text_features, Wv) + bv
        scale = 1.0 / jnp.sqrt(jnp.asarray(HID, query.dtype))
        scores = jnp.einsum('bqh,bkh->bqk', query, key) * scale
        weights = jax.nn.softmax(scores, axis=-1)
        attended = jnp.einsum('bqk,bkh->bqh', weights, value)
        return attended

    def _L0_ffn_ref(x, Wg, ln_scale, ln_bias, W1, b1, W2, b2):
        import jax, jax.numpy as jnp
        import numpy as np
        B, T, D, E, H = (8, 256, 128, 8, 32)
        LN_EPS = 1e-05
        Bs, Ts, Ds = x.shape
        xt = x.reshape(Bs * Ts, Ds)
        logits = xt @ Wg.T
        top1 = jnp.argmax(logits, axis=-1)
        mu = jnp.mean(xt, axis=-1, keepdims=True)
        var = jnp.mean(jnp.square(xt - mu), axis=-1, keepdims=True)
        xhat = (xt - mu) * jax.lax.rsqrt(var + LN_EPS)
        n_experts = Wg.shape[0]

        def body(y, p):
            s_e, b_e, w1, bb1, w2, bb2, eid = p
            h = jax.nn.gelu((xhat * s_e + b_e) @ w1 + bb1, approximate=False)
            out = h @ w2 + bb2
            mask = (top1 == eid)[:, None].astype(out.dtype)
            return (y + mask * out, None)
        y0 = jnp.zeros_like(xt)
        y, _ = jax.lax.scan(body, y0, (ln_scale, ln_bias, W1, b1, W2, b2, jnp.arange(n_experts)))
        return y.reshape(Bs, Ts, Ds)

    def _L1_xattn_ref(x, context, Wq, Wk, Wv, Wo, bo):
        import jax, jax.numpy as jnp
        import numpy as np
        QUERY_DIM = 128
        CONTEXT_DIM = 96
        HEADS = 8
        DIM_HEAD = 64
        INNER = HEADS * DIM_HEAD
        B, S, _ = x.shape
        L = context.shape[1]
        scale = DIM_HEAD ** (-0.5)
        q = (x @ Wq).reshape(B, S, HEADS, DIM_HEAD).transpose(0, 2, 1, 3)
        k = (context @ Wk).reshape(B, L, HEADS, DIM_HEAD).transpose(0, 2, 1, 3)
        v = (context @ Wv).reshape(B, L, HEADS, DIM_HEAD).transpose(0, 2, 1, 3)
        attn = jnp.einsum('bhsd,bhld->bhsl', q, k) * scale
        attn = jax.nn.softmax(attn, axis=-1)
        out = jnp.einsum('bhsl,bhld->bhsd', attn, v)
        out = out.transpose(0, 2, 1, 3).reshape(B, S, INNER)
        return out @ Wo + bo

    def _L1_ffn_ref(x, gw, gb, w1, b1, w3, b3, w2, b2, sw1, sb1, sw3, sb3, sw2, sb2):
        import jax, jax.numpy as jnp
        import numpy as np
        DIM = 128
        INTER = 64
        E = 32
        TOPK = 4
        GROUPS = 8
        TOPK_GROUPS = 4
        SHARED_INTER = 2 * INTER
        ROUTE_SCALE = 1.0
        B, S = (8, 512)

        def _gate(xf, gw, gb):
            T = xf.shape[0]
            scores = jax.nn.softmax((xf @ gw + gb).astype(jnp.float32), axis=-1)
            original_scores = scores
            scores_g = scores.reshape(T, GROUPS, E // GROUPS)
            group_scores = jnp.sum(jax.lax.top_k(scores_g, 2)[0], axis=-1)
            gidx = jax.lax.top_k(group_scores, TOPK_GROUPS)[1]
            keep = jnp.zeros((T, GROUPS), bool).at[jnp.arange(T)[:, None], gidx].set(True)
            masked = jnp.where(keep[:, :, None], scores_g, -jnp.inf).reshape(T, E)
            indices = jax.lax.top_k(masked, TOPK)[1]
            weights = jnp.take_along_axis(original_scores, indices, axis=1) * ROUTE_SCALE
            return (weights.astype(xf.dtype), indices)
        shape = x.shape
        xf = x.reshape(-1, DIM)
        T = xf.shape[0]
        weights, indices = _gate(xf, gw, gb)
        cw = jnp.zeros((T, E), xf.dtype).at[jnp.arange(T)[:, None], indices].add(weights)

        def body(y, p):
            w1e, b1e, w3e, b3e, w2e, b2e, we = p
            h = jax.nn.silu(xf @ w1e + b1e) * (xf @ w3e + b3e)
            return (y + we[:, None] * (h @ w2e + b2e), None)
        y0 = jnp.zeros_like(xf)
        y, _ = jax.lax.scan(body, y0, (w1, b1, w3, b3, w2, b2, cw.T))
        z = jax.nn.silu(xf @ sw1 + sb1) * (xf @ sw3 + sb3) @ sw2 + sb2
        return (y + z).reshape(shape)
    x = x + _L0_xattn_ref(_layernorm(x, axis=-1), ctx_768, L0_xattn_Wq, L0_xattn_bq, L0_xattn_Wk, L0_xattn_bk, L0_xattn_Wv, L0_xattn_bv)
    x = x + _L0_ffn_ref(_layernorm(x, axis=-1), L0_ffn_Wg, L0_ffn_ln_scale, L0_ffn_ln_bias, L0_ffn_W1, L0_ffn_b1, L0_ffn_W2, L0_ffn_b2)
    x = x + _L1_xattn_ref(_layernorm(x, axis=-1), ctx_768, L1_xattn_Wq, L1_xattn_Wk, L1_xattn_Wv, L1_xattn_Wo, L1_xattn_bo)
    x = x + _L1_ffn_ref(_layernorm(x, axis=-1), L1_ffn_gw, L1_ffn_gb, L1_ffn_w1, L1_ffn_b1, L1_ffn_w3, L1_ffn_b3, L1_ffn_w2, L1_ffn_b2, L1_ffn_sw1, L1_ffn_sb1, L1_ffn_sw3, L1_ffn_sb3, L1_ffn_sw2, L1_ffn_sb2)
    return x

_drawn_inputs = setup_inputs


def setup_inputs(seed=0):
    import zlib

    import numpy as np

    out = dict(_drawn_inputs(seed))
    spreads = {'L0_ffn_ln_scale': (1.0, 0.6),
     'L0_ffn_ln_bias': (0.0, 0.8),
     'L0_ffn_b1': (0.0, 0.8),
     'L0_ffn_b2': (0.0, 0.1),
     'L1_ffn_gb': (0.0, 0.292),
     'L1_ffn_b1': (0.0, 0.6),
     'L1_ffn_b3': (0.0, 0.625),
     'L1_ffn_b2': (0.0, 0.35),
     'L1_ffn_sb1': (0.0, 0.1),
     'L1_ffn_sb3': (0.0, 0.1),
     'L1_ffn_sb2': (0.0, 0.1)}
    factors = {'L0_xattn_bq': 8.0,
     'L0_xattn_bk': 8.0,
     'L0_ffn_W1': 3.543,
     'L0_ffn_W2': 3.303,
     'L1_xattn_bo': 4.57}
    for name, (base, spread) in spreads.items():
        noise = np.random.default_rng([zlib.crc32(name.encode()), seed]).standard_normal(out[name].shape)
        drawn = base * np.exp(spread * noise) if base else spread * noise
        out[name] = jnp.asarray(drawn.astype(out[name].dtype))
    for name, factor in factors.items():
        out[name] = (out[name] * factor).astype(out[name].dtype)
    return out
```

```python
from contextlib import ExitStack

import concourse.bass as bass
from concourse import mybir

F32 = mybir.dt.float32
F32R = mybir.dt.float32r
BF16 = mybir.dt.bfloat16
U32 = mybir.dt.uint32
ALU = mybir.AluOpType
ACT = mybir.ActivationFunctionType
AX = mybir.AxisListType.X

P = 128
TOK = 1024
TT = TOK // P
HALF = TOK // 2
D = 128
KEYS = 6404
CD = 96
KT = 126
TILES = 51
CH = 3
CHUNKS = TILES // CH
CK = CH * KT
PADDED = TILES * KT
PAD_AT = KEYS - (TILES - 1) * KT
HEADS = 8
HD = 64
E0, H0 = 8, 32
EG0 = P // H0
G0 = E0 // EG0
E1, H1 = 32, 64
G1 = E1 * H1 // P
GROUPS, TOPK, TOPG = 8, 4, 4
EPS = 1e-5
PAD_SCORE = -1e30
PAIR_W = 3 * P + 2
B_S, B_MX, B_KP, B_ACC, B_AUX = 0, 3, 5, 6, 7


def build_program(nc, x, ctx_rows, ctx_t, a_wq, a_bq, a_wkt, a_bk, a_wv, a_bv,
                  f0_wgt, f0_scale, f0_bias, f0_w1, f0_b1, f0_w2, f0_b2,
                  c_wq_in, c_wk_in, c_wv_in, c_wo_in, c_bo_in,
                  f1_gw, f1_gb, f1_pairs, f1_b2, f1_sb2,
                  ident_in, iota_in, spread0_in, spread1_in, out_t):
    with ExitStack() as ctx:
        def sb(name, shape, dt=F32):
            return ctx.enter_context(nc.sbuf_tensor(name, shape, dt))

        def sem(name):
            return ctx.enter_context(nc.semaphore(name))

        def sems(name, n):
            return [sem(f"{name}{i}") for i in range(n)]

        v_dram = nc.dram_tensor("v_scratch", [HEADS, KT, TILES * HD], F32, kind="Internal").ap()

        ps = ctx.enter_context(nc.psum_tensor("ps", [P, 8, HALF], F32))

        ident = sb("ident", [P, P])
        neg_ident = sb("neg_ident", [P, P])
        ones = sb("ones", [P, P])
        iota = sb("iota", [P, E1])
        eps_col = sb("eps_col", [P, 1])
        zero_col = sb("zero_col", [P, 1])
        x_tok = sb("x_tok", [P, TT, D])
        xn = sb("xn", [P, TT, D])
        xn2 = sb("xn2", [P, TT, D])
        xn_t = sb("xn_t", [P, TOK])
        stats = sb("stats", [P, TT, 6])
        mean_var = sb("mean_var", [P, TT, 2])
        std = sb("std", [P, TT])
        rstd = sb("rstd", [P, TT])
        ctx_mem = sb("ctx_mem", [P, PADDED])
        ctx_f = ctx_mem[0:CD, :]
        keys_hl = sb("keys_hl", [P, TILES, 2, KT], F32R)
        kslot = sb("kslot", [P, CH, 2, KT], F32R)
        vslot = sb("vslot", [KT, CH, P])
        probs = sb("probs", [KT, CH, TOK])
        q_max = sb("q_max", [P, TOK], F32R)
        q_all = sb("q_all", [P, TOK], F32R)
        q_shift = sb("q_shift", [97, TOK], F32R)
        q_pad = sb("q_pad", [97, TOK], F32R)
        chunk_max = sb("chunk_max", [P, TT, CHUNKS])
        row_max = sb("row_max", [P, TT])
        v_mem = sb("v_mem", [P, 2 * TILES * HD])
        v_head = v_mem[0:KT, :].rearrange("p (b f) -> p b f", b=2)
        wq0 = sb("wq0", [P, D])
        bq0 = sb("bq0", [P, 1])
        wkt0 = sb("wkt0", [P, CD + 1])
        wv0 = sb("wv0", [CD + 1, D + 1])
        q0_t = v_mem[:, 0:TOK]
        o0 = v_mem[0:CD + 1, TOK:2 * TOK]
        rsum0 = sb("rsum0", [P, 4, 2])
        wv1_f = v_mem[0:CD, 2 * TOK:2 * TOK + HEADS * HD]
        wv1_hi = sb("wv1_hi", [CD, HEADS * HD], F32R)
        wv1_lo = sb("wv1_lo", [CD, HEADS * HD], F32R)
        sum_mem = sb("sum_mem", [KT, TOK + HALF])
        v_stage = sum_mem[:, :].rearrange("p (j f) -> p j f", j=CH)
        wq1 = sb("wq1", [P, P])
        wk1 = sb("wk1", [CD, P])
        wo1 = sb("wo1", [P, HEADS, D])
        wo_slot = sb("wo_slot", [P, D])
        bo1 = sb("bo1", [1, D])
        psum_pool = sum_mem[:, 0:TOK]
        psum_dve = sum_mem[:, TOK:TOK + HALF]
        acc_raw = sb("acc_raw", [P, HALF])
        rden = sb("rden", [P, HALF])
        acc_norm = sb("acc_norm", [P, HALF])

        in_x, in_a, in_wv, in_f0, in_c, in_f1 = (sem(f"in_{n}") for n in ("x", "a", "wv", "f0", "c", "f1"))
        in_ctx = sems("in_ctx", CH)
        consts, neg_ready = sem("consts"), sem("neg_ready")
        ln_stats, ln_var, ln_std, ln_rstd, ln_out = (sem(f"ln_{n}") for n in ("stats", "var", "std", "rstd", "out"))
        tr_psum, tr_act, tr_dve = sem("tr_psum"), sem("tr_act"), sem("tr_dve")
        max_scored, max_reduced = sems("max_scored", TT), sems("max_reduced", TT)
        slot_keys, attended = sems("slot_keys", CH), sems("attended", CH)
        scored, exped = sems("scored", 2 * CH), sems("exped", 2 * CH)
        max_found, max_row, shifted = sem("max_found"), sem("max_row"), sem("shifted")
        a_q, a_qsb, a_qk, a_qhi, a_qlo, a_rows, a_chi, a_clo, a_wvs, a_qcopy, a_acczero, a_o, a_out, a_rsum, a_x = (
            sem(f"a_{n}") for n in ("q", "qsb", "qk", "qhi", "qlo", "rows", "chi", "clo", "wvs", "qcopy", "acczero",
                                    "o", "out", "rsum", "x"))
        a_cslot, a_vproj, a_vevac, a_vout = (sems(f"a_{n}", CH) for n in ("cslot", "vproj", "vevac", "vout"))
        f_logits, f_step, f_mask, f_w, f_bias, f_biassb, f_hid, f_gelu, f_maskt, f_masktsb, f_spread, f_masked, f_out, f_x = (
            sem(f"f_{n}") for n in ("logits", "step", "mask", "w", "bias", "biassb", "hid", "gelu", "maskt", "masktsb",
                                    "spread", "masked", "out", "x"))
        c_rows, c_wq, c_wk, c_vload, c_qproj, c_qhi, c_qlo, c_qcopy, c_kp, c_khi, c_klo = (
            sem(f"c_{n}") for n in ("rows", "wq", "wk", "vload", "qproj", "qhi", "qlo", "qcopy", "kp", "khi", "klo"))
        c_qcopy0, c_pzero, c_dadd, c_dzero, c_acc, c_acczero, c_sums, c_rden, c_norm, c_out, c_x = (
            sem(f"c_{n}") for n in ("qcopy0", "pzero", "dadd", "dzero", "acc", "acczero", "sums", "rden", "norm", "out", "x"))
        c_vslot, c_padd = sems("c_vslot", CH), sems("c_padd", CH)
        g_step, g_logits, g_exp, g_cw, g_cwt, g_cwtsb, g_spread_ready, g_store = (
            sem(f"g_{n}") for n in ("step", "logits", "exp", "cw", "cwt", "cwtsb", "spread_ready", "store"))
        g_w, g_u, g_silu, g_h, g_gate, g_hg, g_y, g_fin = (
            sems(f"g_{n}", 2) for n in ("w", "u", "silu", "h", "gate", "hg", "y", "fin"))

        f0w = sb("f0w", [P, 3 * 256 + 8 * 3 + 2 + 2 + 8 * 8])
        w1_in = f0w[:, 0:256]
        w1s = f0w[:, 256:512]
        w1b = f0w[:, 512:768]
        sc0 = f0w[:, 768:776]
        bi0 = f0w[:, 776:784]
        wgt = f0w[:, 784:792]
        b1_0 = f0w[:, 792:794]
        hb0 = f0w[:, 794:796]
        lg0 = f0w[:, 796:860]
        w2_0 = sb("w2_0", [P, G0, D])
        b2_0 = sb("b2_0", [E0, D])
        spread0 = sb("spread0", [E0, G0, P])
        mask0 = sb("mask0", [P, TT, E0])
        top8 = sb("top8", [P, TT, 8])
        idx8 = sb("idx8", [P, TT, 8], U32)
        idxf8 = sb("idxf8", [P, TT, 8])
        mask_t = v_mem[0:E0, 5 * TOK:6 * TOK]
        hid0 = v_mem[:, 3 * TOK:5 * TOK].rearrange("p (g t) -> p g t", g=G0)

        gw = sb("gw", [P, E1])
        gb = sb("gb", [1, E1])
        b2_1 = sb("b2_1", [E1, D])
        sb2 = sb("sb2", [P, 1])
        spread1 = sb("spread1", [3 * E1, G1, P], BF16)
        used = [0]

        def over_ctx(*shape):
            n, at = 1, used[0]
            for m in shape:
                n *= m
            used[0] += n
            flat = ctx_mem[:, at:at + n]
            return flat.rearrange("p (a b) -> p a b", a=shape[0]) if len(shape) == 2 else flat

        gl, gp, cw = over_ctx(TT, E1), over_ctx(TT, E1), over_ctx(TT, E1)
        gm, gs = over_ctx(TT), over_ctx(TT)
        pmax, pmin, qmax, qmin, keep = (over_ctx(TT, GROUPS) for _ in range(5))
        cw_t, cw_r = over_ctx(TOK)[0:E1, :], over_ctx(TOK)[0:E1, :]
        x3_t = over_ctx(TOK)
        cw_b = sb("cw_b", [E1, TOK], BF16)
        cw_3 = sb("cw_3", [3 * E1, TOK], BF16)
        pair_w = sb("pair_w", [P, 2, PAIR_W])
        silu = sb("silu", [P, 2, HALF])
        hgate = sb("hgate", [P, 2, HALF])
        block = ctx.enter_context(nc.Block())

        crow_v = ctx_rows.rearrange("(n p) c -> n p c", p=KT)
        v_dram_v = v_dram.rearrange("h p (n d) -> p h n d", n=TILES)

        def f32(ap):
            return ap.bitcast(F32)

        def halves(ap):
            return ap.rearrange("p (a b) -> p a b", a=2)

        def cols(half):
            return slice(half * HALF, (half + 1) * HALF)

        def tile_cols(t):
            return slice(t * P, (t + 1) * P)

        @block.sync
        def _(sp):
            sp.dma_start(x_tok[:, :, :], x.rearrange("(t p) d -> p t d", p=P)).then_inc(in_x, 16)
            sp.dma_start(ident[:, :], ident_in).then_inc(in_x, 16)
            for dst, src in ((wq0[:, :], a_wq), (bq0[:, :], a_bq), (wkt0[:, 0:CD], a_wkt), (wkt0[:, CD:CD + 1], a_bk),
                             (wv0[0:CD, 0:D], a_wv), (wv0[CD:CD + 1, 0:D], a_bv)):
                sp.dma_start(dst, src).then_inc(in_a, 16)
            for q in range(CH):
                part = slice(q * CHUNKS * KT, (q + 1) * CHUNKS * KT)
                sp.dma_start(ctx_f[:, part], ctx_t[:, part]).then_inc(in_ctx[q], 16)
            sp.dma_start(wv1_f, c_wv_in).then_inc(in_wv, 16)
            for dst, src in ((w1_in, f0_w1), (sc0, f0_scale), (bi0, f0_bias), (wgt, f0_wgt), (b1_0, f0_b1),
                             (w2_0[:, :, :], f0_w2), (b2_0[:, :], f0_b2), (spread0[:, :, :], spread0_in),
                             (iota[:, :], iota_in)):
                sp.dma_start(dst, src).then_inc(in_f0, 16)
            for dst, src in ((wo1[:, :, :], c_wo_in), (bo1[:, :], c_bo_in),
                             (wq1[:, :], c_wq_in[0]), (wk1[:, :], c_wk_in[0])):
                sp.dma_start(dst, src).then_inc(in_c, 16)
            for dst, src in ((gw[:, :], f1_gw), (gb[:, :], f1_gb), (b2_1[:, :], f1_b2),
                             (sb2[:, :], f1_sb2), (spread1[:, :, :], spread1_in)):
                sp.dma_start(dst, src).then_inc(in_f1, 16)
            for s in range(2):
                sp.dma_start(pair_w[:, s, :], f1_pairs[s]).then_inc(g_w[s], 16)
            for j in range(CH):
                sp.dma_start(vslot[:, j, 0:CD], crow_v[j]).then_inc(a_cslot[j], 16)

            def store_v(g, j, k1):
                sp.wait_ge(a_vevac[j], k1)
                sp.dma_start(v_dram_v[:, :, bass.ds(g * CH + j, 1), :],
                             v_stage[:, j, :].rearrange("p (h a d) -> p h a d", h=HEADS, a=1)).then_inc(a_vout[j], 16)

            with sp.Fori(0, CHUNKS - 1) as g:
                k1 = sp.snap(g + 1)
                for j in range(CH):
                    store_v(g, j, k1)
                    sp.wait_ge(attended[j], k1)
                    sp.dma_start(vslot[:, j, 0:CD],
                                 crow_v[bass.ds(g * CH + CH + j, 1)].rearrange("a p c -> p (a c)")).then_inc(a_cslot[j], 16)
            for j in range(CH):
                store_v(CHUNKS - 1, j, CHUNKS)
            for j in range(CH):
                sp.wait_ge(a_vout[j], 16 * CHUNKS)
            sp.wait_ge(f_x, 1)
            sp.dma_start(v_head[:, 0, :], v_dram[0]).then_inc(c_vload, 16)
            sp.wait_ge(c_qproj, 1)
            sp.dma_start(wq1[:, :], c_wq_in[1]).then_inc(c_wq, 16)
            sp.wait_ge(c_kp, CHUNKS)
            sp.dma_start(wk1[:, :], c_wk_in[1]).then_inc(c_wk, 16)

            def load_v(h):
                sp.wait_ge(c_vslot[CH - 1], h * CHUNKS + 1)
                sp.dma_start(v_head[:, bass.ds((h + 1) % 2, 1), :],
                             v_dram[bass.ds(h + 1, 1)].rearrange("h p f -> p h f")).then_inc(c_vload, 16)

            with sp.Fori(0, HEADS - 2) as h:
                load_v(h)
                sp.wait_ge(c_qproj, h + 2)
                sp.dma_start(wq1[:, :], c_wq_in[bass.ds(h + 2, 1)].rearrange("a p c -> p (a c)")).then_inc(c_wq, 16)
                sp.wait_ge(c_kp, (h + 2) * CHUNKS)
                sp.dma_start(wk1[:, :], c_wk_in[bass.ds(h + 2, 1)].rearrange("a p c -> p (a c)")).then_inc(c_wk, 16)
            load_v(HEADS - 2)
            with sp.Fori(0, G1 // 2 - 1) as i:
                k1 = sp.snap(2 * i + 1)
                for s in range(2):
                    for half in range(2):
                        sp.wait_ge(g_y[half], k1 + s)
                    sp.dma_start(pair_w[:, s, :],
                                 f1_pairs[bass.ds(2 * i + 2 + s, 1)].rearrange("a p c -> p (a c)")).then_inc(g_w[s], 16)
            for half in range(2):
                sp.wait_ge(g_y[half], G1 - 1)
            sp.dma_start(pair_w[:, 0, :], f1_pairs[G1]).then_inc(g_w[0], 16)
            for half in range(2):
                sp.wait_ge(g_fin[half], 1)
                sp.dma_start(out_t[:, cols(half)], x3_t[:, cols(half)]).then_inc(g_store, 16)
            sp.wait_ge(g_store, 32)

        @block.gpsimd
        def _(pool):
            pool.memset(ones[:, :], 1.0).then_inc(consts, 1)
            pool.wait_ge(consts, 1)
            pool.memset(eps_col[:, :], EPS).then_inc(consts, 1)
            pool.wait_ge(consts, 2)
            pool.memset(zero_col[:, :], 0.0).then_inc(consts, 1)
            pool.wait_ge(consts, 3)
            pool.memset(vslot[:, :, CD:CD + 1], 1.0).then_inc(a_rows, 1)
            pool.wait_ge(a_rows, 1)
            pool.memset(f32(q_pad[CD:CD + 1, :]), PAD_SCORE).then_inc(a_rows, 1)
            pool.wait_ge(a_rows, 2)
            pool.memset(wv0[:, D:D + 1], 0.0).then_inc(a_rows, 1)
            pool.wait_ge(a_rows, 3)
            pool.memset(wv0[CD:CD + 1, D:D + 1], 1.0).then_inc(a_rows, 1)
            pool.wait_ge(a_rows, 4)
            pool.memset(f32(keys_hl[CD:CD + 1, :, 0, :]), 1.0).then_inc(a_rows, 1)
            pool.wait_ge(a_rows, 5)
            pool.memset(f32(keys_hl[CD:P, :, 1, :]), 0.0).then_inc(a_rows, 1)
            pool.wait_ge(a_rows, 6)
            pool.memset(f32(keys_hl[CD:CD + 1, TILES - 1, 1, PAD_AT:KT]), 1.0).then_inc(a_rows, 1)
            pool.wait_ge(a_rows, 7)
            pool.wait_ge(a_qhi, 1)
            pool.tensor_copy(q_shift[0:CD, :], f32(q_max[0:CD, :])).then_inc(a_qcopy, 1)
            pool.wait_ge(a_qcopy, 1)
            pool.tensor_copy(q_pad[0:CD, :], f32(q_max[0:CD, :])).then_inc(a_qcopy, 1)
            pool.wait_ge(a_qcopy, 2)
            pool.wait_ge(slot_keys[CH - 1], CHUNKS)
            pool.memset(f32(keys_hl[HD:CD, :, 1, :]), 0.0).then_inc(c_rows, 1)
            pool.wait_ge(c_rows, 1)
            pool.memset(f32(keys_hl[HD:HD + 1, :, 1, :]), 1.0).then_inc(c_rows, 1)
            pool.wait_ge(c_rows, 2)
            pool.wait_ge(scored[2 * CH - 1], CHUNKS)
            pool.memset(f32(q_shift[HD:CD, :]), 0.0).then_inc(c_rows, 1)
            pool.wait_ge(c_rows, 3)
            pool.memset(f32(q_shift[CD:CD + 1, :]), PAD_SCORE).then_inc(c_rows, 1)
            pool.wait_ge(c_rows, 4)

            def sum_chunk(h1, k1, k, both1):
                pool.wait_ge(c_pzero, h1)
                for j in range(CH):
                    width = HALF if j == CH - 1 else TOK
                    pool.wait_ge(exped[2 * j], both1)
                    if j < CH - 1:
                        pool.wait_ge(exped[2 * j + 1], both1)
                    pool.wait_ge(c_padd[(j - 1) % CH], k1 if j else k)
                    pool.tensor_tensor(psum_pool[:, 0:width], psum_pool[:, 0:width], probs[:, j, 0:width],
                                       ALU.add).then_inc(c_padd[j], 1)

            zeros = zero_col[0:KT, :].to_broadcast([KT, TOK])

            def sum_head(h):
                pool.wait_ge(c_sums, h)
                pool.tensor_tensor(psum_pool, zeros, zeros, ALU.add).then_inc(c_pzero, 1)
                h1 = pool.snap(h + 1)
                with pool.Fori(0, CHUNKS) as g:
                    k = pool.snap(h * CHUNKS + g)
                    sum_chunk(h1, pool.snap(k + 1), k, pool.snap(k + (CHUNKS + 1)))

            pool.wait_ge(consts, 3)
            for j in range(CH):
                pool.wait_ge(a_vout[j], 16 * CHUNKS)
            with pool.Fori(0, HEADS) as h:
                sum_head(h)

        @block.scalar
        def _(act):
            def std_of(n):
                if n == 0:
                    act.wait_ge(consts, 3)
                act.wait_ge(ln_var, n + 1)
                act.activation(std[:, :], mean_var[:, :, 1], ACT.Sqrt, bias=eps_col[:, :]).then_inc(ln_std, 1)

            def turned(n, dst):
                act.wait_ge(tr_psum, 2 * n + 1)
                act.copy(dst[:, 0:HALF], ps[:, 6, :]).then_inc(tr_act, 1)

            for q in range(CH):
                part = slice(q * CHUNKS, (q + 1) * CHUNKS)
                act.wait_ge(in_ctx[q], 16)
                act.copy(keys_hl[0:CD, part, 0, :],
                         ctx_f.rearrange("p (n k) -> p n k", k=KT)[:, part, :]).then_inc(a_chi, 1)
                if q == 0:
                    std_of(0)
                    turned(0, xn_t)
            act.wait_ge(in_wv, 16)
            act.copy(wv1_hi[:, :], wv1_f).then_inc(a_wvs, 1)
            act.wait_ge(a_qk, 2)
            act.copy(halves(q_max[0:CD + 1, :]), ps[0:CD + 1, 0:2, :]).then_inc(a_qhi, 1)

            def exp0(jj, kv, kp):
                act.wait_ge(attended[jj], kp)
                for half in range(2):
                    u = 2 * jj + half
                    act.wait_ge(scored[u], kv)
                    act.activation(probs[:, jj, cols(half)], ps[0:KT, u % 3, :], ACT.Exp,
                                   scale=float(D) ** -0.5).then_inc(exped[u], 1)

            exp0(0, 1, 0)
            with act.Fori(0, CHUNKS - 1) as g:
                k1 = act.snap(g + 1)
                exp0(1, k1, g)
                exp0(2, k1, g)
                exp0(0, act.snap(g + 2), k1)
            exp0(1, CHUNKS, CHUNKS - 1)
            exp0(2, CHUNKS, CHUNKS - 1)
            act.wait_ge(attended[CH - 1], CHUNKS)
            act.copy(o0[:, 0:HALF], ps[0:CD + 1, 6, :]).then_inc(a_o, 1)

            std_of(1)
            turned(1, xn_t)
            std_of(2)
            turned(2, xn_t)
            act.wait_ge(f_biassb, 1)
            for n in range(2 * G0):
                g, half = n // 2, n % 2
                act.wait_ge(f_hid, n + 1)
                act.activation(hid0[:, g, cols(half)], ps[:, 2 + n, :], ACT.Gelu, bias=hb0[:, g:g + 1]).then_inc(f_gelu, 1)
                if n == 0:
                    act.wait_ge(f_maskt, 1)
                    act.copy(halves(mask_t), ps[0:E0, 0:2, :]).then_inc(f_masktsb, 1)

            std_of(3)
            turned(3, xn_t)

            def q_hi(n):
                act.wait_ge(c_qproj, n + 1)
                act.wait_ge(c_qcopy, n)
                act.copy(halves(q_max[:, :]), ps[:, 3:5, :]).then_inc(c_qhi, 1)

            def k_hi(g, kn, slots_read):
                act.wait_ge(c_kp, kn)
                if slots_read is not None:
                    act.wait_ge(slot_keys[CH - 1], slots_read)
                act.copy(keys_hl[:, bass.ds(g * CH, CH), 0, :],
                         ps[:, B_KP, 0:CK].rearrange("p (n k) -> p n k", k=KT)).then_inc(c_khi, 1)

            def tile1(parity, at, jj, both1, both, k):
                act.wait_ge(attended[jj], both)
                act.copy(vslot[:, jj, 0:HD],
                         v_head[:, bass.ds(parity, 1), bass.ds(at, HD)].rearrange("p a d -> p (a d)")).then_inc(c_vslot[jj], 1)
                act.wait_ge(c_padd[jj], k)
                if jj == CH - 1:
                    act.wait_ge(c_dadd, k)
                for half in range(2):
                    u = 2 * jj + half
                    act.wait_ge(scored[u], both1)
                    act.activation(probs[:, jj, cols(half)], ps[0:KT, u % 3, :], ACT.Exp,
                                   scale=float(HD) ** -0.5).then_inc(exped[u], 1)

            def step(parity, g, k, nxt, last):
                both = act.snap(k + CHUNKS)
                both1 = act.snap(k + (CHUNKS + 1))
                at = act.snap(g * (CH * HD))
                tile1(parity, at + HD, 1, both1, both, k)
                if nxt:
                    k_hi(g, both1, both1)
                tile1(parity, at + 2 * HD, 2, both1, both, k)
                if not last:
                    tile1(parity, at + 3 * HD, 0, act.snap(k + (CHUNKS + 2)), both1, act.snap(k + 1))

            def head(h, prev, nxt):
                if prev:
                    act.wait_ge(attended[CH - 1], (h + 1) * CHUNKS)
                    act.wait_ge(c_norm, h - 1)
                    act.copy(acc_raw[:, :], ps[:, B_ACC, :]).then_inc(c_acc, 1)
                act.wait_ge(c_vload, 16 * h + 16)
                parity = act.snap(h % 2)
                k0 = act.snap(h * CHUNKS)
                tile1(parity, 0, 0, act.snap(k0 + (CHUNKS + 1)), act.snap(k0 + CHUNKS), k0)
                if nxt:
                    q_hi(h + 1)
                with act.Fori(0, CHUNKS - 1) as g:
                    step(parity, g, act.snap(k0 + g), nxt, False)
                step(parity, CHUNKS - 1, act.snap(k0 + (CHUNKS - 1)), nxt, True)

            q_hi(0)
            with act.Fori(0, CHUNKS) as g:
                k_hi(g, act.snap(g + 1), None)
            head(0, False, True)
            with act.Fori(1, HEADS - 1) as h:
                head(h, True, True)
            head(HEADS - 1, True, False)
            act.wait_ge(attended[CH - 1], (HEADS + 1) * CHUNKS)
            act.wait_ge(c_norm, HEADS - 1)
            act.copy(acc_raw[:, :], ps[:, B_ACC, :]).then_inc(c_acc, 1)

            std_of(4)
            turned(4, xn_t)
            turned(5, x3_t)
            act.wait_ge(g_exp, 1)
            act.activation(gp, gp, ACT.Exp).then_inc(g_exp, 1)
            act.wait_ge(g_cwt, 1)
            act.copy(halves(cw_t), ps[0:E1, 1:3, :]).then_inc(g_cwtsb, 1)

            def act_item(s, half, i1, i0):
                act.wait_ge(g_u[half], i1)
                act.wait_ge(g_h[half], i0)
                act.activation(silu[:, half, :], ps[:, half, :], ACT.Silu,
                               bias=pair_w[:, s, 3 * P:3 * P + 1]).then_inc(g_silu[half], 1)

            with act.Fori(0, G1 // 2) as i:
                i0 = act.snap(2 * i)
                i1 = act.snap(2 * i + 1)
                i2 = act.snap(2 * i + 2)
                for half in range(2):
                    act_item(0, half, i1, i0)
                for half in range(2):
                    act_item(1, half, i2, i1)
            for half in range(2):
                act_item(0, half, G1 + 1, G1)

        @block.vector
        def _(dve):
            def layernorm(n, src, dst):
                for t in range(TT):
                    ins = dve.bn_stats(stats[:, t, :], src[:, t, :])
                ins.then_inc(ln_stats, 1)
                dve.wait_ge(ln_stats, n + 1)
                for t in range(TT):
                    ins = dve.bn_aggr(mean_var[:, t, :], stats[:, t, :])
                ins.then_inc(ln_var, 1)
                dve.wait_ge(ln_std, n + 1)
                dve.reciprocal(rstd[:, :], std[:, :]).then_inc(ln_rstd, 1)
                dve.wait_ge(ln_rstd, n + 1)
                for t in range(TT):
                    ins = dve.tensor_scalar(dst[:, t, :], src[:, t, :], mean_var[:, t, 0:1], rstd[:, t:t + 1],
                                            ALU.subtract, ALU.mult)
                ins.then_inc(ln_out, 1)

            def turned(n, dst):
                dve.wait_ge(tr_psum, 2 * n + 2)
                dve.tensor_copy(dst[:, HALF:TOK], ps[:, 7, :]).then_inc(tr_dve, 1)

            dve.wait_ge(in_x, 32)
            dve.tensor_scalar(neg_ident[:, :], ident[:, :], -1.0, None, ALU.mult).then_inc(neg_ready, 1)
            layernorm(0, x_tok, xn)
            turned(0, xn_t)
            dve.wait_ge(in_a, 16 * 6)
            dve.wait_ge(a_q, 2)
            dve.tensor_scalar(halves(q0_t), ps[:, 3:5, :], bq0[:, :], None, ALU.add).then_inc(a_qsb, 1)
            for q in range(CH):
                part = slice(q * CHUNKS, (q + 1) * CHUNKS)
                dve.wait_ge(a_chi, q + 1)
                dve.tensor_tensor(keys_hl[0:CD, part, 1, :], ctx_f.rearrange("p (n k) -> p n k", k=KT)[:, part, :],
                                  f32(keys_hl[0:CD, part, 0, :]), ALU.subtract).then_inc(a_clo, 1)
                if q == 0:
                    dve.wait_ge(a_qhi, 1)
                    dve.tensor_tensor(halves(q_all[0:CD, :]), ps[0:CD, 0:2, :], halves(f32(q_max[0:CD, :])),
                                      ALU.subtract).then_inc(a_qlo, 1)
            dve.wait_ge(a_wvs, 1)
            dve.tensor_tensor(wv1_lo[:, :], wv1_f, f32(wv1_hi[:, :]), ALU.subtract).then_inc(a_wvs, 1)
            dve.wait_ge(tr_act, 1)
            dve.wait_ge(tr_dve, 1)
            dve.memset(ps[:, 6:8, :], 0.0).then_inc(a_acczero, 1)

            with dve.Fori(0, CHUNKS) as g:
                k1 = dve.snap(g + 1)
                for i in range(TT):
                    dve.wait_ge(max_scored[i], k1)
                    dve.tensor_reduce(chunk_max[:, i, bass.ds(g, 1)], ps[:, B_MX + i % 2, 0:CK], AX,
                                      ALU.max).then_inc(max_reduced[i], 1)
            dve.wait_ge(max_reduced[TT - 1], CHUNKS)
            dve.tensor_reduce(row_max[:, :], chunk_max[:, :, :], AX, ALU.max).then_inc(max_found, 1)

            def fill0(n, j):
                dve.tensor_copy(kslot[0:CD + 1, j, :, :].rearrange("p a k -> p (a k)"),
                                f32(keys_hl[0:CD + 1, bass.ds(n, 1), :, :]).rearrange("p n a k -> p (n a k)")
                                ).then_inc(slot_keys[j], 1)

            def v_evac(j, k1, sixteen_k):
                dve.wait_ge(a_vout[j], sixteen_k)
                dve.tensor_copy(v_stage[:, j, :], ps[0:KT, 3 + j, :]).then_inc(a_vevac[j], 1)

            dve.wait_ge(a_clo, CH)
            dve.wait_ge(a_rows, 7)
            for j in range(CH):
                fill0(j, j)
            dve.wait_ge(max_row, 1)
            dve.tensor_tensor(halves(q_shift[CD:CD + 1, :]), ps[CD:CD + 1, 3:5, :], halves(f32(q_max[CD:CD + 1, :])),
                              ALU.add).then_inc(shifted, 1)
            with dve.Fori(0, CHUNKS - 1) as g:
                k1 = dve.snap(g + 1)
                k16 = dve.snap(g * 16)
                n1 = dve.snap(g * CH + CH)
                for j in range(CH):
                    dve.wait_ge(a_vproj[j], k1)
                    fill0(n1 + j, j)
                    v_evac(j, k1, k16)
            for j in range(CH):
                dve.wait_ge(a_vproj[j], CHUNKS)
                v_evac(j, CHUNKS, 16 * (CHUNKS - 1))
            dve.wait_ge(attended[CH - 1], CHUNKS)
            dve.tensor_copy(o0[:, HALF:TOK], ps[0:CD + 1, 7, :]).then_inc(a_o, 1)
            dve.wait_ge(in_f0, 16 * 9)
            w1_e = w1_in.rearrange("p (e j) -> p e j", e=E0)
            dve.tensor_tensor(w1s.rearrange("p (e j) -> p e j", e=E0), w1_e,
                              sc0.unsqueeze(2).to_broadcast([P, E0, H0]), ALU.mult).then_inc(f_w, 1)
            dve.tensor_tensor(w1b.rearrange("p (e j) -> p e j", e=E0), w1_e,
                              bi0.unsqueeze(2).to_broadcast([P, E0, H0]), ALU.mult).then_inc(f_w, 1)
            dve.wait_ge(a_out, 1)
            out_tiles = ps[:, 0:4, :].rearrange("p b (u c) -> p b u c", u=2)
            dve.reciprocal(rsum0[:, :, :], out_tiles[:, :, :, D]).then_inc(a_rsum, 1)
            dve.wait_ge(a_rsum, 1)
            for t in range(TT):
                b, u = t % 4, t // 4
                ins = dve.scalar_tensor_tensor(out=x_tok[:, t, :], in0=out_tiles[:, b, u, 0:D],
                                               scalar=rsum0[:, b, u:u + 1], in1=x_tok[:, t, :],
                                               op0=ALU.mult, op1=ALU.add)
            ins.then_inc(a_x, 1)

            dve.wait_ge(f_bias, 1)
            dve.tensor_tensor(hb0, ps[:, 5, 0:G0], b1_0, ALU.add).then_inc(f_biassb, 1)
            dve.wait_ge(a_x, 1)
            layernorm(1, x_tok, xn)
            turned(1, xn_t)
            dve.wait_ge(ln_out, 2)
            layernorm(2, xn, xn2)
            dve.wait_ge(f_logits, 1)
            dve.tensor_copy(lg0, ps[:, 4, 0:TT * E0]).then_inc(f_step, 1)
            turned(2, xn_t)
            dve.wait_ge(f_step, 1)
            for t in range(TT):
                ins = dve.max(top8[:, t, :], lg0[:, t * E0:(t + 1) * E0])
            ins.then_inc(f_step, 1)
            dve.wait_ge(f_step, 2)
            for t in range(TT):
                ins = dve.max_index(idx8[:, t, :], top8[:, t, :], lg0[:, t * E0:(t + 1) * E0])
            ins.then_inc(f_step, 1)
            dve.wait_ge(f_step, 3)
            dve.tensor_copy(idxf8[:, :, :], idx8[:, :, :]).then_inc(f_step, 1)
            dve.wait_ge(f_step, 4)
            for t in range(TT):
                ins = dve.tensor_scalar(mask0[:, t, :], iota[:, 0:E0], idxf8[:, t, 0:1], None, ALU.is_equal)
            ins.then_inc(f_mask, 1)
            for n in range(2 * G0):
                g, half = n // 2, n % 2
                dve.wait_ge(f_gelu, n + 1)
                dve.wait_ge(f_spread, n + 1)
                dve.tensor_tensor(hid0[:, g, cols(half)], ps[:, (6 + n) % 8, :], hid0[:, g, cols(half)],
                                  ALU.mult).then_inc(f_masked, 1)
            dve.wait_ge(f_out, 1)
            dve.tensor_tensor(x_tok[:, :, :], ps[:, 2:4, :].rearrange("p b (t d) -> p (b t) d", d=D), x_tok[:, :, :],
                              ALU.add).then_inc(f_x, 1)

            dve.wait_ge(f_x, 1)
            layernorm(3, x_tok, xn)
            turned(3, xn_t)
            dve.wait_ge(in_c, 64)

            def q_lo(n):
                dve.wait_ge(c_qhi, n + 1)
                dve.tensor_tensor(halves(q_max[HD:P, :]), ps[HD:P, 3:5, :], halves(f32(q_max[HD:P, :])),
                                  ALU.subtract).then_inc(c_qlo, 1)

            def k_lo(g, kn):
                dve.wait_ge(c_khi, kn)
                dve.tensor_tensor(keys_hl[0:HD, bass.ds(g * CH, CH), 1, :],
                                  ps[0:HD, B_KP, 0:CK].rearrange("p (n k) -> p n k", k=KT),
                                  f32(keys_hl[0:HD, bass.ds(g * CH, CH), 0, :]), ALU.subtract).then_inc(c_klo, 1)

            def chunk_maxima(i, g, kn):
                dve.wait_ge(max_scored[i], kn)
                dve.tensor_reduce(chunk_max[:, i, bass.ds(g, 1)], ps[:, B_MX + i % 2, 0:CK], AX,
                                  ALU.max).then_inc(max_reduced[i], 1)

            def fill1(n, j):
                dve.tensor_copy(kslot[:, j, :, :].rearrange("p a k -> p (a k)"),
                                f32(keys_hl[:, bass.ds(n, 1), :, :]).rearrange("p n a k -> p (n a k)")
                                ).then_inc(slot_keys[j], 1)

            def step(g, k, nxt, fill_at):
                both1 = dve.snap(k + (CHUNKS + 1))
                if nxt:
                    both_kn = dve.snap(k + (2 * CHUNKS + 1))
                if fill_at is not None:
                    k2 = dve.snap(k + 2)
                for j in range(CH):
                    if fill_at is not None:
                        dve.wait_ge(scored[2 * j + 1], both1)
                        if j == 0:
                            dve.wait_ge(c_klo, k2)
                            dve.wait_ge(c_khi, k2)
                        fill1(fill_at + j, j)
                    if nxt:
                        if j == 0:
                            k_lo(g, both1)
                        for i in ((0, 1), (2, 3, 4), (5, 6, 7))[j]:
                            chunk_maxima(i, g, both_kn)
                    if j == CH - 1:
                        dve.wait_ge(exped[2 * CH - 1], both1)
                        dve.wait_ge(c_dadd, k)
                        dve.tensor_tensor(psum_dve, psum_dve, probs[:, CH - 1, HALF:TOK], ALU.add).then_inc(c_dadd, 1)

            def prev_head_out(h, prev_index, final=False):
                dve.wait_ge(c_sums, h)
                dve.wait_ge(c_norm, h - 1)
                dve.tensor_copy(wo_slot[:, :], wo1[:, bass.ds(prev_index, 1), :].rearrange("p a d -> p (a d)"))
                dve.reciprocal(rden[:, :], ps[:, B_KP, :]).then_inc(c_rden, 1)
                if not final:
                    dve.memset(psum_dve, 0.0).then_inc(c_dzero, 1)
                    dve.wait_ge(c_dzero, h + 1)
                dve.wait_ge(c_rden, h)
                dve.wait_ge(c_acc, h)
                dve.tensor_tensor(acc_norm[:, :], acc_raw[:, :], rden[:, :], ALU.mult).then_inc(c_norm, 1)
                dve.wait_ge(c_out, h)
                dve.wait_ge(c_x, h - 1)
                dve.tensor_tensor(x_tok[:, :, :], ps[:, 3:5, :].rearrange("p b (t d) -> p (b t) d", d=D),
                                  x_tok[:, :, :], ALU.add).then_inc(c_x, 1)

            def head(h, prev, nxt):
                dve.wait_ge(max_reduced[TT - 1], (h + 2) * CHUNKS)
                dve.tensor_reduce(row_max[:, :], chunk_max[:, :, :], AX, ALU.max).then_inc(max_found, 1)
                dve.wait_ge(scored[2 * CH - 1], (h + 1) * CHUNKS)
                dve.wait_ge(c_qlo, h + 1)
                dve.tensor_copy(q_shift[0:HD, :], f32(q_max[0:HD, :])).then_inc(c_qcopy0, 1)
                dve.tensor_copy(q_all[:, :], f32(q_max[:, :])).then_inc(c_qcopy, 1)
                for half in range(2):
                    dve.wait_ge(max_row, h + 2)
                    at = HD + 32 * half
                    ins = dve.tensor_copy(q_shift[HD:HD + 1, cols(half)], ps[at:at + 1, B_AUX, :])
                ins.then_inc(shifted, 1)
                if prev:
                    dve.wait_ge(c_acc, h)
                dve.memset(ps[:, B_ACC, :], 0.0).then_inc(c_acczero, 1)
                if nxt:
                    q_lo(h + 1)
                if prev:
                    prev_head_out(h, h - 1)
                else:
                    dve.memset(psum_dve, 0.0).then_inc(c_dzero, 1)
                    dve.wait_ge(c_dzero, 1)
                k0 = dve.snap(h * CHUNKS)
                with dve.Fori(0, CHUNKS - 1) as g:
                    step(g, dve.snap(k0 + g), nxt, dve.snap(g * CH + CH))
                step(CHUNKS - 1, dve.snap(k0 + (CHUNKS - 1)), nxt, 0 if nxt else None)

            q_lo(0)
            with dve.Fori(0, CHUNKS) as g:
                k1 = dve.snap(g + 1)
                k_lo(g, k1)
                both1 = dve.snap(g + (CHUNKS + 1))
                for i in range(TT):
                    chunk_maxima(i, g, both1)
            dve.wait_ge(c_rows, 4)
            dve.wait_ge(c_klo, CHUNKS)
            for j in range(CH):
                dve.wait_ge(a_vproj[j], CHUNKS)
                fill1(j, j)
            for j in range(CH):
                dve.wait_ge(a_vout[j], 16 * CHUNKS)
            head(0, False, True)
            with dve.Fori(1, HEADS - 1) as h:
                head(h, True, True)
            head(HEADS - 1, True, False)
            prev_head_out(HEADS, HEADS - 1, final=True)

            dve.wait_ge(c_x, HEADS)
            layernorm(4, x_tok, xn)
            turned(4, xn_t)
            turned(5, x3_t)
            steps = [0]

            def link(ins):
                steps[0] += 1
                ins.then_inc(g_step, 1)
                dve.wait_ge(g_step, steps[0])

            dve.wait_ge(g_logits, 1)
            logits = ps[:, 0, 0:TT * E1].rearrange("p (t e) -> p t e", e=E1)

            def over(col, *shape):
                return col.unsqueeze(len(shape)).to_broadcast([P, *shape])

            link(dve.tensor_reduce(gm, logits, AX, ALU.max))
            dve.tensor_tensor(gp, logits, over(gm, TT, E1), ALU.subtract).then_inc(g_exp, 1)
            dve.wait_ge(g_exp, 2)
            link(dve.tensor_reduce(gs, gp, AX, ALU.add))
            link(dve.reciprocal(gm, gs))
            link(dve.tensor_tensor(gl, gp, over(gm, TT, E1), ALU.mult))
            members = gl.rearrange("p t (g m) -> p t g m", m=E1 // GROUPS)
            dve.tensor_tensor(pmax, members[:, :, :, 0], members[:, :, :, 1], ALU.max)
            dve.tensor_tensor(pmin, members[:, :, :, 0], members[:, :, :, 1], ALU.min)
            dve.tensor_tensor(qmax, members[:, :, :, 2], members[:, :, :, 3], ALU.max)
            link(dve.tensor_tensor(qmin, members[:, :, :, 2], members[:, :, :, 3], ALU.min))
            link(dve.tensor_tensor(pmin, pmin, qmin, ALU.max))
            link(dve.tensor_tensor(qmin, pmax, qmax, ALU.min))
            link(dve.tensor_tensor(pmax, pmax, qmax, ALU.max))
            link(dve.tensor_tensor(pmin, pmin, qmin, ALU.max))
            link(dve.tensor_tensor(pmax, pmax, pmin, ALU.add))

            def first_four(values, width, chosen):
                for t in range(TT):
                    ins = dve.max(top8[:, t, :], values[:, t, :])
                link(ins)
                for t in range(TT):
                    ins = dve.max_index(idx8[:, t, :], top8[:, t, :], values[:, t, :])
                link(ins)
                link(dve.tensor_copy(idxf8[:, :, :], idx8[:, :, :]))
                for t in range(TT):
                    ins = dve.tensor_scalar(chosen[:, t, :], iota[:, 0:width], idxf8[:, t, 0:1], None, ALU.is_equal)
                link(ins)
                for r in range(1, TOPK):
                    for t in range(TT):
                        ins = dve.scalar_tensor_tensor(out=chosen[:, t, :], in0=iota[:, 0:width],
                                                       scalar=idxf8[:, t, r:r + 1], in1=chosen[:, t, :],
                                                       op0=ALU.is_equal, op1=ALU.add)
                    link(ins)

            first_four(pmax, GROUPS, keep)
            link(dve.tensor_scalar(keep, keep, 2.0, -2.0, ALU.mult, ALU.add))
            link(dve.tensor_tensor(gp.rearrange("p t (g m) -> p t g m", m=E1 // GROUPS), members,
                                   over(keep, TT, GROUPS, E1 // GROUPS), ALU.add))
            first_four(gp, E1, cw)
            dve.tensor_tensor(cw, cw, gl, ALU.mult).then_inc(g_cw, 1)
            dve.wait_ge(g_cwtsb, 1)
            link(dve.tensor_copy(cw_3[0:E1, :], cw_t))
            link(dve.tensor_tensor(cw_r, cw_t, cw_3[0:E1, :], ALU.subtract))
            link(dve.tensor_copy(cw_b[:, :], cw_r))
            link(dve.tensor_copy(cw_3[E1:2 * E1, :], cw_b[:, :]))
            link(dve.tensor_tensor(cw_r, cw_r, cw_b[:, :], ALU.subtract))
            dve.tensor_copy(cw_3[2 * E1:3 * E1, :], cw_r).then_inc(g_spread_ready, 1)

            def gated(s, half, i1, i0, shared=False):
                dve.wait_ge(g_silu[half], i1)
                dve.wait_ge(g_y[half], i0)
                ins = dve.scalar_tensor_tensor(out=hgate[:, half, :], in0=ps[:, 2 + half, :],
                                               scalar=pair_w[:, s, 3 * P + 1:3 * P + 2], in1=silu[:, half, :],
                                               op0=ALU.add, op1=ALU.mult)
                ins.then_inc(g_h[half], 1)
                if not shared:
                    dve.wait_ge(g_h[half], i1)
                    dve.wait_ge(g_gate[half], i1)
                    dve.tensor_tensor(hgate[:, half, :], ps[:, 4 + half, :], hgate[:, half, :],
                                      ALU.mult).then_inc(g_hg[half], 1)

            with dve.Fori(0, G1 // 2) as i:
                i0 = dve.snap(2 * i)
                i1 = dve.snap(2 * i + 1)
                i2 = dve.snap(2 * i + 2)
                for half in range(2):
                    gated(0, half, i1, i0)
                for half in range(2):
                    gated(1, half, i2, i1)
            for half in range(2):
                gated(0, half, G1 + 1, G1, shared=True)
            for half in range(2):
                dve.wait_ge(g_y[half], G1 + 1)
                dve.scalar_tensor_tensor(out=x3_t[:, cols(half)], in0=ps[:, 6 + half, :], scalar=sb2[:, :],
                                         in1=x3_t[:, cols(half)], op0=ALU.add, op1=ALU.add).then_inc(g_fin[half], 1)

        @block.tensor
        def _(pe):
            def turn(n, src):
                for t in range(TT):
                    ins = pe.transpose(ps[:, 6 + t // 4, tile_cols(t % 4)], src[:, t, :], ident[:, :])
                    if t % 4 == 3:
                        ins.then_inc(tr_psum, 1)

            def turned(n):
                pe.wait_ge(tr_act, n + 1)
                pe.wait_ge(tr_dve, n + 1)

            pe.wait_ge(in_x, 32)
            pe.wait_ge(ln_out, 1)
            turn(0, xn)
            turned(0)
            pe.wait_ge(in_a, 16 * 6)
            for half in range(2):
                pe.matmul(ps[:, 3 + half, :], wq0[:, :], xn_t[:, cols(half)], start=True, stop=True).then_inc(a_q, 1)
            pe.wait_ge(a_qsb, 1)
            for half in range(2):
                pe.matmul(ps[0:CD + 1, half, :], wkt0[:, :], q0_t[:, cols(half)], start=True, stop=True).then_inc(a_qk, 1)
            pe.wait_ge(a_qhi, 1)
            pe.wait_ge(a_chi, CH)
            pe.wait_ge(a_rows, 7)
            with pe.Fori(0, CHUNKS) as g:
                k1 = pe.snap(g + 1)
                for i in range(TT):
                    pe.wait_ge(max_reduced[(i - 2) % TT], k1 if i >= 2 else g)
                    pe.matmul(ps[:, B_MX + i % 2, 0:CK], q_max[0:CD + 1, tile_cols(i)],
                              keys_hl[0:CD + 1, bass.ds(g * CH, CH), 0, :], start=True, stop=True).then_inc(max_scored[i], 1)

            def max_rows(row_at, bank_at):
                for t in range(TT):
                    p0, b = row_at(t), bank_at(t)
                    ins = pe.matmul(ps[p0:p0 + 1, b, tile_cols(t % 4)], row_max[:, t:t + 1], neg_ident[:, :],
                                    start=True, stop=True)
                return ins

            pe.wait_ge(max_found, 1)
            pe.wait_ge(neg_ready, 1)
            max_rows(lambda t: CD, lambda t: B_MX + t // 4).then_inc(max_row, 1)

            def scores0(jj, kv, kp):
                pe.wait_ge(slot_keys[jj], kv)
                for half in range(2):
                    u = 2 * jj + half
                    pe.wait_ge(exped[(u + 3) % 6], kv if u >= 3 else kp)
                    s = ps[0:KT, u % 3, :]
                    pe.matmul(s, kslot[0:CD + 1, jj, 0, :], q_shift[0:CD + 1, cols(half)], start=True, stop=False)
                    pe.matmul(s, kslot[0:CD, jj, 0, :], q_all[0:CD, cols(half)], start=False, stop=False)
                    pe.matmul(s, kslot[0:CD + 1, jj, 1, :], q_pad[0:CD + 1, cols(half)], start=False,
                              stop=True).then_inc(scored[u], 1)
                pe.wait_ge(a_vevac[jj], kp)
                v = ps[0:KT, 3 + jj, :]
                pe.matmul(v, kslot[0:CD, jj, 0, :], wv1_hi[:, :], start=True, stop=False)
                pe.matmul(v, kslot[0:CD, jj, 0, :], wv1_lo[:, :], start=False, stop=False)
                pe.matmul(v, kslot[0:CD, jj, 1, :], wv1_hi[:, :], start=False, stop=True).then_inc(a_vproj[jj], 1)

            def attend0(j, k1, k16):
                for half in range(2):
                    pe.wait_ge(exped[2 * j + half], k1)
                pe.wait_ge(a_cslot[j], k16)
                for half in range(2):
                    ins = pe.matmul(ps[0:CD + 1, 6 + half, :], vslot[:, j, 0:CD + 1], probs[:, j, cols(half)],
                                    start=False, stop=False, skip_group_check=True)
                ins.then_inc(attended[j], 1)

            pe.wait_ge(shifted, 1)
            pe.wait_ge(a_qlo, 1)
            pe.wait_ge(a_qcopy, 2)
            pe.wait_ge(a_wvs, 2)
            pe.wait_ge(a_acczero, 1)
            scores0(0, 1, 0)
            with pe.Fori(0, CHUNKS - 1) as g:
                k1 = pe.snap(g + 1)
                k16 = pe.snap(g * 16 + 16)
                for j in range(CH):
                    scores0((j + 1) % CH, k1 if j < CH - 1 else pe.snap(g + 2), g if j < CH - 1 else k1)
                    attend0(j, k1, k16)
            for j in range(CH):
                if j < CH - 1:
                    scores0(j + 1, CHUNKS, CHUNKS - 1)
                attend0(j, CHUNKS, 16 * CHUNKS)
            pe.wait_ge(a_o, 2)
            pe.wait_ge(a_vevac[0], CHUNKS)
            for t in range(TT):
                ins = pe.matmul(ps[:, t % 4, (t // 4) * 256:(t // 4) * 256 + D + 1], o0[:, tile_cols(t)], wv0[:, :],
                                start=True, stop=True)
            ins.then_inc(a_out, 1)

            pe.wait_ge(f_w, 2)
            pe.wait_ge(consts, 3)
            pe.wait_ge(a_vevac[CH - 1], CHUNKS)
            for g in range(G0):
                ins = pe.matmul(ps[:, 5, g:g + 1], w1b[:, tile_cols(g)], ones[:, 0:1], start=True, stop=True)
            ins.then_inc(f_bias, 1)
            pe.wait_ge(ln_out, 2)
            turn(1, xn)
            turned(1)
            pe.wait_ge(in_f0, 16 * 9)
            pe.wait_ge(a_vevac[1], CHUNKS)
            for t in range(TT):
                ins = pe.matmul(ps[:, 4, t * E0:(t + 1) * E0], xn_t[:, tile_cols(t)], wgt, start=True, stop=True)
            ins.then_inc(f_logits, 1)
            pe.wait_ge(ln_out, 3)
            turn(2, xn2)
            turned(2)
            pe.wait_ge(a_x, 1)
            pe.wait_ge(f_step, 1)
            pe.wait_ge(f_biassb, 1)
            for n in range(2 * G0):
                g, half = n // 2, n % 2
                pe.matmul(ps[:, 2 + n, :], w1s[:, tile_cols(g)], xn_t[:, cols(half)], start=True, stop=True).then_inc(f_hid, 1)
            pe.wait_ge(f_mask, 1)
            for t in range(TT):
                ins = pe.transpose(ps[0:E0, t // 4, tile_cols(t % 4)], mask0[:, t, :], ident[:, :])
            ins.then_inc(f_maskt, 1)
            pe.wait_ge(f_masktsb, 1)
            for n in range(2 * G0):
                g, half = n // 2, n % 2
                pe.matmul(ps[:, (6 + n) % 8, :], spread0[:, g, :], mask_t[:, cols(half)], start=True, stop=True).then_inc(f_spread, 1)
            pe.wait_ge(f_masked, 2 * G0)
            for t in range(TT):
                o = ps[:, 2 + t // 4, tile_cols(t % 4)]
                for g in range(G0):
                    pe.matmul(o, hid0[:, g, tile_cols(t)], w2_0[:, g, :], start=(g == 0), stop=False)
                ins = pe.matmul(o, mask_t[:, tile_cols(t)], b2_0[:, :], start=False, stop=True)
            ins.then_inc(f_out, 1)

            pe.wait_ge(ln_out, 4)
            turn(3, xn)
            turned(3)
            pe.wait_ge(in_c, 64)

            def q_proj(n):
                for half in range(2):
                    ins = pe.matmul(ps[:, 3 + half, :], wq1[:, :], xn_t[:, cols(half)], start=True, stop=True)
                ins.then_inc(c_qproj, 1)

            def k_proj(g, kb):
                pe.wait_ge(c_klo, kb)
                pe.matmul(ps[:, B_KP, 0:CK], wk1[:, :], ctx_f[:, bass.ds(g * CK, CK)], start=True, stop=True).then_inc(c_kp, 1)

            def max_scores(i, g, kn, both_kn, both_kb):
                if i == 0:
                    pe.wait_ge(c_khi, kn)
                pe.wait_ge(max_reduced[(i - 2) % TT], both_kn if i >= 2 else both_kb)
                pe.matmul(ps[:, B_MX + i % 2, 0:CK], q_max[:, tile_cols(i)],
                          keys_hl[:, bass.ds(g * CH, CH), 0, :], start=True, stop=True).then_inc(max_scored[i], 1)

            def scores1(jj, kv, kp):
                pe.wait_ge(slot_keys[jj], kv)
                for half in range(2):
                    u = 2 * jj + half
                    pe.wait_ge(exped[(u + 3) % 6], kv if u >= 3 else kp)
                    s = ps[0:KT, u % 3, :]
                    pe.matmul(s, kslot[:, jj, 0, :], q_all[:, cols(half)], start=True, stop=False)
                    pe.matmul(s, kslot[0:CD + 1, jj, 1, :], q_shift[:, cols(half)], start=False,
                              stop=True).then_inc(scored[u], 1)

            def attend1(j, k1, both1):
                for half in range(2):
                    pe.wait_ge(exped[2 * j + half], both1)
                pe.wait_ge(c_vslot[j], k1)
                for half in range(2):
                    ins = pe.matmul(ps[half * HD:(half + 1) * HD, B_ACC, :], vslot[:, j, 0:HD],
                                    probs[:, j, cols(half)], start=False, stop=False, skip_group_check=True)
                ins.then_inc(attended[j], 1)

            def step(g, k, nxt, last, x_added):
                k1 = pe.snap(k + 1)
                both = pe.snap(k + CHUNKS)
                both1 = pe.snap(k + (CHUNKS + 1))
                if nxt:
                    both_kb = pe.snap(k + 2 * CHUNKS)
                    both_kn = pe.snap(k + (2 * CHUNKS + 1))
                for j in range(CH):
                    if j < CH - 1:
                        scores1(j + 1, both1, both)
                    elif not last:
                        scores1(0, pe.snap(k + (CHUNKS + 2)), both1)
                    if nxt:
                        if j == 0:
                            k_proj(g, both)
                            if x_added is not None:
                                pe.wait_ge(c_x, x_added)
                        for i in ((), (2, 3), (5, 6))[j]:
                            max_scores(i, g, both1, both_kn, both_kb)
                    attend1(j, k1, both1)
                    if nxt:
                        for i in ((0, 1), (4,), (7,))[j]:
                            max_scores(i, g, both1, both_kn, both_kb)

            def prev_head_out(h, nxt, final):
                pe.wait_ge(c_padd[CH - 1], h * CHUNKS)
                pe.wait_ge(c_dadd, h * CHUNKS)
                one = ones[0:KT, 0:HD]
                pe.matmul(ps[0:HD, B_KP, :], one, psum_pool[:, 0:HALF], start=True, stop=True)
                pe.matmul(ps[HD:P, B_KP, :], one, psum_pool[:, HALF:TOK], start=True, stop=False)
                pe.matmul(ps[HD:P, B_KP, :], one, psum_dve, start=False, stop=True).then_inc(c_sums, 1)
                pe.wait_ge(c_norm, h)
                pe.wait_ge(c_rden, h)
                if not final:
                    pe.wait_ge(c_acczero, h + 1)
                if nxt:
                    pe.wait_ge(c_qlo, h + 2)
                for t in range(TT):
                    rows = slice((t // 4) * HD, (t // 4 + 1) * HD)
                    o = ps[:, 3 + t // 4, tile_cols(t % 4)]
                    ins = pe.matmul(o, acc_norm[rows, tile_cols(t % 4)], wo_slot[rows, :], start=True, stop=not final)
                    if final:
                        ins = pe.matmul(o, ones[0:1, :], bo1[:, :], start=False, stop=True)
                ins.then_inc(c_out, 1)

            def head(h, prev, nxt):
                pe.wait_ge(max_found, h + 2)
                max_rows(lambda t: HD + 32 * (t // 4), lambda t: B_AUX).then_inc(max_row, 1)
                pe.wait_ge(shifted, h + 2)
                pe.wait_ge(c_qcopy, h + 1)
                k0 = pe.snap(h * CHUNKS)
                scores1(0, pe.snap(k0 + (CHUNKS + 1)), pe.snap(k0 + CHUNKS))
                if nxt:
                    pe.wait_ge(c_wq, 16 * h + 16)
                    pe.wait_ge(c_wk, 16 * h + 16)
                    q_proj(h + 1)
                if prev:
                    prev_head_out(h, nxt, False)
                else:
                    pe.wait_ge(c_acczero, 1)
                    pe.wait_ge(c_qlo, 2)
                x_added = h if prev else None
                with pe.Fori(0, CHUNKS - 1) as g:
                    step(g, pe.snap(k0 + g), nxt, False, x_added)
                step(CHUNKS - 1, pe.snap(k0 + (CHUNKS - 1)), nxt, True, x_added)

            q_proj(0)
            pe.wait_ge(c_qlo, 1)
            with pe.Fori(0, CHUNKS) as g:
                k1 = pe.snap(g + 1)
                k_proj(g, g)
                both0 = pe.snap(g + CHUNKS)
                both1 = pe.snap(g + (CHUNKS + 1))
                for i in range(TT):
                    max_scores(i, g, k1, both1, both0)
            pe.wait_ge(c_rows, 4)
            head(0, False, True)
            with pe.Fori(1, HEADS - 1) as h:
                head(h, True, True)
            head(HEADS - 1, True, False)
            prev_head_out(HEADS, False, True)

            pe.wait_ge(ln_out, 5)
            turn(4, xn)
            turned(4)
            turn(5, x_tok)
            pe.wait_ge(in_f1, 16 * 5)
            for t in range(TT):
                o = ps[:, 0, t * E1:(t + 1) * E1]
                pe.matmul(o, xn_t[:, tile_cols(t)], gw[:, :], start=True, stop=False)
                ins = pe.matmul(o, ones[0:1, :], gb[:, :], start=False, stop=True)
            ins.then_inc(g_logits, 1)
            pe.wait_ge(g_cw, 1)
            for t in range(TT):
                ins = pe.transpose(ps[0:E1, 1 + t // 4, tile_cols(t % 4)], cw[:, t, :], ident[:, :])
            ins.then_inc(g_cwt, 1)
            pe.wait_ge(g_cwtsb, 1)
            turned(5)
            for half in range(2):
                pe.matmul(ps[:, 6 + half, :], b2_1[:, :], cw_t[:, cols(half)], start=True, stop=False, skip_group_check=True)
            pe.wait_ge(g_spread_ready, 1)

            def up(s, half, i, i0, w16, shared=False):
                pe.wait_ge(g_w[s], w16)
                pe.wait_ge(g_h[half], i0)
                xs = xn_t[:, cols(half)]
                pe.matmul(ps[:, half, :], pair_w[:, s, 0:P], xs, start=True, stop=True)
                pe.matmul(ps[:, 2 + half, :], pair_w[:, s, P:2 * P], xs, start=True, stop=True).then_inc(g_u[half], 1)
                if not shared:
                    pe.wait_ge(g_hg[half], i0)
                    pe.matmul(ps[:, 4 + half, :], spread1[:, bass.ds(i, 1), :].rearrange("p a c -> p (a c)"),
                              cw_3[:, cols(half)], start=True, stop=True).then_inc(g_gate[half], 1)

            def down(s, half, i1, shared=False):
                if shared:
                    pe.wait_ge(g_h[half], i1)
                else:
                    pe.wait_ge(g_hg[half], i1)
                pe.matmul(ps[:, 6 + half, :], pair_w[:, s, 2 * P:3 * P], hgate[:, half, :], start=False, stop=shared,
                          skip_group_check=True).then_inc(g_y[half], 1)

            def two_pairs(i, last):
                i0 = pe.snap(2 * i)
                i1 = pe.snap(2 * i + 1)
                i2 = pe.snap(2 * i + 2)
                w = pe.snap(16 * i + 16)
                up(0, 1, i0, i0, w)
                down(0, 0, i1)
                up(1, 0, i1, i1, w)
                down(0, 1, i1)
                up(1, 1, i1, i1, w)
                down(1, 0, i2)
                up(0, 0, i2, i2, pe.snap(16 * i + 32), shared=last)
                down(1, 1, i2)

            up(0, 0, 0, 0, 16)
            with pe.Fori(0, G1 // 2 - 1) as i:
                two_pairs(i, False)
            two_pairs(G1 // 2 - 1, True)
            up(0, 1, G1, G1, 16 * (G1 // 2) + 16, shared=True)
            for half in range(2):
                down(0, half, G1 + 1, shared=True)


def kernel(**inputs):
    import numpy as np
    import concourse.bacc as bacc
    import ml_dtypes
    from concourse.bass_utils import run_bass_kernel_spmd

    a = {n: np.asarray(v) for n, v in inputs.items()}
    c = np.ascontiguousarray
    context = a["ctx_768"][0]
    context = np.concatenate([context, context[KEYS - (PADDED - KEYS):]], 0)
    w1, w3, w2 = a["L1_ffn_w1"], a["L1_ffn_w3"], a["L1_ffn_w2"]
    pairs = [np.concatenate([w1[2 * i], w1[2 * i + 1], w3[2 * i], w3[2 * i + 1],
                             w2[2 * i:2 * i + 2].reshape(P, D),
                             a["L1_ffn_b1"][2 * i:2 * i + 2].reshape(P, 1),
                             a["L1_ffn_b3"][2 * i:2 * i + 2].reshape(P, 1)], 1) for i in range(G1)]
    pairs.append(np.concatenate([a["L1_ffn_sw1"], a["L1_ffn_sw3"], a["L1_ffn_sw2"],
                                 a["L1_ffn_sb1"].reshape(P, 1), a["L1_ffn_sb3"].reshape(P, 1)], 1))
    wq = a["L1_xattn_Wq"].reshape(D, HEADS, HD).transpose(1, 0, 2)
    wk = a["L1_xattn_Wk"].reshape(CD, HEADS, HD).transpose(1, 0, 2)
    wo = a["L1_xattn_Wo"].reshape(HEADS, HD, D).transpose(1, 0, 2)
    spread0 = np.zeros((E0, G0, P), np.float32)
    for e in range(E0):
        spread0[e, e // EG0, (e % EG0) * H0:(e % EG0 + 1) * H0] = 1.0
    spread1 = np.zeros((3 * E1, G1, P), ml_dtypes.bfloat16)
    for e in range(E1):
        for part in range(3):
            spread1[part * E1 + e, e // 2, (e % 2) * H1:(e % 2 + 1) * H1] = 1.0
    arrays = {
        "x": a["x"][0],
        "ctx_rows": context,
        "ctx_t": context.T,
        "a_wq": a["L0_xattn_Wq"],
        "a_bq": a["L0_xattn_bq"].reshape(D, 1),
        "a_wkt": a["L0_xattn_Wk"].T,
        "a_bk": a["L0_xattn_bk"].reshape(D, 1),
        "a_wv": a["L0_xattn_Wv"],
        "a_bv": a["L0_xattn_bv"].reshape(1, D),
        "f0_wgt": a["L0_ffn_Wg"].T,
        "f0_scale": a["L0_ffn_ln_scale"].T,
        "f0_bias": a["L0_ffn_ln_bias"].T,
        "f0_w1": a["L0_ffn_W1"].transpose(1, 0, 2).reshape(D, E0 * H0),
        "f0_b1": a["L0_ffn_b1"].reshape(G0, P).T,
        "f0_w2": a["L0_ffn_W2"].reshape(G0, P, D).transpose(1, 0, 2),
        "f0_b2": a["L0_ffn_b2"],
        "c_wq": np.concatenate([wq, wq], 2),
        "c_wk": np.concatenate([wk, wk], 2),
        "c_wv": a["L1_xattn_Wv"],
        "c_wo": np.concatenate([wo, wo], 0),
        "c_bo": a["L1_xattn_bo"].reshape(1, D),
        "f1_gw": a["L1_ffn_gw"],
        "f1_gb": a["L1_ffn_gb"].reshape(1, E1),
        "f1_pairs": np.stack(pairs),
        "f1_b2": a["L1_ffn_b2"],
        "f1_sb2": a["L1_ffn_sb2"].reshape(D, 1),
        "ident": np.eye(P, dtype=np.float32),
        "iota": np.tile(np.arange(E1, dtype=np.float32), (P, 1)),
        "spread0": spread0,
        "spread1": spread1,
    }
    arrays = {f"in_{n}": c(v) for n, v in arrays.items()}
    nc = bacc.Bacc("TRN2", target_bir_lowering=False, num_devices=1)
    args = [nc.dram_tensor(n, v.shape, mybir.dt.from_np(v.dtype), kind="ExternalInput").ap() for n, v in arrays.items()]
    out_t = nc.dram_tensor("out_t", [D, TOK], F32, kind="ExternalOutput").ap()
    build_program(nc, *args, out_t)
    r = run_bass_kernel_spmd(nc, [arrays], core_ids=[0])
    return r.results[0]["out_t"].T.reshape(1, TOK, D)
```

```python
from contextlib import ExitStack

import concourse.bass as bass
from concourse import mybir

F32 = mybir.dt.float32
F32R = mybir.dt.float32r
BF16 = mybir.dt.bfloat16
U32 = mybir.dt.uint32
ALU = mybir.AluOpType
ACT = mybir.ActivationFunctionType
AX = mybir.AxisListType.X

P = 128
TOK = 1024
TT = TOK // P
HALF = TOK // 2
D = 128
KEYS = 6404
CD = 96
KT = 126
TILES = 51
CH = 3
CHUNKS = TILES // CH
CK = CH * KT
PADDED = TILES * KT
PAD_AT = KEYS - (TILES - 1) * KT
HEADS = 8
HD = 64
E0, H0 = 8, 32
EG0 = P // H0
G0 = E0 // EG0
E1, H1 = 32, 64
G1 = E1 * H1 // P
GROUPS, TOPK, TOPG = 8, 4, 4
EPS = 1e-5
PAD_SCORE = -1e30
PAIR_W = 3 * P + 2
B_S, B_MX, B_KP, B_ACC, B_AUX = 0, 3, 5, 6, 7
UNROLL = 3
TURNS = (CHUNKS - 2) // UNROLL


def build_program(nc, x, ctx_rows, ctx_t, a_wq, a_bq, a_wkt, a_bk, a_wv, a_bv,
                  f0_wgt, f0_scale, f0_bias, f0_w1, f0_b1, f0_w2, f0_b2,
                  c_wq_in, c_wk_in, c_wv_in, c_wo_in, c_bo_in,
                  f1_gw, f1_gb, f1_pairs, f1_b2, f1_sb2,
                  ident_in, iota_in, spread0_in, spread1_in, out_t):
    with ExitStack() as ctx:
        def sb(name, shape, dt=F32):
            return ctx.enter_context(nc.sbuf_tensor(name, shape, dt))

        def sem(name):
            return ctx.enter_context(nc.semaphore(name))

        def sems(name, n):
            return [sem(f"{name}{i}") for i in range(n)]

        v_dram = nc.dram_tensor("v_scratch", [TILES, KT, HEADS * HD], F32, kind="Internal").ap()

        ps = ctx.enter_context(nc.psum_tensor("ps", [P, 8, HALF], F32))

        ident = sb("ident", [P, P])
        neg_ident = sb("neg_ident", [P, P])
        ones = sb("ones", [P, P])
        iota = sb("iota", [P, E1])
        eps_col = sb("eps_col", [P, 1])
        zero_col = sb("zero_col", [P, 1])
        x_tok = sb("x_tok", [P, TT, D])
        xn = sb("xn", [P, TT, D])
        xn2 = sb("xn2", [P, TT, D])
        xn_t = sb("xn_t", [P, TOK])
        stats = sb("stats", [P, TT, 6])
        mean_var = sb("mean_var", [P, TT, 2])
        std = sb("std", [P, TT])
        rstd = sb("rstd", [P, TT])
        ctx_mem = sb("ctx_mem", [P, PADDED])
        ctx_f = ctx_mem[0:CD, :]
        keys_hl = sb("keys_hl", [P, TILES, 2, KT], F32R)
        kslot = sb("kslot", [P, CH, 2, KT], F32R)
        vslot = sb("vslot", [KT, CH, P])
        probs = sb("probs", [KT, CH, TOK])
        q_max = sb("q_max", [P, TOK], F32R)
        q_all2 = sb("q_all2", [P, 2, TOK], F32R)
        q_shift2 = sb("q_shift2", [97, 2, TOK], F32R)
        q_all, q_shift = q_all2[:, 0, :], q_shift2[:, 0, :]
        q_pad = sb("q_pad", [97, TOK], F32R)
        chunk_max = sb("chunk_max", [P, TT, CHUNKS])
        row_max = sb("row_max", [P, TT])
        v_mem = sb("v_mem", [P, 2 * TILES * HD])
        v_head = v_mem[0:KT, :].rearrange("p (b f) -> p b f", b=2)
        v_tiles = v_head.rearrange("p b (n d) -> p b n d", n=TILES)
        wq0 = sb("wq0", [P, D])
        bq0 = sb("bq0", [P, 1])
        wkt0 = sb("wkt0", [P, CD + 1])
        wv0 = sb("wv0", [CD + 1, D + 1])
        q0_t = v_mem[:, 0:TOK]
        o0 = v_mem[0:CD + 1, TOK:2 * TOK]
        rsum0 = sb("rsum0", [P, 4, 2])
        wv1_f = v_mem[0:CD, 2 * TOK:2 * TOK + HEADS * HD]
        wv1_hi = sb("wv1_hi", [CD, HEADS * HD], F32R)
        wv1_lo = sb("wv1_lo", [CD, HEADS * HD], F32R)
        sum_mem = sb("sum_mem", [KT, TOK + HALF])
        v_stage = sum_mem[:, :].rearrange("p (j f) -> p j f", j=CH)
        wq1 = sb("wq1", [P, P])
        wk1 = sb("wk1", [CD, P])
        wo1 = sb("wo1", [P, HEADS, D])
        wo_slot = sb("wo_slot", [P, D])
        bo1 = sb("bo1", [P, D])
        psum_pool = sum_mem[:, 0:TOK]
        psum_dve = sum_mem[:, TOK:TOK + HALF]
        acc_raw = sb("acc_raw", [P, HALF])
        rden = sb("rden", [P, TT])
        diag = sb("diag", [HD + TT, TT])

        in_x, in_a, in_wv, in_f0, in_c, in_f1 = (sem(f"in_{n}") for n in ("x", "a", "wv", "f0", "c", "f1"))
        in_ctx = sems("in_ctx", CH)
        consts, neg_ready = sem("consts"), sem("neg_ready")
        ln_stats, ln_var, ln_std, ln_rstd, ln_out = (sem(f"ln_{n}") for n in ("stats", "var", "std", "rstd", "out"))
        tr_psum, tr_act, tr_dve = sem("tr_psum"), sem("tr_act"), sem("tr_dve")
        max_scored, max_reduced = sems("max_scored", TT), sems("max_reduced", TT)
        slot_keys, attended = sems("slot_keys", CH), sems("attended", CH)
        scored, exped = sems("scored", 2 * CH), sems("exped", 2 * CH)
        max_found, max_row, shifted = sem("max_found"), sem("max_row"), sem("shifted")
        a_q, a_qsb, a_qk, a_qhi, a_qlo, a_rows, a_chi, a_clo, a_wvs, a_qcopy, a_acczero, a_o, a_out, a_rsum, a_x = (
            sem(f"a_{n}") for n in ("q", "qsb", "qk", "qhi", "qlo", "rows", "chi", "clo", "wvs", "qcopy", "acczero",
                                    "o", "out", "rsum", "x"))
        a_vkeys = sems("a_vkeys", CH)
        a_cslot, a_vproj, a_vevac, a_vout = (sems(f"a_{n}", CH) for n in ("cslot", "vproj", "vevac", "vout"))
        f_logits, f_step, f_mask, f_w, f_bias, f_biassb, f_hid, f_gelu, f_maskt, f_masktsb, f_spread, f_masked, f_out, f_x = (
            sem(f"f_{n}") for n in ("logits", "step", "mask", "w", "bias", "biassb", "hid", "gelu", "maskt", "masktsb",
                                    "spread", "masked", "out", "x"))
        c_rows, c_wq, c_wk, c_vload, c_qproj, c_qhi, c_qlo, c_qcopy, c_kp, c_khi, c_klo = (
            sem(f"c_{n}") for n in ("rows", "wq", "wk", "vload", "qproj", "qhi", "qlo", "qcopy", "kp", "khi", "klo"))
        c_dadd, c_total, c_acc, c_acczero, c_sums, c_rden, c_wo, c_out, c_x = (
            sem(f"c_{n}") for n in ("dadd", "total", "acc", "acczero", "sums", "rden", "wo", "out", "x"))
        c_bo = sem("c_bo")
        c_vslot, c_padd = sems("c_vslot", CH), sems("c_padd", CH)
        g_step, g_logits, g_exp, g_cw, g_cwt, g_cwtsb, g_spread_ready, g_store = (
            sem(f"g_{n}") for n in ("step", "logits", "exp", "cw", "cwt", "cwtsb", "spread_ready", "store"))
        g_w, g_u, g_silu, g_h, g_gate, g_hg, g_y, g_fin = (
            sems(f"g_{n}", 2) for n in ("w", "u", "silu", "h", "gate", "hg", "y", "fin"))

        f0w = sb("f0w", [P, 3 * 256 + 8 * 3 + 2 + 2 + 8 * 8])
        w1_in = f0w[:, 0:256]
        w1s = f0w[:, 256:512]
        w1b = f0w[:, 512:768]
        sc0 = f0w[:, 768:776]
        bi0 = f0w[:, 776:784]
        wgt = f0w[:, 784:792]
        b1_0 = f0w[:, 792:794]
        hb0 = f0w[:, 794:796]
        lg0 = f0w[:, 796:860]
        w2_0 = sb("w2_0", [P, G0, D])
        b2_0 = sb("b2_0", [E0, D])
        spread0 = sb("spread0", [E0, G0, P])
        mask0 = sb("mask0", [P, TT, E0])
        top8 = sb("top8", [P, TT, 8])
        idx8 = sb("idx8", [P, TT, 8], U32)
        idxf8 = sb("idxf8", [P, TT, 8])
        mask_t = v_mem[0:E0, 5 * TOK:6 * TOK]
        hid0 = v_mem[:, 3 * TOK:5 * TOK].rearrange("p (g t) -> p g t", g=G0)

        gw = sb("gw", [P, E1])
        gb = sb("gb", [1, E1])
        b2_1 = sb("b2_1", [E1, D])
        sb2 = sb("sb2", [P, 1])
        spread1 = sb("spread1", [3 * E1, G1, P], BF16)
        used = [0]

        def over_ctx(*shape):
            n, at = 1, used[0]
            for m in shape:
                n *= m
            used[0] += n
            flat = ctx_mem[:, at:at + n]
            return flat.rearrange("p (a b) -> p a b", a=shape[0]) if len(shape) == 2 else flat

        gl, gp, cw = over_ctx(TT, E1), over_ctx(TT, E1), over_ctx(TT, E1)
        gm, gs = over_ctx(TT), over_ctx(TT)
        pmax, pmin, qmax, qmin, keep = (over_ctx(TT, GROUPS) for _ in range(5))
        cw_t, cw_r = over_ctx(TOK)[0:E1, :], over_ctx(TOK)[0:E1, :]
        x3_t = over_ctx(TOK)
        cw_b = sb("cw_b", [E1, TOK], BF16)
        cw_3 = sb("cw_3", [3 * E1, TOK], BF16)
        pair_w = sb("pair_w", [P, 2, PAIR_W])
        silu = sb("silu", [P, 2, HALF])
        hgate = sb("hgate", [P, 2, HALF])
        block = ctx.enter_context(nc.Block())

        crow_v = ctx_rows.rearrange("(n p) c -> n p c", p=KT)
        v_dram_v = v_dram.rearrange("n p (h d) -> h p n d", h=HEADS)

        def f32(ap):
            return ap.bitcast(F32)

        def halves(ap):
            return ap.rearrange("p (a b) -> p a b", a=2)

        def cols(half):
            return slice(half * HALF, (half + 1) * HALF)

        def flat(ap):
            return ap.rearrange("p a b -> p (a b)")

        def tile_cols(t):
            return slice(t * P, (t + 1) * P)

        @block.sync
        def _(sp):
            sp.dma_start(x_tok[:, :, :], x.rearrange("(t p) d -> p t d", p=P)).then_inc(in_x, 16)
            sp.dma_start(ident[:, :], ident_in).then_inc(in_x, 16)
            for dst, src in ((wq0[:, :], a_wq), (bq0[:, :], a_bq), (wkt0[:, 0:CD], a_wkt), (wkt0[:, CD:CD + 1], a_bk),
                             (wv0[0:CD, 0:D], a_wv), (wv0[CD:CD + 1, 0:D], a_bv)):
                sp.dma_start(dst, src).then_inc(in_a, 16)
            for q in range(CH):
                part = slice(q * CHUNKS * KT, (q + 1) * CHUNKS * KT)
                sp.dma_start(ctx_f[:, part], ctx_t[:, part]).then_inc(in_ctx[q], 16)
            sp.dma_start(wv1_f, c_wv_in).then_inc(in_wv, 16)
            for dst, src in ((w1_in, f0_w1), (sc0, f0_scale), (bi0, f0_bias), (wgt, f0_wgt), (b1_0, f0_b1),
                             (w2_0[:, :, :], f0_w2), (b2_0[:, :], f0_b2), (spread0[:, :, :], spread0_in),
                             (iota[:, :], iota_in)):
                sp.dma_start(dst, src).then_inc(in_f0, 16)
            for dst, src in ((wo1[:, :, :], c_wo_in), (bo1[:, :], c_bo_in),
                             (wq1[:, :], c_wq_in[0]), (wk1[:, :], c_wk_in[0]),
                             (diag[HD:HD + TT, :], ident_in[0:TT, 0:TT])):
                sp.dma_start(dst, src).then_inc(in_c, 16)
            for dst, src in ((gw[:, :], f1_gw), (gb[:, :], f1_gb), (b2_1[:, :], f1_b2),
                             (sb2[:, :], f1_sb2), (spread1[:, :, :], spread1_in)):
                sp.dma_start(dst, src).then_inc(in_f1, 16)
            for s in range(2):
                sp.dma_start(pair_w[:, s, :], f1_pairs[s]).then_inc(g_w[s], 16)
            for j in range(CH):
                sp.dma_start(vslot[:, j, 0:CD], crow_v[j]).then_inc(a_cslot[j], 16)

            with sp.Fori(0, CHUNKS) as g:
                k1 = sp.snap(g + 1)
                for j in range(CH):
                    sp.wait_ge(a_vevac[j], k1)
                    sp.dma_start(v_dram[bass.ds(g * CH + j, 1)].rearrange("a p c -> p (a c)"),
                                 v_stage[:, j, :]).then_inc(a_vout[j], 16)
            with sp.Fori(0, CHUNKS - 1) as g:
                k1 = sp.snap(g + 1)
                for j in range(CH):
                    sp.wait_ge(attended[j], k1)
                    sp.dma_start(vslot[:, j, 0:CD],
                                 crow_v[bass.ds(g * CH + CH + j, 1)].rearrange("a p c -> p (a c)")).then_inc(a_cslot[j], 16)
            for j in range(CH):
                sp.wait_ge(a_vout[j], 16 * CHUNKS)
            sp.wait_ge(f_x, 1)
            sp.dma_start(v_tiles[:, 0], v_dram_v[0]).then_inc(c_vload, 16)
            sp.wait_ge(c_qproj, 1)
            sp.dma_start(wq1[:, :], c_wq_in[1]).then_inc(c_wq, 16)
            sp.wait_ge(c_kp, CHUNKS)
            sp.dma_start(wk1[:, :], c_wk_in[1]).then_inc(c_wk, 16)

            def load_v(h):
                sp.wait_ge(c_vslot[CH - 1], h * CHUNKS + 1)
                sp.dma_start(v_tiles[:, bass.ds((h + 1) % 2, 1)].rearrange("p b n d -> p (b n) d"),
                             v_dram_v[bass.ds(h + 1, 1)].rearrange("h p n d -> (h p) n d")).then_inc(c_vload, 16)

            with sp.Fori(0, HEADS - 2) as h:
                load_v(h)
                sp.wait_ge(c_qproj, h + 2)
                sp.dma_start(wq1[:, :], c_wq_in[bass.ds(h + 2, 1)].rearrange("a p c -> p (a c)")).then_inc(c_wq, 16)
                sp.wait_ge(c_kp, (h + 2) * CHUNKS)
                sp.dma_start(wk1[:, :], c_wk_in[bass.ds(h + 2, 1)].rearrange("a p c -> p (a c)")).then_inc(c_wk, 16)
            load_v(HEADS - 2)
            with sp.Fori(0, G1 // 2 - 1) as i:
                k1 = sp.snap(2 * i + 1)
                for s in range(2):
                    for half in range(2):
                        sp.wait_ge(g_y[half], k1 + s)
                    sp.dma_start(pair_w[:, s, :],
                                 f1_pairs[bass.ds(2 * i + 2 + s, 1)].rearrange("a p c -> p (a c)")).then_inc(g_w[s], 16)
            for half in range(2):
                sp.wait_ge(g_y[half], G1 - 1)
            sp.dma_start(pair_w[:, 0, :], f1_pairs[G1]).then_inc(g_w[0], 16)
            for half in range(2):
                sp.wait_ge(g_fin[half], 1)
                sp.dma_start(out_t[:, cols(half)], x3_t[:, cols(half)]).then_inc(g_store, 16)
            sp.wait_ge(g_store, 32)

        @block.gpsimd
        def _(pool):
            pool.memset(ones[:, :], 1.0).then_inc(consts, 1)
            pool.wait_ge(consts, 1)
            pool.memset(eps_col[:, :], EPS).then_inc(consts, 1)
            pool.wait_ge(consts, 2)
            pool.memset(zero_col[:, :], 0.0).then_inc(consts, 1)
            pool.wait_ge(consts, 3)
            pool.memset(vslot[:, :, CD:CD + 1], 1.0).then_inc(a_rows, 1)
            pool.wait_ge(a_rows, 1)
            pool.memset(f32(q_pad[CD:CD + 1, :]), PAD_SCORE).then_inc(a_rows, 1)
            pool.wait_ge(a_rows, 2)
            pool.memset(wv0[:, D:D + 1], 0.0).then_inc(a_rows, 1)
            pool.wait_ge(a_rows, 3)
            pool.memset(wv0[CD:CD + 1, D:D + 1], 1.0).then_inc(a_rows, 1)
            pool.wait_ge(a_rows, 4)
            pool.memset(f32(keys_hl[CD:CD + 1, :, 0, :]), 1.0).then_inc(a_rows, 1)
            pool.wait_ge(a_rows, 5)
            pool.memset(f32(keys_hl[CD:P, :, 1, :]), 0.0).then_inc(a_rows, 1)
            pool.wait_ge(a_rows, 6)
            pool.memset(f32(keys_hl[CD:CD + 1, TILES - 1, 1, PAD_AT:KT]), 1.0).then_inc(a_rows, 1)
            pool.wait_ge(a_rows, 7)
            pool.wait_ge(a_qhi, 1)
            pool.tensor_copy(q_shift[0:CD, :], f32(q_max[0:CD, :])).then_inc(a_qcopy, 1)
            pool.wait_ge(a_qcopy, 1)
            pool.tensor_copy(q_pad[0:CD, :], f32(q_max[0:CD, :])).then_inc(a_qcopy, 1)
            pool.wait_ge(a_qcopy, 2)
            pool.wait_ge(slot_keys[CH - 1], CHUNKS)
            pool.memset(f32(keys_hl[HD:CD, :, 1, :]), 0.0).then_inc(c_rows, 1)
            pool.wait_ge(c_rows, 1)
            pool.memset(f32(keys_hl[HD:HD + TT, :, 1, :]), 1.0).then_inc(c_rows, 1)
            pool.wait_ge(c_rows, 2)
            pool.wait_ge(scored[2 * CH - 1], CHUNKS)
            pool.memset(f32(q_shift2[HD:CD, :, :]), 0.0).then_inc(c_rows, 1)
            pool.wait_ge(c_rows, 3)
            pool.memset(f32(q_shift2[CD:CD + 1, :, :]), PAD_SCORE).then_inc(c_rows, 1)
            pool.wait_ge(c_rows, 4)

            def add(j, width, last_add, both1, first=False):
                pool.wait_ge(exped[2 * j], both1)
                if width == TOK:
                    pool.wait_ge(exped[2 * j + 1], both1)
                pool.wait_ge(c_padd[(j - 1) % CH], last_add)
                other = zero_col[0:KT, :].to_broadcast([KT, TOK]) if first else psum_pool[:, 0:width]
                pool.tensor_tensor(psum_pool[:, 0:width], other, probs[:, j, 0:width], ALU.add).then_inc(c_padd[j], 1)

            def add_chunk(k, h=None):
                k1 = pool.snap(k + 1)
                both1 = pool.snap(k + (CHUNKS + 1))
                if h is not None:
                    pool.wait_ge(c_sums, h)
                add(0, TOK, k, both1, first=h is not None)
                add(1, TOK, k1, both1)
                add(2, HALF, k1, both1)

            pool.wait_ge(consts, 3)
            for j in range(CH):
                pool.wait_ge(a_vout[j], 16 * CHUNKS)
            with pool.Fori(0, HEADS) as h:
                k0 = pool.snap(h * CHUNKS)
                add_chunk(k0, h)
                with pool.Fori(1, CHUNKS) as g:
                    add_chunk(pool.snap(k0 + g))
                pool.wait_ge(c_padd[CH - 1], h * CHUNKS + CHUNKS)
                pool.wait_ge(c_dadd, h * CHUNKS + CHUNKS)
                pool.tensor_tensor(psum_pool[:, HALF:TOK], psum_pool[:, HALF:TOK], psum_dve, ALU.add).then_inc(c_total, 1)

        @block.scalar
        def _(act):
            def std_of(n):
                if n == 0:
                    act.wait_ge(consts, 3)
                act.wait_ge(ln_var, n + 1)
                act.activation(std[:, :], mean_var[:, :, 1], ACT.Sqrt, bias=eps_col[:, :]).then_inc(ln_std, 1)

            def turned(n, dst):
                act.wait_ge(tr_psum, 2 * n + 1)
                act.copy(dst[:, 0:HALF], ps[:, 6, :]).then_inc(tr_act, 1)

            for q in range(CH):
                part = slice(q * CHUNKS, (q + 1) * CHUNKS)
                act.wait_ge(in_ctx[q], 16)
                act.copy(keys_hl[0:CD, part, 0, :],
                         ctx_f.rearrange("p (n k) -> p n k", k=KT)[:, part, :]).then_inc(a_chi, 1)
                if q == 0:
                    std_of(0)
                    turned(0, xn_t)
            act.wait_ge(in_wv, 16)
            act.copy(wv1_hi[:, :], wv1_f).then_inc(a_wvs, 1)
            act.wait_ge(a_qk, 2)
            act.copy(halves(q_max[0:CD + 1, :]), ps[0:CD + 1, 0:2, :]).then_inc(a_qhi, 1)

            def v_keys(n, j):
                act.copy(kslot[0:CD, j, :, :].rearrange("p a k -> p (a k)"),
                         f32(keys_hl[0:CD, bass.ds(n, 1), :, :]).rearrange("p n a k -> p (n a k)")
                         ).then_inc(a_vkeys[j], 1)

            def v_evac(j, k1, sixteen_k):
                act.wait_ge(a_vproj[j], k1)
                act.wait_ge(a_vout[j], sixteen_k)
                act.copy(v_stage[:, j, :], ps[0:KT, 4 + j, :]).then_inc(a_vevac[j], 1)

            act.wait_ge(a_clo, CH)
            for j in range(CH):
                v_keys(j, j)
            with act.Fori(0, CHUNKS - 1) as g:
                k1 = act.snap(g + 1)
                k16 = act.snap(g * 16)
                n1 = act.snap(g * CH + CH)
                for j in range(CH):
                    act.wait_ge(a_vproj[j], k1)
                    v_keys(n1 + j, j)
                    v_evac(j, k1, k16)
            for j in range(CH):
                v_evac(j, CHUNKS, 16 * (CHUNKS - 1))

            def exp0(jj, kv, kp):
                act.wait_ge(attended[jj], kp)
                for half in range(2):
                    u = 2 * jj + half
                    act.wait_ge(scored[u], kv)
                    act.activation(probs[:, jj, cols(half)], ps[0:KT, u % 3, :], ACT.Exp,
                                   scale=float(D) ** -0.5).then_inc(exped[u], 1)

            exp0(0, 1, 0)
            with act.Fori(0, CHUNKS - 1) as g:
                k1 = act.snap(g + 1)
                exp0(1, k1, g)
                exp0(2, k1, g)
                exp0(0, act.snap(g + 2), k1)
            exp0(1, CHUNKS, CHUNKS - 1)
            exp0(2, CHUNKS, CHUNKS - 1)
            act.wait_ge(attended[CH - 1], CHUNKS)
            act.copy(o0[:, 0:HALF], ps[0:CD + 1, 6, :]).then_inc(a_o, 1)

            std_of(1)
            turned(1, xn_t)
            std_of(2)
            turned(2, xn_t)
            act.wait_ge(f_biassb, 1)
            for n in range(2 * G0):
                g, half = n // 2, n % 2
                act.wait_ge(f_hid, n + 1)
                act.activation(hid0[:, g, cols(half)], ps[:, 2 + n, :], ACT.Gelu, bias=hb0[:, g:g + 1]).then_inc(f_gelu, 1)
                if n == 0:
                    act.wait_ge(f_maskt, 1)
                    act.copy(halves(mask_t), ps[0:E0, 0:2, :]).then_inc(f_masktsb, 1)

            std_of(3)
            turned(3, xn_t)

            def q_hi(n):
                act.wait_ge(c_qproj, n + 1)
                act.wait_ge(c_qcopy, 2 * n)
                act.copy(halves(q_max[:, :]), ps[:, 3:5, :]).then_inc(c_qhi, 1)

            def q_moving(n, part):
                slot = act.snap(n % 2) if not isinstance(n, int) else n % 2
                if part == 0:
                    act.wait_ge(c_qhi, n + 1)
                    dst, src = q_shift2[0:HD, bass.ds(slot, 1), :], q_max[0:HD, :]
                else:
                    act.wait_ge(c_qlo, n + 1)
                    dst, src = q_all2[:, bass.ds(slot, 1), :], q_max[:, :]
                act.copy(dst.rearrange("p a t -> p (a t)"), f32(src)).then_inc(c_qcopy, 1)

            def k_hi(g, kn, slots_read):
                act.wait_ge(c_kp, kn)
                if slots_read is not None:
                    act.wait_ge(slot_keys[CH - 1], slots_read)
                act.copy(keys_hl[:, bass.ds(g * CH, CH), 0, :],
                         ps[:, B_KP, 0:CK].rearrange("p (n k) -> p n k", k=KT)).then_inc(c_khi, 1)

            def tile1(parity, at, jj, both1, both, k):
                act.wait_ge(attended[jj], both)
                act.copy(vslot[:, jj, 0:HD],
                         v_head[:, bass.ds(parity, 1), bass.ds(at, HD)].rearrange("p a d -> p (a d)")).then_inc(c_vslot[jj], 1)
                act.wait_ge(c_padd[jj], k)
                if jj == CH - 1:
                    act.wait_ge(c_dadd, k)
                for half in range(2):
                    u = 2 * jj + half
                    act.wait_ge(scored[u], both1)
                    act.activation(probs[:, jj, cols(half)], ps[0:KT, u % 3, :], ACT.Exp,
                                   scale=float(HD) ** -0.5).then_inc(exped[u], 1)

            def step(parity, g, k, nxt, last=False, q_of=None):
                both = act.snap(k + CHUNKS)
                both1 = act.snap(k + (CHUNKS + 1))
                at = act.snap(g * (CH * HD)) if not isinstance(g, int) else g * CH * HD
                if nxt:
                    k_hi(g, both1, both1)
                tile1(parity, at + HD, 1, both1, both, k)
                if q_of is not None:
                    q_moving(q_of, 0)
                tile1(parity, at + 2 * HD, 2, both1, both, k)
                if q_of is not None:
                    q_moving(q_of, 1)
                if not last:
                    tile1(parity, at + 3 * HD, 0, act.snap(k + (CHUNKS + 2)), both1, act.snap(k + 1))

            def acc_out(h):
                act.wait_ge(attended[CH - 1], (h + 1) * CHUNKS)
                act.wait_ge(c_out, 2 * h - 2)
                act.copy(acc_raw[:, :], ps[:, B_ACC, :]).then_inc(c_acc, 1)

            def head(h, prev, nxt):
                if nxt:
                    q_hi(h + 1)
                if prev:
                    acc_out(h)
                act.wait_ge(c_vload, 16 * h + 16)
                parity = act.snap(h % 2)
                k0 = act.snap(h * CHUNKS)
                tile1(parity, 0, 0, act.snap(k0 + (CHUNKS + 1)), act.snap(k0 + CHUNKS), k0)
                step(parity, 0, k0, nxt, q_of=h + 1 if nxt else None)
                with act.Fori(0, TURNS) as n:
                    for u in range(UNROLL):
                        g = act.snap(n * UNROLL + (u + 1))
                        step(parity, g, act.snap(k0 + g), nxt)
                step(parity, CHUNKS - 1, act.snap(k0 + (CHUNKS - 1)), nxt, last=True)

            q_hi(0)
            with act.Fori(0, CHUNKS) as g:
                k_hi(g, act.snap(g + 1), None)
            q_moving(0, 0)
            q_moving(0, 1)
            head(0, False, True)
            with act.Fori(1, HEADS - 1) as h:
                head(h, True, True)
            head(HEADS - 1, True, False)
            acc_out(HEADS)

            std_of(4)
            turned(4, xn_t)
            turned(5, x3_t)
            act.wait_ge(g_exp, 1)
            act.activation(gp, gp, ACT.Exp).then_inc(g_exp, 1)
            act.wait_ge(g_cwt, 1)
            act.copy(halves(cw_t), ps[0:E1, 1:3, :]).then_inc(g_cwtsb, 1)

            def act_item(s, half, i1, i0):
                act.wait_ge(g_u[half], i1)
                act.wait_ge(g_h[half], i0)
                act.activation(silu[:, half, :], ps[:, half, :], ACT.Silu,
                               bias=pair_w[:, s, 3 * P:3 * P + 1]).then_inc(g_silu[half], 1)

            with act.Fori(0, G1 // 2) as i:
                i0 = act.snap(2 * i)
                i1 = act.snap(2 * i + 1)
                i2 = act.snap(2 * i + 2)
                for half in range(2):
                    act_item(0, half, i1, i0)
                for half in range(2):
                    act_item(1, half, i2, i1)
            for half in range(2):
                act_item(0, half, G1 + 1, G1)

        @block.vector
        def _(dve):
            def layernorm(n, src, dst):
                for t in range(TT):
                    ins = dve.bn_stats(stats[:, t, :], src[:, t, :])
                ins.then_inc(ln_stats, 1)
                dve.wait_ge(ln_stats, n + 1)
                for t in range(TT):
                    ins = dve.bn_aggr(mean_var[:, t, :], stats[:, t, :])
                ins.then_inc(ln_var, 1)
                dve.wait_ge(ln_std, n + 1)
                dve.reciprocal(rstd[:, :], std[:, :]).then_inc(ln_rstd, 1)
                dve.wait_ge(ln_rstd, n + 1)
                for t in range(TT):
                    ins = dve.tensor_scalar(dst[:, t, :], src[:, t, :], mean_var[:, t, 0:1], rstd[:, t:t + 1],
                                            ALU.subtract, ALU.mult)
                ins.then_inc(ln_out, 1)

            def turned(n, dst):
                dve.wait_ge(tr_psum, 2 * n + 2)
                dve.tensor_copy(dst[:, HALF:TOK], ps[:, 7, :]).then_inc(tr_dve, 1)

            dve.wait_ge(in_x, 32)
            dve.tensor_scalar(neg_ident[:, :], ident[:, :], -1.0, None, ALU.mult).then_inc(neg_ready, 1)
            layernorm(0, x_tok, xn)
            turned(0, xn_t)
            dve.wait_ge(in_a, 16 * 6)
            dve.wait_ge(a_q, 2)
            dve.tensor_scalar(halves(q0_t), ps[:, 3:5, :], bq0[:, :], None, ALU.add).then_inc(a_qsb, 1)
            for q in range(CH):
                part = slice(q * CHUNKS, (q + 1) * CHUNKS)
                dve.wait_ge(a_chi, q + 1)
                dve.tensor_tensor(keys_hl[0:CD, part, 1, :], ctx_f.rearrange("p (n k) -> p n k", k=KT)[:, part, :],
                                  f32(keys_hl[0:CD, part, 0, :]), ALU.subtract).then_inc(a_clo, 1)
                if q == 0:
                    dve.wait_ge(a_qhi, 1)
                    dve.tensor_tensor(halves(q_all[0:CD, :]), ps[0:CD, 0:2, :], halves(f32(q_max[0:CD, :])),
                                      ALU.subtract).then_inc(a_qlo, 1)
            dve.wait_ge(a_wvs, 1)
            dve.tensor_tensor(wv1_lo[:, :], wv1_f, f32(wv1_hi[:, :]), ALU.subtract).then_inc(a_wvs, 1)
            with dve.Fori(0, CHUNKS) as g:
                k1 = dve.snap(g + 1)
                for i in range(TT):
                    dve.wait_ge(max_scored[i], k1)
                    dve.tensor_reduce(chunk_max[:, i, bass.ds(g, 1)], ps[:, i % 4, 0:CK], AX,
                                      ALU.max).then_inc(max_reduced[i], 1)
            dve.wait_ge(max_reduced[TT - 1], CHUNKS)
            dve.tensor_reduce(row_max[:, :], chunk_max[:, :, :], AX, ALU.max).then_inc(max_found, 1)

            def fill0(n, j):
                dve.tensor_copy(kslot[0:CD + 1, j, :, :].rearrange("p a k -> p (a k)"),
                                f32(keys_hl[0:CD + 1, bass.ds(n, 1), :, :]).rearrange("p n a k -> p (n a k)")
                                ).then_inc(slot_keys[j], 1)

            dve.wait_ge(a_rows, 7)
            for j in range(CH):
                dve.wait_ge(a_vproj[j], CHUNKS)
                fill0(j, j)
            dve.wait_ge(tr_act, 1)
            dve.wait_ge(tr_dve, 1)
            dve.wait_ge(a_vevac[CH - 1], CHUNKS)
            dve.memset(ps[:, 6:8, :], 0.0).then_inc(a_acczero, 1)
            dve.wait_ge(max_row, 1)
            dve.tensor_tensor(halves(q_shift[CD:CD + 1, :]), ps[CD:CD + 1, 3:5, :], halves(f32(q_max[CD:CD + 1, :])),
                              ALU.add).then_inc(shifted, 1)
            with dve.Fori(0, CHUNKS - 1) as g:
                k1 = dve.snap(g + 1)
                n1 = dve.snap(g * CH + CH)
                for j in range(CH):
                    dve.wait_ge(scored[2 * j + 1], k1)
                    fill0(n1 + j, j)
            dve.wait_ge(attended[CH - 1], CHUNKS)
            dve.tensor_copy(o0[:, HALF:TOK], ps[0:CD + 1, 7, :]).then_inc(a_o, 1)
            dve.wait_ge(in_f0, 16 * 9)
            w1_e = w1_in.rearrange("p (e j) -> p e j", e=E0)
            dve.tensor_tensor(w1s.rearrange("p (e j) -> p e j", e=E0), w1_e,
                              sc0.unsqueeze(2).to_broadcast([P, E0, H0]), ALU.mult).then_inc(f_w, 1)
            dve.tensor_tensor(w1b.rearrange("p (e j) -> p e j", e=E0), w1_e,
                              bi0.unsqueeze(2).to_broadcast([P, E0, H0]), ALU.mult).then_inc(f_w, 1)
            dve.wait_ge(a_out, 1)
            out_tiles = ps[:, 0:4, :].rearrange("p b (u c) -> p b u c", u=2)
            dve.reciprocal(rsum0[:, :, :], out_tiles[:, :, :, D]).then_inc(a_rsum, 1)
            dve.wait_ge(a_rsum, 1)
            for t in range(TT):
                b, u = t % 4, t // 4
                ins = dve.scalar_tensor_tensor(out=x_tok[:, t, :], in0=out_tiles[:, b, u, 0:D],
                                               scalar=rsum0[:, b, u:u + 1], in1=x_tok[:, t, :],
                                               op0=ALU.mult, op1=ALU.add)
            ins.then_inc(a_x, 1)

            dve.wait_ge(f_bias, 1)
            dve.tensor_tensor(hb0, ps[:, 5, 0:G0], b1_0, ALU.add).then_inc(f_biassb, 1)
            dve.wait_ge(a_x, 1)
            layernorm(1, x_tok, xn)
            turned(1, xn_t)
            dve.wait_ge(ln_out, 2)
            layernorm(2, xn, xn2)
            dve.wait_ge(f_logits, 1)
            dve.tensor_copy(lg0, ps[:, 4, 0:TT * E0]).then_inc(f_step, 1)
            turned(2, xn_t)
            dve.wait_ge(f_step, 1)
            for t in range(TT):
                ins = dve.max(top8[:, t, :], lg0[:, t * E0:(t + 1) * E0])
            ins.then_inc(f_step, 1)
            dve.wait_ge(f_step, 2)
            for t in range(TT):
                ins = dve.max_index(idx8[:, t, :], top8[:, t, :], lg0[:, t * E0:(t + 1) * E0])
            ins.then_inc(f_step, 1)
            dve.wait_ge(f_step, 3)
            dve.tensor_copy(idxf8[:, :, :], idx8[:, :, :]).then_inc(f_step, 1)
            dve.wait_ge(f_step, 4)
            for t in range(TT):
                ins = dve.tensor_scalar(mask0[:, t, :], iota[:, 0:E0], idxf8[:, t, 0:1], None, ALU.is_equal)
            ins.then_inc(f_mask, 1)
            for n in range(2 * G0):
                g, half = n // 2, n % 2
                dve.wait_ge(f_gelu, n + 1)
                dve.wait_ge(f_spread, n + 1)
                dve.tensor_tensor(hid0[:, g, cols(half)], ps[:, (6 + n) % 8, :], hid0[:, g, cols(half)],
                                  ALU.mult).then_inc(f_masked, 1)
            dve.wait_ge(f_out, 1)
            dve.tensor_tensor(x_tok[:, :, :], ps[:, 2:4, :].rearrange("p b (t d) -> p (b t) d", d=D), x_tok[:, :, :],
                              ALU.add).then_inc(f_x, 1)

            dve.wait_ge(f_x, 1)
            layernorm(3, x_tok, xn)
            turned(3, xn_t)
            dve.wait_ge(in_c, 80)

            def q_lo(n):
                dve.wait_ge(c_qhi, n + 1)
                dve.tensor_tensor(halves(q_max[HD:P, :]), ps[HD:P, 3:5, :], halves(f32(q_max[HD:P, :])),
                                  ALU.subtract).then_inc(c_qlo, 1)

            def k_lo(g, kn):
                dve.wait_ge(c_khi, kn)
                dve.tensor_tensor(keys_hl[0:HD, bass.ds(g * CH, CH), 1, :],
                                  ps[0:HD, B_KP, 0:CK].rearrange("p (n k) -> p n k", k=KT),
                                  f32(keys_hl[0:HD, bass.ds(g * CH, CH), 0, :]), ALU.subtract).then_inc(c_klo, 1)

            def chunk_maxima(i, g, kn, banks):
                dve.wait_ge(max_scored[i], kn)
                dve.tensor_reduce(chunk_max[:, i, bass.ds(g, 1)], ps[:, banks[i % len(banks)], 0:CK], AX,
                                  ALU.max).then_inc(max_reduced[i], 1)

            def fill1(n, j):
                dve.tensor_copy(kslot[:, j, :, :].rearrange("p a k -> p (a k)"),
                                f32(keys_hl[:, bass.ds(n, 1), :, :]).rearrange("p n a k -> p (n a k)")
                                ).then_inc(slot_keys[j], 1)

            def add_output(h, part, banks):
                dve.wait_ge(c_out, 2 * h - 1 + part)
                for t in range(4 * part, 4 * part + 4):
                    ins = dve.scalar_tensor_tensor(out=x_tok[:, t, :], in0=ps[:, banks[part], tile_cols(t % 4)],
                                                   scalar=rden[:, t:t + 1], in1=x_tok[:, t, :],
                                                   op0=ALU.mult, op1=ALU.add)
                ins.then_inc(c_x, 1)

            def reciprocals(h):
                dve.wait_ge(c_sums, h)
                dve.wait_ge(c_x, 2 * h - 2)
                dve.reciprocal(rden[:, :], ps[:, B_AUX, 2 * P:2 * P + TT]).then_inc(c_rden, 1)
                dve.wait_ge(c_rden, h)

            def step(g, k, nxt, fill_at, output_of=None, first=False, banks=(3, 4, 7)):
                both1 = dve.snap(k + (CHUNKS + 1))
                if nxt:
                    both_kn = dve.snap(k + (2 * CHUNKS + 1))
                if fill_at is not None:
                    k2 = dve.snap(k + 2)
                for j in range(CH):
                    if fill_at is not None:
                        dve.wait_ge(scored[2 * j + 1], both1)
                        if j == 0:
                            dve.wait_ge(c_klo, k2)
                            dve.wait_ge(c_khi, k2)
                        fill1(fill_at + j, j)
                    if nxt and j == 0:
                        k_lo(g, both1)
                    if output_of is not None and j == 0:
                        reciprocals(output_of)
                    maxima = ((0, 1), (2, 3, 4), (5, 6, 7))[j]
                    for i in maxima:
                        if output_of is not None and j and i == maxima[-1]:
                            add_output(output_of, j - 1, (B_AUX, B_AUX))
                        if nxt:
                            chunk_maxima(i, g, both_kn, banks)
                    if j == CH - 1:
                        dve.wait_ge(exped[2 * CH - 1], both1)
                        if first:
                            dve.tensor_copy(psum_dve, probs[:, CH - 1, HALF:TOK]).then_inc(c_dadd, 1)
                        else:
                            dve.wait_ge(c_dadd, k)
                            dve.tensor_tensor(psum_dve, psum_dve, probs[:, CH - 1, HALF:TOK], ALU.add).then_inc(c_dadd, 1)

            def copy_wo(h, prev_index):
                dve.wait_ge(c_out, 2 * h - 2)
                dve.tensor_copy(wo_slot[:, :], wo1[:, bass.ds(prev_index, 1), :].rearrange("p a d -> p (a d)")).then_inc(c_wo, 1)

            def head(h, prev, nxt):
                dve.wait_ge(max_reduced[TT - 1], (h + 2) * CHUNKS)
                dve.tensor_reduce(row_max[:, :], chunk_max[:, :, :], AX, ALU.max).then_inc(max_found, 1)
                if prev:
                    copy_wo(h, h - 1)
                slot = dve.snap(h % 2) if prev else 0
                dve.wait_ge(max_row, h + 2)
                dve.tensor_tensor(q_shift2[HD:HD + TT, bass.ds(slot, 1), :].rearrange("p a (t c) -> p (a t) c", c=P),
                                  ps[HD:HD + TT, B_AUX, 0:P].unsqueeze(1).to_broadcast([TT, TT, P]),
                                  diag[HD:HD + TT, :].unsqueeze(2).to_broadcast([TT, TT, P]), ALU.mult).then_inc(shifted, 1)
                if prev:
                    dve.wait_ge(c_acc, h)
                dve.memset(ps[:, B_ACC, :], 0.0).then_inc(c_acczero, 1)
                if nxt:
                    q_lo(h + 1)
                k0 = dve.snap(h * CHUNKS)
                step(0, k0, nxt, CH, output_of=h if prev else None, first=True, banks=(3, 4))
                with dve.Fori(0, TURNS) as n:
                    for u in range(UNROLL):
                        g = dve.snap(n * UNROLL + (u + 1))
                        step(g, dve.snap(k0 + g), nxt, dve.snap(g * CH + CH))
                step(CHUNKS - 1, dve.snap(k0 + (CHUNKS - 1)), nxt, 0 if nxt else None)

            q_lo(0)
            with dve.Fori(0, CHUNKS) as g:
                k1 = dve.snap(g + 1)
                k_lo(g, k1)
                both1 = dve.snap(g + (CHUNKS + 1))
                for i in range(TT):
                    chunk_maxima(i, g, both1, (0, 1, 2, 7))
            dve.wait_ge(c_rows, 4)
            dve.wait_ge(c_klo, CHUNKS)
            for j in range(CH):
                dve.wait_ge(scored[2 * j + 1], CHUNKS)
                fill1(j, j)
            for j in range(CH):
                dve.wait_ge(a_vout[j], 16 * CHUNKS)
            dve.tensor_tensor(x_tok[:, :, :], x_tok[:, :, :], bo1[:, :].unsqueeze(1).to_broadcast([P, TT, D]),
                              ALU.add).then_inc(c_bo, 1)
            dve.wait_ge(c_bo, 1)
            head(0, False, True)
            with dve.Fori(1, HEADS - 1) as h:
                head(h, True, True)
            head(HEADS - 1, True, False)
            copy_wo(HEADS, HEADS - 1)
            reciprocals(HEADS)
            for part in range(2):
                add_output(HEADS, part, (3, 4))

            dve.wait_ge(c_x, 2 * HEADS)
            layernorm(4, x_tok, xn)
            turned(4, xn_t)
            turned(5, x3_t)
            steps = [0]

            def link(ins):
                steps[0] += 1
                ins.then_inc(g_step, 1)
                dve.wait_ge(g_step, steps[0])

            dve.wait_ge(g_logits, 1)
            logits = ps[:, 0, 0:TT * E1].rearrange("p (t e) -> p t e", e=E1)

            def over(col, *shape):
                return col.unsqueeze(len(shape)).to_broadcast([P, *shape])

            link(dve.tensor_reduce(gm, logits, AX, ALU.max))
            dve.tensor_tensor(gp, logits, over(gm, TT, E1), ALU.subtract).then_inc(g_exp, 1)
            dve.wait_ge(g_exp, 2)
            link(dve.tensor_reduce(gs, gp, AX, ALU.add))
            link(dve.reciprocal(gm, gs))
            link(dve.tensor_tensor(gl, gp, over(gm, TT, E1), ALU.mult))
            members = gl.rearrange("p t (g m) -> p t g m", m=E1 // GROUPS)
            dve.tensor_tensor(pmax, members[:, :, :, 0], members[:, :, :, 1], ALU.max)
            dve.tensor_tensor(pmin, members[:, :, :, 0], members[:, :, :, 1], ALU.min)
            dve.tensor_tensor(qmax, members[:, :, :, 2], members[:, :, :, 3], ALU.max)
            link(dve.tensor_tensor(qmin, members[:, :, :, 2], members[:, :, :, 3], ALU.min))
            link(dve.tensor_tensor(pmin, pmin, qmin, ALU.max))
            link(dve.tensor_tensor(qmin, pmax, qmax, ALU.min))
            link(dve.tensor_tensor(pmax, pmax, qmax, ALU.max))
            link(dve.tensor_tensor(pmin, pmin, qmin, ALU.max))
            link(dve.tensor_tensor(pmax, pmax, pmin, ALU.add))

            def first_four(values, width, chosen):
                for t in range(TT):
                    ins = dve.max(top8[:, t, :], values[:, t, :])
                link(ins)
                for t in range(TT):
                    ins = dve.max_index(idx8[:, t, :], top8[:, t, :], values[:, t, :])
                link(ins)
                link(dve.tensor_copy(idxf8[:, :, :], idx8[:, :, :]))
                for t in range(TT):
                    ins = dve.tensor_scalar(chosen[:, t, :], iota[:, 0:width], idxf8[:, t, 0:1], None, ALU.is_equal)
                link(ins)
                for r in range(1, TOPK):
                    for t in range(TT):
                        ins = dve.scalar_tensor_tensor(out=chosen[:, t, :], in0=iota[:, 0:width],
                                                       scalar=idxf8[:, t, r:r + 1], in1=chosen[:, t, :],
                                                       op0=ALU.is_equal, op1=ALU.add)
                    link(ins)

            first_four(pmax, GROUPS, keep)
            link(dve.tensor_scalar(keep, keep, 2.0, -2.0, ALU.mult, ALU.add))
            link(dve.tensor_tensor(gp.rearrange("p t (g m) -> p t g m", m=E1 // GROUPS), members,
                                   over(keep, TT, GROUPS, E1 // GROUPS), ALU.add))
            first_four(gp, E1, cw)
            dve.tensor_tensor(cw, cw, gl, ALU.mult).then_inc(g_cw, 1)
            dve.wait_ge(g_cwtsb, 1)
            link(dve.tensor_copy(cw_3[0:E1, :], cw_t))
            link(dve.tensor_tensor(cw_r, cw_t, cw_3[0:E1, :], ALU.subtract))
            link(dve.tensor_copy(cw_b[:, :], cw_r))
            link(dve.tensor_copy(cw_3[E1:2 * E1, :], cw_b[:, :]))
            link(dve.tensor_tensor(cw_r, cw_r, cw_b[:, :], ALU.subtract))
            dve.tensor_copy(cw_3[2 * E1:3 * E1, :], cw_r).then_inc(g_spread_ready, 1)

            def gated(s, half, i1, i0, shared=False):
                dve.wait_ge(g_silu[half], i1)
                dve.wait_ge(g_y[half], i0)
                ins = dve.scalar_tensor_tensor(out=hgate[:, half, :], in0=ps[:, 2 + half, :],
                                               scalar=pair_w[:, s, 3 * P + 1:3 * P + 2], in1=silu[:, half, :],
                                               op0=ALU.add, op1=ALU.mult)
                ins.then_inc(g_h[half], 1)
                if not shared:
                    dve.wait_ge(g_h[half], i1)
                    dve.wait_ge(g_gate[half], i1)
                    dve.tensor_tensor(hgate[:, half, :], ps[:, 4 + half, :], hgate[:, half, :],
                                      ALU.mult).then_inc(g_hg[half], 1)

            with dve.Fori(0, G1 // 2) as i:
                i0 = dve.snap(2 * i)
                i1 = dve.snap(2 * i + 1)
                i2 = dve.snap(2 * i + 2)
                for half in range(2):
                    gated(0, half, i1, i0)
                for half in range(2):
                    gated(1, half, i2, i1)
            for half in range(2):
                gated(0, half, G1 + 1, G1, shared=True)
            for half in range(2):
                dve.wait_ge(g_y[half], G1 + 1)
                dve.scalar_tensor_tensor(out=x3_t[:, cols(half)], in0=ps[:, 6 + half, :], scalar=sb2[:, :],
                                         in1=x3_t[:, cols(half)], op0=ALU.add, op1=ALU.add).then_inc(g_fin[half], 1)

        @block.tensor
        def _(pe):
            def turn(n, src):
                for t in range(TT):
                    ins = pe.transpose(ps[:, 6 + t // 4, tile_cols(t % 4)], src[:, t, :], ident[:, :])
                    if t % 4 == 3:
                        ins.then_inc(tr_psum, 1)

            def turned(n):
                pe.wait_ge(tr_act, n + 1)
                pe.wait_ge(tr_dve, n + 1)

            pe.wait_ge(in_x, 32)
            pe.wait_ge(ln_out, 1)
            turn(0, xn)
            turned(0)
            pe.wait_ge(in_a, 16 * 6)
            for half in range(2):
                pe.matmul(ps[:, 3 + half, :], wq0[:, :], xn_t[:, cols(half)], start=True, stop=True).then_inc(a_q, 1)
            pe.wait_ge(a_qsb, 1)
            for half in range(2):
                pe.matmul(ps[0:CD + 1, half, :], wkt0[:, :], q0_t[:, cols(half)], start=True, stop=True).then_inc(a_qk, 1)
            pe.wait_ge(a_qhi, 1)
            pe.wait_ge(a_chi, CH)
            pe.wait_ge(a_rows, 7)
            pe.wait_ge(a_qlo, 1)
            pe.wait_ge(a_wvs, 2)
            with pe.Fori(0, CHUNKS) as g:
                k1 = pe.snap(g + 1)
                for i in range(TT):
                    pe.wait_ge(max_reduced[(i - 4) % TT], k1 if i >= 4 else g)
                    pe.matmul(ps[:, i % 4, 0:CK], q_max[0:CD + 1, tile_cols(i)],
                              keys_hl[0:CD + 1, bass.ds(g * CH, CH), 0, :], start=True, stop=True).then_inc(max_scored[i], 1)
                    if i in (2, 4, 6):
                        j = i // 2 - 1
                        pe.wait_ge(a_vkeys[j], k1)
                        pe.wait_ge(a_vevac[j], g)
                        v = ps[0:KT, 4 + j, :]
                        pe.matmul(v, kslot[0:CD, j, 0, :], wv1_hi[:, :], start=True, stop=False)
                        pe.matmul(v, kslot[0:CD, j, 0, :], wv1_lo[:, :], start=False, stop=False)
                        pe.matmul(v, kslot[0:CD, j, 1, :], wv1_hi[:, :], start=False, stop=True).then_inc(a_vproj[j], 1)

            pe.wait_ge(max_found, 1)
            pe.wait_ge(neg_ready, 1)
            pe.wait_ge(a_vevac[0], CHUNKS)
            for t in range(TT):
                ins = pe.matmul(ps[CD:CD + 1, B_MX + t // 4, tile_cols(t % 4)], row_max[:, t:t + 1], neg_ident[:, :],
                                start=True, stop=True)
            ins.then_inc(max_row, 1)

            def scores0(jj, kv, kp):
                pe.wait_ge(slot_keys[jj], kv)
                for half in range(2):
                    u = 2 * jj + half
                    pe.wait_ge(exped[(u + 3) % 6], kv if u >= 3 else kp)
                    s = ps[0:KT, u % 3, :]
                    pe.matmul(s, kslot[0:CD + 1, jj, 0, :], q_shift[0:CD + 1, cols(half)], start=True, stop=False)
                    pe.matmul(s, kslot[0:CD, jj, 0, :], q_all[0:CD, cols(half)], start=False, stop=False)
                    pe.matmul(s, kslot[0:CD + 1, jj, 1, :], q_pad[0:CD + 1, cols(half)], start=False,
                              stop=True).then_inc(scored[u], 1)

            def attend0(j, k1, k16):
                for half in range(2):
                    pe.wait_ge(exped[2 * j + half], k1)
                pe.wait_ge(a_cslot[j], k16)
                for half in range(2):
                    ins = pe.matmul(ps[0:CD + 1, 6 + half, :], vslot[:, j, 0:CD + 1], probs[:, j, cols(half)],
                                    start=False, stop=False, skip_group_check=True)
                ins.then_inc(attended[j], 1)

            pe.wait_ge(shifted, 1)
            pe.wait_ge(a_qcopy, 2)
            pe.wait_ge(a_acczero, 1)
            scores0(0, 1, 0)
            with pe.Fori(0, CHUNKS - 1) as g:
                k1 = pe.snap(g + 1)
                k16 = pe.snap(g * 16 + 16)
                for j in range(CH):
                    scores0((j + 1) % CH, k1 if j < CH - 1 else pe.snap(g + 2), g if j < CH - 1 else k1)
                    attend0(j, k1, k16)
            for j in range(CH):
                if j < CH - 1:
                    scores0(j + 1, CHUNKS, CHUNKS - 1)
                attend0(j, CHUNKS, 16 * CHUNKS)
            pe.wait_ge(a_o, 2)
            for t in range(TT):
                ins = pe.matmul(ps[:, t % 4, (t // 4) * 256:(t // 4) * 256 + D + 1], o0[:, tile_cols(t)], wv0[:, :],
                                start=True, stop=True)
            ins.then_inc(a_out, 1)

            pe.wait_ge(f_w, 2)
            pe.wait_ge(consts, 3)
            for g in range(G0):
                ins = pe.matmul(ps[:, 5, g:g + 1], w1b[:, tile_cols(g)], ones[:, 0:1], start=True, stop=True)
            ins.then_inc(f_bias, 1)
            pe.wait_ge(ln_out, 2)
            turn(1, xn)
            turned(1)
            pe.wait_ge(in_f0, 16 * 9)
            for t in range(TT):
                ins = pe.matmul(ps[:, 4, t * E0:(t + 1) * E0], xn_t[:, tile_cols(t)], wgt, start=True, stop=True)
            ins.then_inc(f_logits, 1)
            pe.wait_ge(ln_out, 3)
            turn(2, xn2)
            turned(2)
            pe.wait_ge(a_x, 1)
            pe.wait_ge(f_step, 1)
            pe.wait_ge(f_biassb, 1)
            for n in range(2 * G0):
                g, half = n // 2, n % 2
                pe.matmul(ps[:, 2 + n, :], w1s[:, tile_cols(g)], xn_t[:, cols(half)], start=True, stop=True).then_inc(f_hid, 1)
            pe.wait_ge(f_mask, 1)
            for t in range(TT):
                ins = pe.transpose(ps[0:E0, t // 4, tile_cols(t % 4)], mask0[:, t, :], ident[:, :])
            ins.then_inc(f_maskt, 1)
            pe.wait_ge(f_masktsb, 1)
            for n in range(2 * G0):
                g, half = n // 2, n % 2
                pe.matmul(ps[:, (6 + n) % 8, :], spread0[:, g, :], mask_t[:, cols(half)], start=True, stop=True).then_inc(f_spread, 1)
            pe.wait_ge(f_masked, 2 * G0)
            for t in range(TT):
                o = ps[:, 2 + t // 4, tile_cols(t % 4)]
                for g in range(G0):
                    pe.matmul(o, hid0[:, g, tile_cols(t)], w2_0[:, g, :], start=(g == 0), stop=False)
                ins = pe.matmul(o, mask_t[:, tile_cols(t)], b2_0[:, :], start=False, stop=True)
            ins.then_inc(f_out, 1)

            pe.wait_ge(ln_out, 4)
            turn(3, xn)
            turned(3)
            pe.wait_ge(in_c, 80)

            def q_proj(n):
                for half in range(2):
                    ins = pe.matmul(ps[:, 3 + half, :], wq1[:, :], xn_t[:, cols(half)], start=True, stop=True)
                ins.then_inc(c_qproj, 1)

            def k_proj(g, kb):
                pe.wait_ge(c_klo, kb)
                pe.matmul(ps[:, B_KP, 0:CK], wk1[:, :], ctx_f[:, bass.ds(g * CK, CK)], start=True, stop=True).then_inc(c_kp, 1)

            def max_scores(i, g, kn, both_kn, both_kb, banks):
                if i == 0:
                    pe.wait_ge(c_khi, kn)
                if i >= len(banks):
                    pe.wait_ge(max_reduced[i - len(banks)], both_kn)
                elif both_kb is not None:
                    last = [n for n in range(TT) if n % len(banks) == i][-1]
                    pe.wait_ge(max_reduced[last], both_kb)
                pe.matmul(ps[:, banks[i % len(banks)], 0:CK], q_max[:, tile_cols(i)],
                          keys_hl[:, bass.ds(g * CH, CH), 0, :], start=True, stop=True).then_inc(max_scored[i], 1)

            def scores1(jj, kv, kp, slot):
                pe.wait_ge(slot_keys[jj], kv)
                for half in range(2):
                    u = 2 * jj + half
                    pe.wait_ge(exped[(u + 3) % 6], kv if u >= 3 else kp)
                    s = ps[0:KT, u % 3, :]
                    pe.matmul(s, kslot[:, jj, 0, :], flat(q_all2[:, bass.ds(slot, 1), cols(half)]), start=True, stop=False)
                    pe.matmul(s, kslot[0:CD + 1, jj, 1, :], flat(q_shift2[:, bass.ds(slot, 1), cols(half)]), start=False,
                              stop=True).then_inc(scored[u], 1)

            def attend1(j, k1, both1):
                for half in range(2):
                    pe.wait_ge(exped[2 * j + half], both1)
                pe.wait_ge(c_vslot[j], k1)
                for half in range(2):
                    ins = pe.matmul(ps[half * HD:(half + 1) * HD, B_ACC, :], vslot[:, j, 0:HD],
                                    probs[:, j, cols(half)], start=False, stop=False, skip_group_check=True)
                ins.then_inc(attended[j], 1)

            def sum_rows(h):
                pe.wait_ge(c_total, h)
                for t in range(TT):
                    ins = pe.matmul(ps[:, B_AUX, 2 * P + t:2 * P + t + 1], psum_pool[:, tile_cols(t)], ones[0:KT, 0:1],
                                    start=True, stop=True)
                ins.then_inc(c_sums, 1)

            def project_out(h, part, bank, bias):
                if part == 0:
                    pe.wait_ge(c_acc, h)
                    pe.wait_ge(c_wo, h)
                    pe.wait_ge(c_rden, h)
                elif not bias:
                    pe.wait_ge(c_x, 2 * h - 1)
                rows = slice(part * HD, (part + 1) * HD)
                for u in range(4):
                    ins = pe.matmul(ps[:, bank, tile_cols(u)], acc_raw[rows, tile_cols(u)], wo_slot[rows, :],
                                    start=True, stop=True)
                ins.then_inc(c_out, 1)

            def step(slot, g, k, nxt, last=False, start_of=None, output_of=None, x_added=None, banks=(3, 4, 7), tail=True):
                k1 = pe.snap(k + 1)
                both = pe.snap(k + CHUNKS)
                both1 = pe.snap(k + (CHUNKS + 1))
                if nxt:
                    both_kb = pe.snap(k + 2 * CHUNKS) if len(banks) > 2 else None
                    both_kn = pe.snap(k + (2 * CHUNKS + 1))
                    k_proj(g, both)

                def maxima(*which):
                    for i in which:
                        if nxt:
                            max_scores(i, g, both1, both_kn, both_kb, banks)

                scores1(1, both1, both, slot)
                if output_of is not None:
                    sum_rows(output_of)
                if start_of is not None:
                    pe.wait_ge(c_acczero, start_of + 1)
                    if nxt:
                        pe.wait_ge(c_qlo, start_of + 2)
                attend1(0, k1, both1)
                maxima(0, 1)
                scores1(2, both1, both, slot)
                if x_added is not None and nxt:
                    pe.wait_ge(c_x, x_added)
                maxima(2, 3)
                attend1(1, k1, both1)
                if output_of is not None:
                    project_out(output_of, 0, B_AUX, False)
                maxima(4)
                if not last:
                    scores1(0, pe.snap(k + (CHUNKS + 2)), both1, slot)
                maxima(5, 6)
                if tail:
                    attend1(2, k1, both1)
                if output_of is not None:
                    project_out(output_of, 1, B_AUX, False)
                maxima(7)

            def head(h, prev, nxt):
                if nxt:
                    pe.wait_ge(c_wq, 16 * h + 16)
                    pe.wait_ge(c_wk, 16 * h + 16)
                    for i in (TT - 2, TT - 1):
                        pe.wait_ge(max_reduced[i], (h + 2) * CHUNKS)
                    q_proj(h + 1)
                pe.wait_ge(max_found, h + 2)
                pe.matmul(ps[HD:HD + TT, B_AUX, 0:P], row_max[:, :], neg_ident[:, :], start=True, stop=True).then_inc(max_row, 1)
                k0 = pe.snap(h * CHUNKS)
                slot = 0
                if prev:
                    slot = pe.snap(h % 2)
                    attend1(CH - 1, k0, pe.snap(k0 + CHUNKS))
                both, both1 = pe.snap(k0 + CHUNKS), pe.snap(k0 + (CHUNKS + 1))
                pe.wait_ge(shifted, h + 2)
                pe.wait_ge(c_qcopy, 2 * h + 2)
                scores1(0, both1, both, slot)
                step(slot, 0, k0, nxt, start_of=h, output_of=h if prev else None, banks=(3, 4))
                x_added = pe.snap(2 * h) if prev else None
                with pe.Fori(0, TURNS) as n:
                    for u in range(UNROLL):
                        g = pe.snap(n * UNROLL + (u + 1))
                        step(slot, g, pe.snap(k0 + g), nxt, x_added=x_added)
                step(slot, CHUNKS - 1, pe.snap(k0 + (CHUNKS - 1)), nxt, last=True, tail=not nxt)

            q_proj(0)
            pe.wait_ge(c_qlo, 1)
            k_proj(0, 0)

            def first_maxima(g, k1, both0, both1, last):
                for i in range(TT):
                    max_scores(i, g, k1, both1, both0, (0, 1, 2, 7))
                    if i == 0 and not last:
                        k_proj(g + 1, k1)

            with pe.Fori(0, CHUNKS - 1) as g:
                first_maxima(g, pe.snap(g + 1), pe.snap(g + CHUNKS), pe.snap(g + (CHUNKS + 1)), False)
            first_maxima(CHUNKS - 1, CHUNKS, 2 * CHUNKS - 1, 2 * CHUNKS, True)
            pe.wait_ge(c_rows, 4)
            head(0, False, True)
            with pe.Fori(1, HEADS - 1) as h:
                head(h, True, True)
            head(HEADS - 1, True, False)
            pe.wait_ge(c_x, 2 * HEADS - 2)
            sum_rows(HEADS)
            for part in range(2):
                project_out(HEADS, part, 3 + part, True)

            pe.wait_ge(ln_out, 5)
            turn(4, xn)
            turned(4)
            turn(5, x_tok)
            pe.wait_ge(in_f1, 16 * 5)
            for t in range(TT):
                o = ps[:, 0, t * E1:(t + 1) * E1]
                pe.matmul(o, xn_t[:, tile_cols(t)], gw[:, :], start=True, stop=False)
                ins = pe.matmul(o, ones[0:1, :], gb[:, :], start=False, stop=True)
            ins.then_inc(g_logits, 1)
            pe.wait_ge(g_cw, 1)
            for t in range(TT):
                ins = pe.transpose(ps[0:E1, 1 + t // 4, tile_cols(t % 4)], cw[:, t, :], ident[:, :])
            ins.then_inc(g_cwt, 1)
            pe.wait_ge(g_cwtsb, 1)
            turned(5)
            for half in range(2):
                pe.matmul(ps[:, 6 + half, :], b2_1[:, :], cw_t[:, cols(half)], start=True, stop=False, skip_group_check=True)
            pe.wait_ge(g_spread_ready, 1)

            def up(s, half, i, i0, w16, shared=False):
                pe.wait_ge(g_w[s], w16)
                pe.wait_ge(g_h[half], i0)
                xs = xn_t[:, cols(half)]
                pe.matmul(ps[:, half, :], pair_w[:, s, 0:P], xs, start=True, stop=True)
                pe.matmul(ps[:, 2 + half, :], pair_w[:, s, P:2 * P], xs, start=True, stop=True).then_inc(g_u[half], 1)
                if not shared:
                    pe.wait_ge(g_hg[half], i0)
                    pe.matmul(ps[:, 4 + half, :], spread1[:, bass.ds(i, 1), :].rearrange("p a c -> p (a c)"),
                              cw_3[:, cols(half)], start=True, stop=True).then_inc(g_gate[half], 1)

            def down(s, half, i1, shared=False):
                if shared:
                    pe.wait_ge(g_h[half], i1)
                else:
                    pe.wait_ge(g_hg[half], i1)
                pe.matmul(ps[:, 6 + half, :], pair_w[:, s, 2 * P:3 * P], hgate[:, half, :], start=False, stop=shared,
                          skip_group_check=True).then_inc(g_y[half], 1)

            def two_pairs(i, last):
                i0 = pe.snap(2 * i)
                i1 = pe.snap(2 * i + 1)
                i2 = pe.snap(2 * i + 2)
                w = pe.snap(16 * i + 16)
                up(0, 1, i0, i0, w)
                down(0, 0, i1)
                up(1, 0, i1, i1, w)
                down(0, 1, i1)
                up(1, 1, i1, i1, w)
                down(1, 0, i2)
                up(0, 0, i2, i2, pe.snap(16 * i + 32), shared=last)
                down(1, 1, i2)

            up(0, 0, 0, 0, 16)
            with pe.Fori(0, G1 // 2 - 1) as i:
                two_pairs(i, False)
            two_pairs(G1 // 2 - 1, True)
            up(0, 1, G1, G1, 16 * (G1 // 2) + 16, shared=True)
            for half in range(2):
                down(0, half, G1 + 1, shared=True)


def kernel(**inputs):
    import numpy as np
    import concourse.bacc as bacc
    import ml_dtypes
    from concourse.bass_utils import run_bass_kernel_spmd

    a = {n: np.asarray(v) for n, v in inputs.items()}
    c = np.ascontiguousarray
    context = a["ctx_768"][0]
    context = np.concatenate([context, context[KEYS - (PADDED - KEYS):]], 0)
    w1, w3, w2 = a["L1_ffn_w1"], a["L1_ffn_w3"], a["L1_ffn_w2"]
    pairs = [np.concatenate([w1[2 * i], w1[2 * i + 1], w3[2 * i], w3[2 * i + 1],
                             w2[2 * i:2 * i + 2].reshape(P, D),
                             a["L1_ffn_b1"][2 * i:2 * i + 2].reshape(P, 1),
                             a["L1_ffn_b3"][2 * i:2 * i + 2].reshape(P, 1)], 1) for i in range(G1)]
    pairs.append(np.concatenate([a["L1_ffn_sw1"], a["L1_ffn_sw3"], a["L1_ffn_sw2"],
                                 a["L1_ffn_sb1"].reshape(P, 1), a["L1_ffn_sb3"].reshape(P, 1)], 1))
    wq = a["L1_xattn_Wq"].reshape(D, HEADS, HD).transpose(1, 0, 2)
    wk = a["L1_xattn_Wk"].reshape(CD, HEADS, HD).transpose(1, 0, 2)
    wo = a["L1_xattn_Wo"].reshape(HEADS, HD, D).transpose(1, 0, 2)
    spread0 = np.zeros((E0, G0, P), np.float32)
    for e in range(E0):
        spread0[e, e // EG0, (e % EG0) * H0:(e % EG0 + 1) * H0] = 1.0
    spread1 = np.zeros((3 * E1, G1, P), ml_dtypes.bfloat16)
    for e in range(E1):
        for part in range(3):
            spread1[part * E1 + e, e // 2, (e % 2) * H1:(e % 2 + 1) * H1] = 1.0
    arrays = {
        "x": a["x"][0],
        "ctx_rows": context,
        "ctx_t": context.T,
        "a_wq": a["L0_xattn_Wq"],
        "a_bq": a["L0_xattn_bq"].reshape(D, 1),
        "a_wkt": a["L0_xattn_Wk"].T,
        "a_bk": a["L0_xattn_bk"].reshape(D, 1),
        "a_wv": a["L0_xattn_Wv"],
        "a_bv": a["L0_xattn_bv"].reshape(1, D),
        "f0_wgt": a["L0_ffn_Wg"].T,
        "f0_scale": a["L0_ffn_ln_scale"].T,
        "f0_bias": a["L0_ffn_ln_bias"].T,
        "f0_w1": a["L0_ffn_W1"].transpose(1, 0, 2).reshape(D, E0 * H0),
        "f0_b1": a["L0_ffn_b1"].reshape(G0, P).T,
        "f0_w2": a["L0_ffn_W2"].reshape(G0, P, D).transpose(1, 0, 2),
        "f0_b2": a["L0_ffn_b2"],
        "c_wq": np.concatenate([wq, wq], 2),
        "c_wk": np.concatenate([wk, wk], 2),
        "c_wv": a["L1_xattn_Wv"],
        "c_wo": np.concatenate([wo, wo], 0),
        "c_bo": np.tile(a["L1_xattn_bo"], (P, 1)),
        "f1_gw": a["L1_ffn_gw"],
        "f1_gb": a["L1_ffn_gb"].reshape(1, E1),
        "f1_pairs": np.stack(pairs),
        "f1_b2": a["L1_ffn_b2"],
        "f1_sb2": a["L1_ffn_sb2"].reshape(D, 1),
        "ident": np.eye(P, dtype=np.float32),
        "iota": np.tile(np.arange(E1, dtype=np.float32), (P, 1)),
        "spread0": spread0,
        "spread1": spread1,
    }
    arrays = {f"in_{n}": c(v) for n, v in arrays.items()}
    nc = bacc.Bacc("TRN2", target_bir_lowering=False, num_devices=1)
    args = [nc.dram_tensor(n, v.shape, mybir.dt.from_np(v.dtype), kind="ExternalInput").ap() for n, v in arrays.items()]
    out_t = nc.dram_tensor("out_t", [D, TOK], F32, kind="ExternalOutput").ap()
    build_program(nc, *args, out_t)
    r = run_bass_kernel_spmd(nc, [arrays], core_ids=[0])
    return r.results[0]["out_t"].T.reshape(1, TOK, D)
```

```python
from contextlib import ExitStack

import concourse.bass as bass
from concourse import mybir

F32 = mybir.dt.float32
F32R = mybir.dt.float32r
BF16 = mybir.dt.bfloat16
U32 = mybir.dt.uint32
ALU = mybir.AluOpType
ACT = mybir.ActivationFunctionType
AX = mybir.AxisListType.X

P = 128
TOK = 1024
TT = TOK // P
HALF = TOK // 2
D = 128
KEYS = 6404
CD = 96
KT = 126
TILES = 51
CH = 3
CHUNKS = TILES // CH
CK = CH * KT
PADDED = TILES * KT
PAD_AT = KEYS - (TILES - 1) * KT
HEADS = 8
HD = 64
E0, H0 = 8, 32
EG0 = P // H0
G0 = E0 // EG0
E1, H1 = 32, 64
G1 = E1 * H1 // P
GROUPS, TOPK = 8, 4
EPS = 1e-5
PAD_SCORE = -1e30
PAIR_W = 3 * P + 2
B_MX, B_KP, B_AUX, B_ACC = 3, 5, 6, 7
Q_BANKS = (B_KP, B_AUX)
UNROLL = 3
TURNS = (CHUNKS - 2) // UNROLL


def build_program(nc, x, ctx_rows, ctx_t, a_wq, a_bq, a_wkt, a_bk, a_wv, a_bv,
                  f0_wgt, f0_scale, f0_bias, f0_w1, f0_b1, f0_w2, f0_b2,
                  c_wq_in, c_wk_in, c_wv_in, c_wo_in, c_bo_in,
                  f1_gw, f1_gb, f1_pairs, f1_b2, f1_sb2,
                  ident_in, iota_in, spread0_in, spread1_in, out_t):
    with ExitStack() as ctx:
        def sb(name, shape, dt=F32):
            return ctx.enter_context(nc.sbuf_tensor(name, shape, dt))

        def sem(name):
            return ctx.enter_context(nc.semaphore(name))

        def sems(name, n):
            return [sem(f"{name}{i}") for i in range(n)]

        v_dram = nc.dram_tensor("v_scratch", [TILES, KT, HEADS * HD], F32, kind="Internal").ap()

        ps = ctx.enter_context(nc.psum_tensor("ps", [P, 8, HALF], F32))

        ident = sb("ident", [P, P])
        neg_ident = sb("neg_ident", [P, P])
        ones = sb("ones", [P, P])
        iota = sb("iota", [P, E1])
        eps_col = sb("eps_col", [P, 1])
        zero_col = sb("zero_col", [P, 1])
        x_tok = sb("x_tok", [P, TT, D])
        xn = sb("xn", [P, TT, D])
        xn2 = sb("xn2", [P, TT, D])
        xn_t = sb("xn_t", [P, TOK])
        stats = sb("stats", [P, TT, 6])
        mean_var = sb("mean_var", [P, TT, 2])
        std = sb("std", [P, TT])
        rstd = sb("rstd", [P, TT])
        ctx_mem = sb("ctx_mem", [P, PADDED])
        ctx_f = ctx_mem[0:CD, :]
        keys_hl = sb("keys_hl", [P, TILES, 2, KT], F32R)
        kslot = sb("kslot", [P, CH, 2, KT], F32R)
        vslot = sb("vslot", [KT, CH, P])
        probs = sb("probs", [KT, CH, TOK])
        k_full = probs[0:HD, 0, 0:CK].rearrange("p (n k) -> p n k", k=KT)
        q_max = sb("q_max", [P, TOK], F32R)
        q_all2 = sb("q_all2", [P, 2, TOK], F32R)
        q_shift2 = sb("q_shift2", [P, 2, TOK], F32R)
        q_all, q_shift = q_all2[:, 0, :], q_shift2[:, 0, :]
        q_pad = sb("q_pad", [97, TOK], F32R)
        chunk_max = sb("chunk_max", [P, TT, CHUNKS])
        row_max = sb("row_max", [P, TT])
        v_mem = sb("v_mem", [P, 2 * TILES * HD])
        v_head = v_mem[0:KT, :].rearrange("p (b f) -> p b f", b=2)
        v_tiles = v_head.rearrange("p b (n d) -> p b n d", n=TILES)
        wq0 = sb("wq0", [P, D])
        bq0 = sb("bq0", [P, 1])
        wkt0 = sb("wkt0", [P, CD + 1])
        wv0 = sb("wv0", [CD + 1, D + 1])
        q0_t = v_mem[:, 0:TOK]
        o0 = v_mem[0:CD + 1, TOK:2 * TOK]
        rsum0 = sb("rsum0", [P, 4, 2])
        wv1_f = v_mem[0:CD, 2 * TOK:2 * TOK + HEADS * HD]
        wv1_hi = sb("wv1_hi", [P, HEADS * HD], F32R)
        wv1_lo = sb("wv1_lo", [P, HEADS * HD], F32R)
        p_hi, p_lo = q_all2[0:KT, 1, :], q_shift2[0:KT, 1, :]
        rows_hi, rows_lo = (w[0:KT, 0:CH * P].rearrange("p (j c) -> p j c", j=CH)[:, :, 0:CD + 1] for w in (wv1_hi, wv1_lo))
        sum_mem = sb("sum_mem", [KT, TOK + HALF])
        v_stage = sum_mem[:, :].rearrange("p (j f) -> p j f", j=CH)
        wq1 = sb("wq1", [P, P])
        wk1 = sb("wk1", [CD, P])
        wo1 = sb("wo1", [P, HEADS, D])
        wo_slot = sb("wo_slot", [P, D])
        bo1 = sb("bo1", [P, D])
        psum_pool = sum_mem[:, 0:TOK]
        psum_dve = sum_mem[:, TOK:TOK + HALF]
        acc_raw = sb("acc_raw", [P, HALF])
        rden = sb("rden", [P, TT])
        diag = sb("diag", [HD + TT, TT])

        in_x, in_a, in_wv, in_f0, in_c, in_f1 = (sem(f"in_{n}") for n in ("x", "a", "wv", "f0", "c", "f1"))
        in_ctx = sems("in_ctx", CH)
        consts, neg_ready = sem("consts"), sem("neg_ready")
        ln_stats, ln_var, ln_std, ln_rstd, ln_out = (sem(f"ln_{n}") for n in ("stats", "var", "std", "rstd", "out"))
        tr_psum, tr_act, tr_dve = sem("tr_psum"), sem("tr_act"), sem("tr_dve")
        max_scored, max_reduced = sems("max_scored", TT), sems("max_reduced", TT)
        slot_keys, attended = sems("slot_keys", CH), sems("attended", CH)
        scored, exped = sems("scored", 2 * CH), sems("exped", 2 * CH)
        max_found, max_row, shifted = sem("max_found"), sem("max_row"), sem("shifted")
        a_q, a_qsb, a_qhi, a_qlo, a_rows, a_chi, a_clo, a_wvs, a_qcopy, a_acczero, a_o, a_out, a_rsum, a_x = (
            sem(f"a_{n}") for n in ("q", "qsb", "qhi", "qlo", "rows", "chi", "clo", "wvs", "qcopy", "acczero",
                                    "o", "out", "rsum", "x"))
        a_plo0, a_av0 = sems("a_plo0", CH), sems("a_av0", CH)
        a_vkeys = sems("a_vkeys", CH)
        a_cslot, a_vproj, a_vevac, a_vout = (sems(f"a_{n}", CH) for n in ("cslot", "vproj", "vevac", "vout"))
        f_pe, f_step, f_mask, f_w, f_biassb, f_gelu, f_masktsb, f_masked, f_x = (
            sem(f"f_{n}") for n in ("pe", "step", "mask", "w", "biassb", "gelu", "masktsb", "masked", "x"))
        PE_BIAS, PE_LOGITS, PE_HIDDEN, PE_MASK, PE_SPREAD, PE_OUT = 1, 2, (3, 4, 6, 7), 5, 8, 12
        c_rows, c_wq, c_wk, c_vload, c_qproj, c_qhi, c_qlo, c_qcopy, c_kp, c_khi, c_klo = (
            sem(f"c_{n}") for n in ("rows", "wq", "wk", "vload", "qproj", "qhi", "qlo", "qcopy", "kp", "khi", "klo"))
        c_dadd, c_total, c_acc, c_acczero, c_sums, c_rden, c_wo, c_out, c_x = (
            sem(f"c_{n}") for n in ("dadd", "total", "acc", "acczero", "sums", "rden", "wo", "out", "x"))
        c_kfull = sem("c_kfull")
        c_dadd1 = sem("c_dadd1")
        c_vslot, c_padd = sems("c_vslot", CH), sems("c_padd", CH)
        g_step, g_logits, g_exp, g_cw, g_cwt, g_cwtsb, g_spread_ready, g_store = (
            sem(f"g_{n}") for n in ("step", "logits", "exp", "cw", "cwt", "cwtsb", "spread_ready", "store"))
        g_xs, g_whi, g_wlo = sem("g_xs"), sem("g_whi"), sem("g_wlo")
        g_w13 = sems("g_w13", 2)
        g_w, g_u, g_silu, g_h, g_gate, g_hg, g_y, g_fin = (
            sems(f"g_{n}", 2) for n in ("w", "u", "silu", "h", "gate", "hg", "y", "fin"))

        f0w = sb("f0w", [P, 3 * 256 + 8 * 3 + 2 + 2 + 8 * 8])
        w1_in = f0w[:, 0:256]
        w1s = f0w[:, 256:512]
        w1b = f0w[:, 512:768]
        sc0 = f0w[:, 768:776]
        bi0 = f0w[:, 776:784]
        wgt = f0w[:, 784:792]
        b1_0 = f0w[:, 792:794]
        hb0 = f0w[:, 794:796]
        lg0 = f0w[:, 796:860]
        w2_0 = sb("w2_0", [P, G0, D])
        b2_0 = sb("b2_0", [E0, D])
        spread0 = sb("spread0", [E0, G0, P])
        mask0 = sb("mask0", [P, TT, E0])
        top8 = sb("top8", [P, TT, 8])
        idx8 = sb("idx8", [P, TT, 8], U32)
        idxf8 = sb("idxf8", [P, TT, 8])
        mask_t = v_mem[0:E0, 5 * TOK:6 * TOK]
        hid0 = v_mem[:, 3 * TOK:5 * TOK].rearrange("p (g t) -> p g t", g=G0)

        gw = sb("gw", [P, E1])
        gb = sb("gb", [P, E1])
        b2_1 = sb("b2_1", [E1, D])
        sb2 = sb("sb2", [P, 1])
        spread1 = sb("spread1", [3 * E1, G1, P], BF16)
        used = [0]

        def over_ctx(*shape):
            n, at = 1, used[0]
            for m in shape:
                n *= m
            used[0] += n
            flat = ctx_mem[:, at:at + n]
            return flat.rearrange("p (a b) -> p a b", a=shape[0]) if len(shape) == 2 else flat

        gl, gp, cw = over_ctx(TT, E1), over_ctx(TT, E1), over_ctx(TT, E1)
        gm, gs = over_ctx(TT), over_ctx(TT)
        pmax, pmin, qmax, qmin, keep = (over_ctx(TT, GROUPS) for _ in range(5))
        cw_t, cw_r = over_ctx(TOK)[0:E1, :], over_ctx(TOK)[0:E1, :]
        x3_t, ranks = over_ctx(TOK), over_ctx(TT * TOPK * E1)
        cw_b = sb("cw_b", [E1, TOK], BF16)
        cw_3 = sb("cw_3", [3 * E1, TOK], BF16)
        pair_w = sb("pair_w", [P, 2, PAIR_W])
        silu = sb("silu", [P, 2, HALF])
        parts = keys_hl[:, :, :, :].rearrange("p n a k -> p (n a k)")
        x_hi, x_lo = parts[:, 0:TOK], parts[:, TOK:2 * TOK]
        w_parts = parts[:, 2 * TOK:2 * TOK + 8 * P].rearrange("p (s a c) -> p s a c", s=2, a=2)
        hgate = sb("hgate", [P, 2, HALF])
        block = ctx.enter_context(nc.Block())

        crow_v = ctx_rows.rearrange("(n p) c -> n p c", p=KT)
        v_dram_v = v_dram.rearrange("n p (h d) -> h p n d", h=HEADS)

        def f32(ap):
            return ap.bitcast(F32)

        def halves(ap):
            return ap.rearrange("p (a b) -> p a b", a=2)

        def cols(half):
            return slice(half * HALF, (half + 1) * HALF)

        def context_lo(eng, q):
            part = slice(q * CHUNKS, (q + 1) * CHUNKS)
            eng.wait_ge(a_chi, q + 1)
            eng.tensor_tensor(keys_hl[0:CD, part, 1, :], ctx_f.rearrange("p (n k) -> p n k", k=KT)[:, part, :],
                              f32(keys_hl[0:CD, part, 0, :]), ALU.subtract).then_inc(a_clo, 1)

        def flat(ap):
            return ap.rearrange("p a b -> p (a b)")

        def tile_cols(t):
            return slice(t * P, (t + 1) * P)

        @block.sync
        def _(sp):
            sp.dma_start(x_tok[:, :, :], x.rearrange("(t p) d -> p t d", p=P)).then_inc(in_x, 16)
            sp.dma_start(ident[:, :], ident_in).then_inc(in_x, 16)
            for dst, src in ((wq0[:, :], a_wq), (bq0[:, :], a_bq), (wkt0[:, 0:CD], a_wkt), (wkt0[:, CD:CD + 1], a_bk),
                             (wv0[0:CD, 0:D], a_wv), (wv0[CD:CD + 1, 0:D], a_bv)):
                sp.dma_start(dst, src).then_inc(in_a, 16)
            for q in range(CH):
                part = slice(q * CHUNKS * KT, (q + 1) * CHUNKS * KT)
                sp.dma_start(ctx_f[:, part], ctx_t[:, part]).then_inc(in_ctx[q], 16)
            sp.dma_start(wv1_f, c_wv_in).then_inc(in_wv, 16)
            for dst, src in ((w1_in, f0_w1), (sc0, f0_scale), (bi0, f0_bias), (wgt, f0_wgt), (b1_0, f0_b1),
                             (w2_0[:, :, :], f0_w2), (b2_0[:, :], f0_b2), (spread0[:, :, :], spread0_in),
                             (iota[:, :], iota_in)):
                sp.dma_start(dst, src).then_inc(in_f0, 16)
            for dst, src in ((wo1[:, :, :], c_wo_in), (bo1[:, :], c_bo_in),
                             (wq1[:, :], c_wq_in[0]), (wk1[:, :], c_wk_in[0]),
                             (diag[HD:HD + TT, :], ident_in[0:TT, 0:TT])):
                sp.dma_start(dst, src).then_inc(in_c, 16)
            for dst, src in ((gw[:, :], f1_gw), (gb[:, :], f1_gb), (b2_1[:, :], f1_b2),
                             (sb2[:, :], f1_sb2), (spread1[:, :, :], spread1_in)):
                sp.dma_start(dst, src).then_inc(in_f1, 16)
            for s in range(2):
                sp.dma_start(pair_w[:, s, 0:2 * P], f1_pairs[s][:, 0:2 * P]).then_inc(g_w13[s], 16)
                sp.dma_start(pair_w[:, s, 2 * P:PAIR_W], f1_pairs[s][:, 2 * P:PAIR_W]).then_inc(g_w[s], 16)
            for j in range(CH):
                sp.dma_start(vslot[:, j, 0:CD], crow_v[j]).then_inc(a_cslot[j], 16)

            with sp.Fori(0, CHUNKS) as g:
                k1 = sp.snap(g + 1)
                for j in range(CH):
                    sp.wait_ge(a_vevac[j], k1)
                    sp.dma_start(v_dram[bass.ds(g * CH + j, 1)].rearrange("a p c -> p (a c)"),
                                 v_stage[:, j, :]).then_inc(a_vout[j], 16)
            with sp.Fori(0, CHUNKS - 1) as g:
                k1 = sp.snap(g + 1)
                for j in range(CH):
                    sp.wait_ge(c_vslot[j], k1)
                    sp.dma_start(vslot[:, j, 0:CD],
                                 crow_v[bass.ds(g * CH + CH + j, 1)].rearrange("a p c -> p (a c)")).then_inc(a_cslot[j], 16)
            for j in range(CH):
                sp.wait_ge(a_vout[j], 16 * CHUNKS)
            sp.wait_ge(f_x, 1)
            sp.dma_start(v_tiles[:, 0], v_dram_v[0]).then_inc(c_vload, 16)
            sp.wait_ge(c_qproj, 1)
            sp.dma_start(wq1[:, :], c_wq_in[1]).then_inc(c_wq, 16)
            sp.wait_ge(c_kp, CHUNKS)
            sp.dma_start(wk1[:, :], c_wk_in[1]).then_inc(c_wk, 16)

            def load_v(h):
                sp.wait_ge(c_vslot[CH - 1], (h + 1) * CHUNKS + 1)
                sp.dma_start(v_tiles[:, bass.ds((h + 1) % 2, 1)].rearrange("p b n d -> p (b n) d"),
                             v_dram_v[bass.ds(h + 1, 1)].rearrange("h p n d -> (h p) n d")).then_inc(c_vload, 16)

            with sp.Fori(0, HEADS - 2) as h:
                load_v(h)
                sp.wait_ge(c_qproj, h + 2)
                sp.dma_start(wq1[:, :], c_wq_in[bass.ds(h + 2, 1)].rearrange("a p c -> p (a c)")).then_inc(c_wq, 16)
                sp.wait_ge(c_kp, (h + 2) * CHUNKS)
                sp.dma_start(wk1[:, :], c_wk_in[bass.ds(h + 2, 1)].rearrange("a p c -> p (a c)")).then_inc(c_wk, 16)
            load_v(HEADS - 2)
            def load_up(m, split, s):
                sp.wait_ge(g_wlo, split)
                sp.dma_start(pair_w[:, s, 0:2 * P],
                             f1_pairs[bass.ds(m, 1), :, 0:2 * P].rearrange("a p c -> p (a c)")).then_inc(g_w13[s], 16)

            def load_down(m, used, s):
                for half in range(2):
                    sp.wait_ge(g_y[half], used)
                sp.dma_start(pair_w[:, s, 2 * P:PAIR_W],
                             f1_pairs[bass.ds(m, 1), :, 2 * P:PAIR_W].rearrange("a p c -> p (a c)")).then_inc(g_w[s], 16)

            for s in range(2):
                load_up(2 + s, 1 + s, s)
            with sp.Fori(0, G1 // 2 - 2) as i:
                for s in range(2):
                    load_down(2 * i + 2 + s, 2 * i + 1 + s, s)
                    load_up(2 * i + 4 + s, 2 * i + 3 + s, s)
            load_down(G1 - 2, G1 - 3, 0)
            load_up(G1, G1 - 1, 0)
            load_down(G1 - 1, G1 - 2, 1)
            load_down(G1, G1 - 1, 0)
            for half in range(2):
                sp.wait_ge(g_fin[half], 1)
                sp.dma_start(out_t[:, cols(half)], x3_t[:, cols(half)]).then_inc(g_store, 16)
            sp.wait_ge(g_store, 32)

        @block.gpsimd
        def _(pool):
            pool.memset(ones[:, :], 1.0).then_inc(consts, 1)
            pool.wait_ge(consts, 1)
            pool.memset(eps_col[:, :], EPS).then_inc(consts, 1)
            pool.wait_ge(consts, 2)
            pool.memset(zero_col[:, :], 0.0).then_inc(consts, 1)
            pool.wait_ge(consts, 3)
            pool.memset(vslot[:, :, CD:CD + 1], 1.0).then_inc(a_rows, 1)
            pool.wait_ge(a_rows, 1)
            pool.memset(f32(q_pad[CD:CD + 1, :]), PAD_SCORE).then_inc(a_rows, 1)
            pool.wait_ge(a_rows, 2)
            pool.memset(wv0[:, D:D + 1], 0.0).then_inc(a_rows, 1)
            pool.wait_ge(a_rows, 3)
            pool.memset(wv0[CD:CD + 1, D:D + 1], 1.0).then_inc(a_rows, 1)
            pool.wait_ge(a_rows, 4)
            pool.memset(f32(keys_hl[CD:CD + 1, :, 0, :]), 1.0).then_inc(a_rows, 1)
            pool.wait_ge(a_rows, 5)
            pool.memset(f32(keys_hl[CD:P, :, 1, :]), 0.0).then_inc(a_rows, 1)
            pool.wait_ge(a_rows, 6)
            pool.memset(f32(keys_hl[CD:CD + 1, TILES - 1, 1, PAD_AT:KT]), 1.0).then_inc(a_rows, 1)
            pool.wait_ge(a_rows, 7)
            context_lo(pool, 2)
            pool.wait_ge(a_clo, CH)
            pool.wait_ge(a_qhi, 1)
            pool.tensor_copy(q_shift[0:CD, :], f32(q_max[0:CD, :])).then_inc(a_qcopy, 1)
            pool.wait_ge(a_qcopy, 1)
            pool.tensor_copy(q_pad[0:CD, :], f32(q_max[0:CD, :])).then_inc(a_qcopy, 1)
            pool.wait_ge(a_qcopy, 2)
            with pool.Fori(0, CHUNKS) as g:
                vkeys = pool.snap(g + (CHUNKS + 1))
                k1 = pool.snap(g + 1)
                for j in range(CH):
                    pool.wait_ge(a_vkeys[j], vkeys)
                    pool.wait_ge(c_vslot[(j - 1) % CH], k1 if j else g)
                    pool.tensor_tensor(rows_lo[:, j, :], vslot[:, j, 0:CD + 1], f32(rows_hi[:, j, :]),
                                       ALU.subtract).then_inc(c_vslot[j], 1)
            pool.wait_ge(c_vslot[CH - 1], CHUNKS)
            pool.wait_ge(slot_keys[CH - 1], CHUNKS)
            pool.memset(f32(keys_hl[HD:CD, :, 1, :]), 0.0).then_inc(c_rows, 1)
            pool.wait_ge(c_rows, 1)
            pool.memset(f32(keys_hl[HD:HD + TT, :, 1, :]), 1.0).then_inc(c_rows, 1)
            pool.wait_ge(c_rows, 2)
            pool.wait_ge(attended[CH - 1], CHUNKS)
            pool.memset(f32(q_shift2[HD:CD, :, :]), 0.0).then_inc(c_rows, 1)
            pool.wait_ge(c_rows, 3)
            pool.memset(f32(q_shift2[CD:CD + 1, :, :]), PAD_SCORE).then_inc(c_rows, 1)
            pool.wait_ge(c_rows, 4)

            with pool.Fori(0, CHUNKS) as g:
                pool.wait_ge(c_kfull, g + 1)
                pool.tensor_tensor(keys_hl[0:HD, bass.ds(g * CH, CH), 1, :], k_full,
                                   f32(keys_hl[0:HD, bass.ds(g * CH, CH), 0, :]), ALU.subtract).then_inc(c_klo, 1)

            def add(j, width, last_add, both1, first=False):
                pool.wait_ge(exped[2 * j], both1)
                if width == TOK:
                    pool.wait_ge(exped[2 * j + 1], both1)
                pool.wait_ge(c_padd[(j - 1) % CH], last_add)
                other = zero_col[0:KT, :].to_broadcast([KT, TOK]) if first else psum_pool[:, 0:width]
                pool.tensor_tensor(psum_pool[:, 0:width], other, probs[:, j, 0:width], ALU.add).then_inc(c_padd[j], 1)

            def add_chunk(k, h=None, last_head=False):
                both = pool.snap(k + CHUNKS)
                both1 = pool.snap(k + (CHUNKS + 1))
                if h is not None:
                    pool.wait_ge(c_sums, h)
                add(0, TOK, both, both1, first=h is not None)
                add(1, HALF if last_head else TOK, both1, both1)
                add(2, HALF, both1, both1)

            pool.wait_ge(consts, 3)
            for j in range(CH):
                pool.wait_ge(a_vout[j], 16 * CHUNKS)

            def sum_head(h, last_head):
                k0 = pool.snap(h * CHUNKS)
                add_chunk(k0, h, last_head)
                with pool.Fori(1, CHUNKS) as g:
                    add_chunk(pool.snap(k0 + g), last_head=last_head)
                pool.wait_ge(c_padd[CH - 1], h * CHUNKS + 2 * CHUNKS)
                pool.wait_ge(c_dadd, h * CHUNKS + CHUNKS)
                pool.tensor_tensor(psum_pool[:, HALF:TOK], psum_pool[:, HALF:TOK], psum_dve, ALU.add).then_inc(c_total, 1)

            with pool.Fori(0, HEADS - 1) as h:
                sum_head(h, False)
            sum_head(HEADS - 1, True)

            def w_lo(m1, s):
                pool.wait_ge(g_whi, m1)
                pool.tensor_tensor(w_parts[:, s, 1, :], pair_w[:, s, 0:2 * P], f32(w_parts[:, s, 0, :]),
                                   ALU.subtract).then_inc(g_wlo, 1)

            pool.wait_ge(g_xs, 1)
            pool.tensor_tensor(x_lo, xn_t[:, :], f32(x_hi), ALU.subtract).then_inc(g_xs, 1)
            with pool.Fori(0, G1 // 2) as i:
                for s in range(2):
                    w_lo(2 * i + 1 + s, s)
            w_lo(G1 + 1, 0)

        @block.scalar
        def _(act):
            def std_of(n):
                if n == 0:
                    act.wait_ge(consts, 3)
                act.wait_ge(ln_var, n + 1)
                act.activation(std[:, :], mean_var[:, :, 1], ACT.Sqrt, bias=eps_col[:, :]).then_inc(ln_std, 1)

            def turned(n, dst):
                act.wait_ge(tr_psum, 2 * n + 1)
                act.copy(dst[:, 0:HALF], ps[:, 6, :]).then_inc(tr_act, 1)

            std_of(0)
            for q in range(CH):
                part = slice(q * CHUNKS, (q + 1) * CHUNKS)
                act.wait_ge(in_ctx[q], 16)
                act.copy(keys_hl[0:CD, part, 0, :],
                         ctx_f.rearrange("p (n k) -> p n k", k=KT)[:, part, :]).then_inc(a_chi, 1)
                if q == 0:
                    turned(0, xn_t)
            act.wait_ge(in_wv, 16)
            act.copy(wv1_hi[0:CD, :], wv1_f).then_inc(a_wvs, 1)
            act.wait_ge(a_q, 4)
            act.copy(halves(q_max[0:CD + 1, :]), ps[0:CD + 1, 0:2, :]).then_inc(a_qhi, 1)

            def v_keys(n, j):
                act.copy(kslot[0:CD, j, :, :].rearrange("p a k -> p (a k)"),
                         f32(keys_hl[0:CD, bass.ds(n, 1), :, :]).rearrange("p n a k -> p (n a k)")
                         ).then_inc(a_vkeys[j], 1)

            def v_evac(j, k1, sixteen_k):
                act.wait_ge(a_vproj[j], k1)
                act.wait_ge(a_vout[j], sixteen_k)
                act.copy(v_stage[:, j, :], ps[0:KT, 4 + j, :]).then_inc(a_vevac[j], 1)

            act.wait_ge(a_clo, CH)
            for j in range(CH):
                v_keys(j, j)
            with act.Fori(0, CHUNKS - 1) as g:
                k1 = act.snap(g + 1)
                k16 = act.snap(g * 16)
                n1 = act.snap(g * CH + CH)
                for j in range(CH):
                    act.wait_ge(a_vproj[j], k1)
                    v_keys(n1 + j, j)
                    v_evac(j, k1, k16)
            for j in range(CH):
                v_evac(j, CHUNKS, 16 * (CHUNKS - 1))

            def exp0(jj, kv, kp):
                act.wait_ge(c_padd[jj], kp)
                act.wait_ge(a_plo0[jj], kp)
                for half in range(2):
                    u = 2 * jj + half
                    act.wait_ge(scored[u], kv)
                    act.activation(probs[:, jj, cols(half)], ps[0:KT, u, :], ACT.Exp, scale=float(D) ** -0.5)

            def exp0_hi(jj, kv, kp):
                for half in range(2):
                    u = 2 * jj + half
                    act.wait_ge((a_av0, attended)[half][(jj - 1) % CH], kv if jj else kp)
                    act.activation(p_hi[:, cols(half)], ps[0:KT, u, :], ACT.Exp,
                                   scale=float(D) ** -0.5).then_inc(exped[u], 1)

            def exp_tiles(k, k1, k2):
                exp0(1, k1, k)
                exp0_hi(0, k1, k)
                exp0(2, k1, k)
                exp0_hi(1, k1, k)
                if k2 is not None:
                    exp0(0, k2, k1)
                exp0_hi(2, k1, k)

            exp0(0, 1, 0)
            with act.Fori(0, CHUNKS - 1) as g:
                exp_tiles(g, act.snap(g + 1), act.snap(g + 2))
            exp_tiles(CHUNKS - 1, CHUNKS, None)
            act.wait_ge(attended[CH - 1], CHUNKS)
            act.copy(o0[:, 0:HALF], ps[0:CD + 1, 6, :]).then_inc(a_o, 1)

            std_of(1)
            turned(1, xn_t)
            std_of(2)
            turned(2, xn_t)
            act.wait_ge(f_biassb, 1)
            for n in range(2 * G0):
                g, half = n // 2, n % 2
                act.wait_ge(f_pe, PE_HIDDEN[n])
                act.activation(hid0[:, g, cols(half)], ps[:, 2 + n, :], ACT.Gelu, bias=hb0[:, g:g + 1]).then_inc(f_gelu, 1)
                if n == 0:
                    act.wait_ge(f_pe, PE_MASK)
                    act.copy(halves(mask_t), ps[0:E0, 0:2, :]).then_inc(f_masktsb, 1)

            std_of(3)
            turned(3, xn_t)

            def q_hi(n):
                act.wait_ge(c_qproj, n + 1)
                act.wait_ge(c_qcopy, 2 * n)
                act.copy(halves(q_max[:, :]), ps[:, B_KP:B_AUX + 1, :]).then_inc(c_qhi, 1)

            def q_moving(n, part):
                slot = act.snap(n % 2) if not isinstance(n, int) else n % 2
                if part == 0:
                    act.wait_ge(c_qhi, n + 1)
                    dst, src = q_shift2[0:HD, bass.ds(slot, 1), :], q_max[0:HD, :]
                else:
                    act.wait_ge(c_qlo, n + 1)
                    dst, src = q_all2[:, bass.ds(slot, 1), :], q_max[:, :]
                act.copy(dst.rearrange("p a t -> p (a t)"), f32(src)).then_inc(c_qcopy, 1)

            def k_hi(g, kn, slots_read):
                act.wait_ge(c_kp, kn)
                if slots_read is not None:
                    act.wait_ge(slot_keys[CH - 1], slots_read)
                act.copy(keys_hl[:, bass.ds(g * CH, CH), 0, :],
                         ps[:, B_KP, 0:CK].rearrange("p (n k) -> p n k", k=KT)).then_inc(c_khi, 1)

            def tile1(parity, at, jj, both1, both, k, extra=None):
                act.wait_ge(attended[jj], both)
                act.copy(vslot[:, jj, 0:HD],
                         v_head[:, bass.ds(parity, 1), bass.ds(at, HD)].rearrange("p a d -> p (a d)")).then_inc(c_vslot[jj], 1)
                act.wait_ge(c_padd[jj], both)
                if jj == CH - 1:
                    act.wait_ge(c_dadd, k)
                if extra is not None:
                    act.wait_ge(c_dadd1, extra)
                for half in range(2):
                    u = 2 * jj + half
                    act.wait_ge(scored[u], both1)
                    act.activation(probs[:, jj, cols(half)], ps[0:KT, u % 3, :], ACT.Exp,
                                   scale=float(HD) ** -0.5).then_inc(exped[u], 1)

            def step(parity, g, k, nxt, last=False, q_of=None):
                both = act.snap(k + CHUNKS)
                both1 = act.snap(k + (CHUNKS + 1))
                at = act.snap(g * (CH * HD)) if not isinstance(g, int) else g * CH * HD
                if nxt and q_of is None:
                    k_hi(g, both1, both1)
                tile1(parity, at + HD, 1, both1, both, k, None if nxt else g)
                if nxt and q_of is not None:
                    k_hi(g, both1, both1)
                if q_of is not None:
                    q_moving(q_of, 0)
                tile1(parity, at + 2 * HD, 2, both1, both, k)
                if q_of is not None:
                    q_moving(q_of, 1)
                if not last:
                    tile1(parity, at + 3 * HD, 0, act.snap(k + (CHUNKS + 2)), both1, act.snap(k + 1))

            def acc_out(h):
                act.wait_ge(attended[CH - 1], (h + 1) * CHUNKS)
                act.wait_ge(c_out, 2 * h - 2)
                act.copy(acc_raw[:, :], ps[:, B_ACC, :]).then_inc(c_acc, 1)

            def head(h, prev, nxt):
                if nxt:
                    q_hi(h + 1)
                if prev:
                    acc_out(h)
                act.wait_ge(c_vload, 16 * h + 16)
                parity = act.snap(h % 2)
                k0 = act.snap(h * CHUNKS)
                tile1(parity, 0, 0, act.snap(k0 + (CHUNKS + 1)), act.snap(k0 + CHUNKS), k0)
                step(parity, 0, k0, nxt, q_of=h + 1 if nxt else None)
                with act.Fori(0, TURNS) as n:
                    for u in range(UNROLL):
                        g = act.snap(n * UNROLL + (u + 1))
                        step(parity, g, act.snap(k0 + g), nxt)
                step(parity, CHUNKS - 1, act.snap(k0 + (CHUNKS - 1)), nxt, last=True)

            q_hi(0)
            with act.Fori(0, CHUNKS) as g:
                k_hi(g, act.snap(g + 1), None)
                act.wait_ge(c_klo, g)
                act.copy(k_full, ps[0:HD, B_KP, 0:CK].rearrange("p (n k) -> p n k", k=KT)).then_inc(c_kfull, 1)
            q_moving(0, 0)
            q_moving(0, 1)
            head(0, False, True)
            with act.Fori(1, HEADS - 1) as h:
                head(h, True, True)
            head(HEADS - 1, True, False)
            acc_out(HEADS)

            std_of(4)
            turned(4, xn_t)

            def w_hi(s, loads, last_up):
                act.wait_ge(g_w13[s], loads)
                if last_up is not None:
                    act.wait_ge(g_u[1], last_up)
                act.copy(w_parts[:, s, 0, :], pair_w[:, s, 0:2 * P]).then_inc(g_whi, 1)

            act.wait_ge(tr_act, 5)
            act.wait_ge(tr_dve, 5)
            act.copy(x_hi, xn_t[:, :]).then_inc(g_xs, 1)
            for s in range(2):
                w_hi(s, 16, None)
            act.wait_ge(g_exp, 1)
            act.activation(gp, gp, ACT.Exp).then_inc(g_exp, 1)
            turned(5, x3_t)
            def act_item(m, s, half, m1, loads):
                if half == 0:
                    act.wait_ge(g_w[s], loads)
                act.wait_ge(g_u[half], m1)
                if not (isinstance(m, int) and m == 0):
                    act.wait_ge(g_h[half], m)
                act.activation(silu[:, half, :], ps[:, half, :], ACT.Silu,
                               bias=pair_w[:, s, 3 * P:3 * P + 1]).then_inc(g_silu[half], 1)

            for half in range(2):
                act_item(0, 0, half, 1, 16)
            w_hi(0, 32, 1)
            act.wait_ge(g_cwt, 1)
            act.copy(halves(cw_t), ps[0:E1, 4:6, :]).then_inc(g_cwtsb, 1)

            def act_pairs(i, last):
                m = [act.snap(2 * i + n) for n in (1, 2, 3)]
                loads = [act.snap(16 * i + n) for n in (16, 32, 48)]
                for n in range(2):
                    for half in range(2):
                        act_item(m[n], 1 - n, half, m[n + 1], loads[n])
                    if not last:
                        w_hi(1 - n, loads[n + 1], m[n + 1])

            with act.Fori(0, G1 // 2 - 1) as i:
                act_pairs(i, False)
            act_pairs(G1 // 2 - 1, True)

        @block.vector
        def _(dve):
            def layernorm(n, src, dst):
                for t in range(TT):
                    ins = dve.bn_stats(stats[:, t, :], src[:, t, :])
                ins.then_inc(ln_stats, 1)
                dve.wait_ge(ln_stats, n + 1)
                for t in range(TT):
                    ins = dve.bn_aggr(mean_var[:, t, :], stats[:, t, :])
                ins.then_inc(ln_var, 1)
                dve.wait_ge(ln_std, n + 1)
                dve.reciprocal(rstd[:, :], std[:, :]).then_inc(ln_rstd, 1)
                dve.wait_ge(ln_rstd, n + 1)
                for t in range(TT):
                    dve.tensor_scalar(dst[:, t, :], src[:, t, :], mean_var[:, t, 0:1], rstd[:, t:t + 1],
                                      ALU.subtract, ALU.mult).then_inc(ln_out, 1)

            def turned(n, dst):
                dve.wait_ge(tr_psum, 2 * n + 2)
                dve.tensor_copy(dst[:, HALF:TOK], ps[:, 7, :]).then_inc(tr_dve, 1)

            dve.wait_ge(in_x, 32)
            dve.tensor_scalar(neg_ident[:, :], ident[:, :], -1.0, None, ALU.mult).then_inc(neg_ready, 1)
            layernorm(0, x_tok, xn)
            turned(0, xn_t)
            context_lo(dve, 0)
            dve.wait_ge(in_a, 16 * 6)
            dve.wait_ge(a_q, 2)
            dve.tensor_scalar(halves(q0_t), ps[:, 3:5, :], bq0[:, :], None, ALU.add).then_inc(a_qsb, 1)
            context_lo(dve, 1)
            dve.wait_ge(a_qhi, 1)
            dve.tensor_tensor(halves(q_all[0:CD, :]), ps[0:CD, 0:2, :], halves(f32(q_max[0:CD, :])),
                              ALU.subtract).then_inc(a_qlo, 1)
            dve.wait_ge(a_wvs, 1)
            dve.tensor_tensor(wv1_lo[0:CD, :], wv1_f, f32(wv1_hi[0:CD, :]), ALU.subtract).then_inc(a_wvs, 1)
            with dve.Fori(0, CHUNKS) as g:
                k1 = dve.snap(g + 1)
                for i in range(TT):
                    dve.wait_ge(max_scored[i], k1)
                    dve.tensor_reduce(chunk_max[:, i, bass.ds(g, 1)], ps[:, i % 4, 0:CK], AX,
                                      ALU.max).then_inc(max_reduced[i], 1)
            dve.wait_ge(max_reduced[TT - 1], CHUNKS)
            dve.tensor_reduce(row_max[:, :], chunk_max[:, :, :], AX, ALU.max).then_inc(max_found, 1)

            def fill0(n, j):
                dve.tensor_copy(kslot[0:CD + 1, j, :, :].rearrange("p a k -> p (a k)"),
                                f32(keys_hl[0:CD + 1, bass.ds(n, 1), :, :]).rearrange("p n a k -> p (n a k)")
                                ).then_inc(slot_keys[j], 1)

            dve.wait_ge(a_rows, 7)
            for j in range(CH):
                dve.wait_ge(a_vproj[j], CHUNKS)
                fill0(j, j)
            dve.wait_ge(tr_act, 1)
            dve.wait_ge(tr_dve, 1)
            dve.wait_ge(a_vevac[CH - 1], CHUNKS)
            dve.memset(ps[:, 6:8, :], 0.0).then_inc(a_acczero, 1)
            dve.wait_ge(max_row, 1)
            dve.tensor_tensor(halves(q_shift[CD:CD + 1, :]), ps[CD:CD + 1, 3:5, :], halves(f32(q_max[CD:CD + 1, :])),
                              ALU.add).then_inc(shifted, 1)

            def context_rows_hi(j, k, k16):
                dve.wait_ge(a_cslot[j], k16)
                dve.wait_ge(attended[j], k)
                dve.tensor_copy(rows_hi[:, j, :], vslot[:, j, 0:CD + 1]).then_inc(a_vkeys[j], 1)

            def probs_lo(j, k1):
                for half in range(2):
                    dve.wait_ge(exped[2 * j + half], k1)
                    dve.tensor_tensor(p_lo[:, cols(half)], probs[:, j, cols(half)], f32(p_hi[:, cols(half)]),
                                      ALU.subtract).then_inc((a_plo0, c_padd)[half][j], 1)

            with dve.Fori(0, CHUNKS - 1) as g:
                k1 = dve.snap(g + 1)
                n1 = dve.snap(g * CH + CH)
                k16 = dve.snap(g * 16 + 16)
                for j in range(CH):
                    context_rows_hi(j, g, k16)
                    probs_lo(j, k1)
                    dve.wait_ge(scored[2 * j + 1], k1)
                    fill0(n1 + j, j)
            for j in range(CH):
                context_rows_hi(j, CHUNKS - 1, 16 * CHUNKS)
                probs_lo(j, CHUNKS)
            dve.wait_ge(attended[CH - 1], CHUNKS)
            dve.tensor_copy(o0[:, HALF:TOK], ps[0:CD + 1, 7, :]).then_inc(a_o, 1)
            dve.wait_ge(in_f0, 16 * 9)
            w1_e = w1_in.rearrange("p (e j) -> p e j", e=E0)
            dve.tensor_tensor(w1s.rearrange("p (e j) -> p e j", e=E0), w1_e,
                              sc0.unsqueeze(2).to_broadcast([P, E0, H0]), ALU.mult).then_inc(f_w, 1)
            dve.tensor_tensor(w1b.rearrange("p (e j) -> p e j", e=E0), w1_e,
                              bi0.unsqueeze(2).to_broadcast([P, E0, H0]), ALU.mult).then_inc(f_w, 1)
            dve.wait_ge(a_out, 1)
            out_tiles = ps[:, 0:4, :].rearrange("p b (u c) -> p b u c", u=2)
            dve.reciprocal(rsum0[:, :, :], out_tiles[:, :, :, D]).then_inc(a_rsum, 1)
            dve.wait_ge(a_rsum, 1)
            for t in range(TT):
                b, u = t % 4, t // 4
                ins = dve.scalar_tensor_tensor(out=x_tok[:, t, :], in0=out_tiles[:, b, u, 0:D],
                                               scalar=rsum0[:, b, u:u + 1], in1=x_tok[:, t, :],
                                               op0=ALU.mult, op1=ALU.add)
            ins.then_inc(a_x, 1)

            dve.wait_ge(f_pe, PE_BIAS)
            dve.tensor_tensor(hb0, ps[:, 5, 0:G0], b1_0, ALU.add).then_inc(f_biassb, 1)
            dve.wait_ge(a_x, 1)
            layernorm(1, x_tok, xn)
            turned(1, xn_t)
            dve.wait_ge(ln_out, 2 * TT)
            layernorm(2, xn, xn2)
            dve.wait_ge(f_pe, PE_LOGITS)
            dve.tensor_copy(lg0, ps[:, 4, 0:TT * E0]).then_inc(f_step, 1)
            turned(2, xn_t)
            dve.wait_ge(f_step, 1)
            for t in range(TT):
                ins = dve.max(top8[:, t, :], lg0[:, t * E0:(t + 1) * E0])
            ins.then_inc(f_step, 1)
            dve.wait_ge(f_step, 2)
            for t in range(TT):
                ins = dve.max_index(idx8[:, t, :], top8[:, t, :], lg0[:, t * E0:(t + 1) * E0])
            ins.then_inc(f_step, 1)
            dve.wait_ge(f_step, 3)
            dve.tensor_copy(idxf8[:, :, :], idx8[:, :, :]).then_inc(f_step, 1)
            dve.wait_ge(f_step, 4)
            for t in range(TT):
                ins = dve.tensor_scalar(mask0[:, t, :], iota[:, 0:E0], idxf8[:, t, 0:1], None, ALU.is_equal)
            ins.then_inc(f_mask, 1)
            for n in range(2 * G0):
                g, half = n // 2, n % 2
                dve.wait_ge(f_gelu, n + 1)
                dve.wait_ge(f_pe, PE_SPREAD + n)
                dve.tensor_tensor(hid0[:, g, cols(half)], ps[:, (6 + n) % 8, :], hid0[:, g, cols(half)],
                                  ALU.mult).then_inc(f_masked, 1)
            dve.wait_ge(f_pe, PE_OUT)
            dve.tensor_tensor(x_tok[:, :, :], ps[:, 2:4, :].rearrange("p b (t d) -> p (b t) d", d=D), x_tok[:, :, :],
                              ALU.add).then_inc(f_x, 1)

            dve.wait_ge(f_x, 1)
            layernorm(3, x_tok, xn)
            turned(3, xn_t)
            dve.wait_ge(in_c, 80)

            def q_lo(n):
                dve.wait_ge(c_qhi, n + 1)
                dve.tensor_tensor(halves(q_max[HD:P, :]), ps[HD:P, B_KP:B_AUX + 1, :], halves(f32(q_max[HD:P, :])),
                                  ALU.subtract).then_inc(c_qlo, 1)

            def k_lo(g, kn):
                dve.wait_ge(c_khi, kn)
                dve.tensor_tensor(keys_hl[0:HD, bass.ds(g * CH, CH), 1, :],
                                  ps[0:HD, B_KP, 0:CK].rearrange("p (n k) -> p n k", k=KT),
                                  f32(keys_hl[0:HD, bass.ds(g * CH, CH), 0, :]), ALU.subtract).then_inc(c_klo, 1)

            def chunk_maxima(i, g, kn, banks):
                dve.wait_ge(max_scored[i], kn)
                dve.tensor_reduce(chunk_max[:, i, bass.ds(g, 1)], ps[:, banks[i % len(banks)], 0:CK], AX,
                                  ALU.max).then_inc(max_reduced[i], 1)

            def fill1(n, j):
                dve.tensor_copy(kslot[:, j, :, :].rearrange("p a k -> p (a k)"),
                                f32(keys_hl[:, bass.ds(n, 1), :, :]).rearrange("p n a k -> p (n a k)")
                                ).then_inc(slot_keys[j], 1)

            def add_output(h, part, banks):
                dve.wait_ge(c_out, 2 * h - 1 + part)
                for t in range(4 * part, 4 * part + 4):
                    ins = dve.scalar_tensor_tensor(out=x_tok[:, t, :], in0=ps[:, banks[part], tile_cols(t % 4)],
                                                   scalar=rden[:, t:t + 1], in1=x_tok[:, t, :],
                                                   op0=ALU.mult, op1=ALU.add)
                ins.then_inc(c_x, 1)

            def reciprocals(h):
                dve.wait_ge(c_sums, h)
                dve.wait_ge(c_x, 2 * h - 2)
                dve.reciprocal(rden[:, :], ps[:, B_AUX, 2 * P:2 * P + TT]).then_inc(c_rden, 1)
                dve.wait_ge(c_rden, h)

            dve_zeros = zero_col[0:KT, :].to_broadcast([KT, HALF])

            def step(g, k, nxt, fill_at, output_of=None, first=False, banks=(3, 4, B_AUX), found=None):
                both1 = dve.snap(k + (CHUNKS + 1))
                if nxt:
                    both_kn = dve.snap(k + (2 * CHUNKS + 1))
                if fill_at is not None:
                    k2 = dve.snap(k + 2)
                for j in range(CH):
                    if fill_at is not None:
                        dve.wait_ge(scored[2 * j + 1], both1)
                        if j == 0:
                            dve.wait_ge(c_klo, k2)
                            dve.wait_ge(c_khi, k2)
                        fill1(fill_at + j, j)
                    if nxt and j == 0:
                        k_lo(g, both1)
                    maxima = ((0, 1), (2, 3, 4), (5, 6, 7))[j]
                    for i in maxima:
                        if nxt:
                            chunk_maxima(i, g, both_kn, banks)
                    if output_of is not None and j == 0:
                        reciprocals(output_of)
                    if output_of is not None and j:
                        add_output(output_of, j - 1, (B_AUX, B_AUX))
                    if j == 1 and not nxt:
                        dve.wait_ge(exped[3], both1)
                        dve.wait_ge(c_dadd, k)
                        dve.tensor_tensor(psum_dve, psum_dve if not first else dve_zeros, probs[:, 1, HALF:TOK],
                                          ALU.add).then_inc(c_dadd1, 1)
                    if j == CH - 1 and not nxt:
                        dve.wait_ge(c_dadd1, g + 1)
                    if j == CH - 1 and found is not None:
                        row_maxima(found)
                    if j == CH - 1 and found is None:
                        dve.wait_ge(exped[2 * CH - 1], both1)
                        if first and nxt:
                            dve.tensor_copy(psum_dve, probs[:, CH - 1, HALF:TOK]).then_inc(c_dadd, 1)
                        else:
                            dve.wait_ge(c_dadd, k)
                            dve.tensor_tensor(psum_dve, psum_dve, probs[:, CH - 1, HALF:TOK], ALU.add).then_inc(c_dadd, 1)

            def copy_wo(h, prev_index):
                dve.wait_ge(c_out, 2 * h - 2)
                dve.tensor_copy(wo_slot[:, :], wo1[:, bass.ds(prev_index, 1), :].rearrange("p a d -> p (a d)")).then_inc(c_wo, 1)

            def row_maxima(h):
                dve.wait_ge(max_reduced[TT - 1], (h + 2) * CHUNKS)
                dve.tensor_reduce(row_max[:, :], chunk_max[:, :, :], AX, ALU.max).then_inc(max_found, 1)

            def head(h, prev, nxt):
                if not prev:
                    row_maxima(0)
                slot = dve.snap(h % 2) if prev else 0
                dve.wait_ge(max_row, h + 2)
                for half in range(2):
                    tiles = TT // 2
                    dve.tensor_tensor(q_shift2[HD:HD + TT, bass.ds(slot, 1), cols(half)].rearrange("p a (t c) -> p (a t) c", c=P),
                                      ps[HD:HD + TT, B_MX, 0:P].unsqueeze(1).to_broadcast([TT, tiles, P]),
                                      diag[HD:HD + TT, half * tiles:(half + 1) * tiles].unsqueeze(2).to_broadcast([TT, tiles, P]),
                                      ALU.mult).then_inc(shifted, 1)
                if prev:
                    dve.wait_ge(c_acc, h)
                else:
                    dve.wait_ge(tr_dve, 4)
                dve.memset(ps[:, B_ACC, :], 0.0).then_inc(c_acczero, 1)
                if nxt:
                    q_lo(h + 1)
                if prev:
                    dve.wait_ge(exped[2 * CH - 1], (h + 1) * CHUNKS)
                    dve.wait_ge(c_dadd, h * CHUNKS - 1)
                    dve.tensor_tensor(psum_dve, psum_dve, probs[:, CH - 1, HALF:TOK], ALU.add).then_inc(c_dadd, 1)
                    copy_wo(h, h - 1)
                k0 = dve.snap(h * CHUNKS)
                step(0, k0, nxt, CH, output_of=h if prev else None, first=True, banks=(3, 4))
                with dve.Fori(0, TURNS) as n:
                    for u in range(UNROLL):
                        g = dve.snap(n * UNROLL + (u + 1))
                        step(g, dve.snap(k0 + g), nxt, dve.snap(g * CH + CH))
                step(CHUNKS - 1, dve.snap(k0 + (CHUNKS - 1)), nxt, 0 if nxt else None, found=h + 1 if nxt else None)

            q_lo(0)
            with dve.Fori(0, CHUNKS) as g:
                both1 = dve.snap(g + (CHUNKS + 1))
                for i in range(TT):
                    chunk_maxima(i, g, both1, (0, 1, 2, B_AUX))
            dve.wait_ge(c_rows, 4)
            dve.wait_ge(c_klo, CHUNKS)
            for j in range(CH):
                dve.wait_ge(scored[2 * j + 1], CHUNKS)
                fill1(j, j)
            for j in range(CH):
                dve.wait_ge(a_vout[j], 16 * CHUNKS)
            dve.tensor_tensor(x_tok[:, :, :], x_tok[:, :, :], bo1[:, :].unsqueeze(1).to_broadcast([P, TT, D]),
                              ALU.add).then_inc(f_x, 1)
            dve.wait_ge(f_x, 2)
            head(0, False, True)
            with dve.Fori(1, HEADS - 1) as h:
                head(h, True, True)
            head(HEADS - 1, True, False)
            copy_wo(HEADS, HEADS - 1)
            reciprocals(HEADS)
            for part in range(2):
                add_output(HEADS, part, (3, 4))

            dve.wait_ge(c_x, 2 * HEADS)
            layernorm(4, x_tok, xn)
            turned(4, xn_t)
            steps = [0]

            def link(ins):
                steps[0] += 1
                ins.then_inc(g_step, 1)
                dve.wait_ge(g_step, steps[0])

            dve.wait_ge(g_logits, 1)
            logits = ps[:, 0, 0:TT * E1].rearrange("p (t e) -> p t e", e=E1)

            def over(col, *shape):
                return col.unsqueeze(len(shape)).to_broadcast([P, *shape])

            dve.wait_ge(in_f1, 16 * 5)
            link(dve.tensor_tensor(gl, logits, gb[:, :].unsqueeze(1).to_broadcast([P, TT, E1]), ALU.add))
            link(dve.tensor_reduce(gm, gl, AX, ALU.max))
            dve.tensor_tensor(gp, gl, over(gm, TT, E1), ALU.subtract).then_inc(g_exp, 1)
            turned(5, x3_t)
            dve.wait_ge(g_exp, 2)
            link(dve.tensor_reduce(gs, gp, AX, ALU.add))
            link(dve.reciprocal(gm, gs))
            link(dve.tensor_tensor(gl, gp, over(gm, TT, E1), ALU.mult))
            members = gl.rearrange("p t (g m) -> p t g m", m=E1 // GROUPS)
            dve.tensor_tensor(pmax, members[:, :, :, 0], members[:, :, :, 1], ALU.max)
            dve.tensor_tensor(pmin, members[:, :, :, 0], members[:, :, :, 1], ALU.min)
            dve.tensor_tensor(qmax, members[:, :, :, 2], members[:, :, :, 3], ALU.max)
            link(dve.tensor_tensor(qmin, members[:, :, :, 2], members[:, :, :, 3], ALU.min))
            link(dve.tensor_tensor(pmin, pmin, qmin, ALU.max))
            link(dve.tensor_tensor(qmin, pmax, qmax, ALU.min))
            link(dve.tensor_tensor(pmax, pmax, qmax, ALU.max))
            link(dve.tensor_tensor(pmin, pmin, qmin, ALU.max))
            link(dve.tensor_tensor(pmax, pmax, pmin, ALU.add))

            def first_four(values, width, chosen):
                for t in range(TT):
                    ins = dve.max(top8[:, t, :], values[:, t, :])
                link(ins)
                for t in range(TT):
                    ins = dve.max_index(idx8[:, t, :], top8[:, t, :], values[:, t, :])
                link(ins)
                link(dve.tensor_copy(idxf8[:, :, :], idx8[:, :, :]))
                hits = ranks[:, 0:TT * TOPK * width].rearrange("p (t r e) -> p t r e", t=TT, r=TOPK)
                link(dve.tensor_tensor(hits, iota[:, 0:width].unsqueeze(1).unsqueeze(1).to_broadcast([P, TT, TOPK, width]),
                                       idxf8[:, :, 0:TOPK].unsqueeze(3).to_broadcast([P, TT, TOPK, width]), ALU.is_equal))
                link(dve.tensor_reduce(chosen, hits.rearrange("p t r e -> p t e r"), AX, ALU.add))


            def gated(m, s, half, m1, shared=False):
                dve.wait_ge(g_silu[half], m1)
                if not shared:
                    dve.wait_ge(g_y[half], m)
                ins = dve.scalar_tensor_tensor(out=hgate[:, half, :], in0=ps[:, 2 + half, :],
                                               scalar=pair_w[:, s, 3 * P + 1:3 * P + 2], in1=silu[:, half, :],
                                               op0=ALU.add, op1=ALU.mult)
                ins.then_inc(g_h[half], 1)
                if not shared:
                    dve.wait_ge(g_h[half], m1)
                    dve.wait_ge(g_gate[half], m)
                    dve.tensor_tensor(hgate[:, half, :], ps[:, 4 + half, :], hgate[:, half, :],
                                      ALU.mult).then_inc(g_hg[half], 1)

            first_four(pmax, GROUPS, keep)
            for half in range(2):
                gated(0, 0, half, 1, shared=True)
            link(dve.tensor_scalar(keep, keep, 2.0, -2.0, ALU.mult, ALU.add))
            link(dve.tensor_tensor(gp.rearrange("p t (g m) -> p t g m", m=E1 // GROUPS), members,
                                   over(keep, TT, GROUPS, E1 // GROUPS), ALU.add))
            first_four(gp, E1, cw)
            dve.tensor_tensor(cw, cw, gl, ALU.mult).then_inc(g_cw, 1)
            dve.wait_ge(g_cwtsb, 1)
            link(dve.tensor_copy(cw_3[0:E1, :], cw_t))
            link(dve.tensor_tensor(cw_r, cw_t, cw_3[0:E1, :], ALU.subtract))
            link(dve.tensor_copy(cw_b[:, :], cw_r))
            link(dve.tensor_copy(cw_3[E1:2 * E1, :], cw_b[:, :]))
            link(dve.tensor_tensor(cw_r, cw_r, cw_b[:, :], ALU.subtract))
            dve.tensor_copy(cw_3[2 * E1:3 * E1, :], cw_r).then_inc(g_spread_ready, 1)

            with dve.Fori(0, G1 // 2) as i:
                m = [dve.snap(2 * i + n) for n in (1, 2, 3)]
                for n in range(2):
                    for half in range(2):
                        gated(m[n], 1 - n, half, m[n + 1])
            for half in range(2):
                dve.wait_ge(g_y[half], G1 + 1)
                dve.scalar_tensor_tensor(out=x3_t[:, cols(half)], in0=ps[:, 6 + half, :], scalar=sb2[:, :],
                                         in1=x3_t[:, cols(half)], op0=ALU.add, op1=ALU.add).then_inc(g_fin[half], 1)

        @block.tensor
        def _(pe):
            def turn(n, src, layernorm=None):
                for t in range(TT):
                    if layernorm is not None:
                        pe.wait_ge(ln_out, layernorm * TT + t + 1)
                    ins = pe.transpose(ps[:, 6 + t // 4, tile_cols(t % 4)], src[:, t, :], ident[:, :])
                    if t % 4 == 3:
                        ins.then_inc(tr_psum, 1)

            def turned(n):
                pe.wait_ge(tr_act, n + 1)
                pe.wait_ge(tr_dve, n + 1)

            pe.wait_ge(in_x, 32)
            turn(0, xn, 0)
            turned(0)
            pe.wait_ge(in_a, 16 * 6)
            for half in range(2):
                pe.matmul(ps[:, 3 + half, :], wq0[:, :], xn_t[:, cols(half)], start=True, stop=True).then_inc(a_q, 1)
            pe.wait_ge(a_qsb, 1)
            for half in range(2):
                pe.matmul(ps[0:CD + 1, half, :], wkt0[:, :], q0_t[:, cols(half)], start=True, stop=True).then_inc(a_q, 1)
            pe.wait_ge(a_qhi, 1)
            pe.wait_ge(a_chi, CH)
            pe.wait_ge(a_rows, 7)
            pe.wait_ge(a_qlo, 1)
            pe.wait_ge(a_wvs, 2)
            with pe.Fori(0, CHUNKS) as g:
                k1 = pe.snap(g + 1)
                for i in range(TT):
                    pe.wait_ge(max_reduced[(i - 4) % TT], k1 if i >= 4 else g)
                    pe.matmul(ps[:, i % 4, 0:CK], q_max[0:CD + 1, tile_cols(i)],
                              keys_hl[0:CD + 1, bass.ds(g * CH, CH), 0, :], start=True, stop=True).then_inc(max_scored[i], 1)
                    if i in (2, 4, 6):
                        j = i // 2 - 1
                        pe.wait_ge(a_vkeys[j], k1)
                        pe.wait_ge(a_vevac[j], g)
                        v = ps[0:KT, 4 + j, :]
                        pe.matmul(v, kslot[0:CD, j, 0, :], wv1_hi[0:CD, :], start=True, stop=False)
                        pe.matmul(v, kslot[0:CD, j, 0, :], wv1_lo[0:CD, :], start=False, stop=False)
                        pe.matmul(v, kslot[0:CD, j, 1, :], wv1_hi[0:CD, :], start=False, stop=True).then_inc(a_vproj[j], 1)

            pe.wait_ge(max_found, 1)
            pe.wait_ge(neg_ready, 1)
            pe.wait_ge(a_vevac[0], CHUNKS)
            for t in range(TT):
                ins = pe.matmul(ps[CD:CD + 1, B_MX + t // 4, tile_cols(t % 4)], row_max[:, t:t + 1], neg_ident[:, :],
                                start=True, stop=True)
            ins.then_inc(max_row, 1)

            def scores0(jj, kv, kp):
                pe.wait_ge(slot_keys[jj], kv)
                for half in range(2):
                    u = 2 * jj + half
                    pe.wait_ge(exped[u], kp)
                    s = ps[0:KT, u, :]
                    pe.matmul(s, kslot[0:CD + 1, jj, 0, :], q_shift[0:CD + 1, cols(half)], start=True, stop=False)
                    pe.matmul(s, kslot[0:CD, jj, 0, :], q_all[0:CD, cols(half)], start=False, stop=False)
                    pe.matmul(s, kslot[0:CD + 1, jj, 1, :], q_pad[0:CD + 1, cols(half)], start=False,
                              stop=True).then_inc(scored[u], 1)

            def attend0(j, k1):
                pe.wait_ge(c_vslot[j], k1)
                for half in range(2):
                    o = ps[0:CD + 1, 6 + half, :]
                    pe.wait_ge((a_plo0, c_padd)[half][j], k1)
                    pe.matmul(o, rows_hi[:, j, :], p_hi[:, cols(half)], start=False, stop=False, skip_group_check=True)
                    pe.matmul(o, rows_lo[:, j, :], p_hi[:, cols(half)], start=False, stop=False, skip_group_check=True)
                    pe.matmul(o, rows_hi[:, j, :], p_lo[:, cols(half)], start=False, stop=False,
                              skip_group_check=True).then_inc((a_av0, attended)[half][j], 1)

            pe.wait_ge(shifted, 1)
            pe.wait_ge(a_qcopy, 2)
            pe.wait_ge(a_acczero, 1)
            pe.wait_ge(a_vevac[CH - 1], CHUNKS)

            def chunk0(k, k1, k2):
                scores0(2, k1, k)
                attend0(0, k1)
                if k2 is not None:
                    scores0(0, k2, k1)
                attend0(1, k1)
                if k2 is not None:
                    scores0(1, k2, k1)
                attend0(2, k1)

            scores0(0, 1, 0)
            scores0(1, 1, 0)
            with pe.Fori(0, CHUNKS - 1) as g:
                chunk0(g, pe.snap(g + 1), pe.snap(g + 2))
            chunk0(CHUNKS - 1, CHUNKS, None)
            pe.wait_ge(a_o, 2)
            for t in range(TT):
                ins = pe.matmul(ps[:, t % 4, (t // 4) * 256:(t // 4) * 256 + D + 1], o0[:, tile_cols(t)], wv0[:, :],
                                start=True, stop=True)
            ins.then_inc(a_out, 1)

            pe.wait_ge(f_w, 2)
            pe.wait_ge(consts, 3)
            for g in range(G0):
                ins = pe.matmul(ps[:, 5, g:g + 1], w1b[:, tile_cols(g)], ones[:, 0:1], start=True, stop=True)
            ins.then_inc(f_pe, 1)
            turn(1, xn, 1)
            turned(1)
            pe.wait_ge(in_f0, 16 * 9)
            for t in range(TT):
                ins = pe.matmul(ps[:, 4, t * E0:(t + 1) * E0], xn_t[:, tile_cols(t)], wgt, start=True, stop=True)
            ins.then_inc(f_pe, 1)
            turn(2, xn2, 2)
            turned(2)
            pe.wait_ge(a_x, 1)
            pe.wait_ge(f_step, 1)
            pe.wait_ge(f_biassb, 1)

            def hidden(n):
                g, half = n // 2, n % 2
                pe.matmul(ps[:, 2 + n, :], w1s[:, tile_cols(g)], xn_t[:, cols(half)], start=True, stop=True).then_inc(f_pe, 1)

            for n in range(2):
                hidden(n)
            pe.wait_ge(f_mask, 1)
            for t in range(TT):
                ins = pe.transpose(ps[0:E0, t // 4, tile_cols(t % 4)], mask0[:, t, :], ident[:, :])
            ins.then_inc(f_pe, 1)
            for n in range(2, 2 * G0):
                hidden(n)
            pe.wait_ge(f_masktsb, 1)
            for n in range(2 * G0):
                g, half = n // 2, n % 2
                pe.matmul(ps[:, (6 + n) % 8, :], spread0[:, g, :], mask_t[:, cols(half)], start=True, stop=True).then_inc(f_pe, 1)
            pe.wait_ge(f_masked, 2 * G0)
            for t in range(TT):
                o = ps[:, 2 + t // 4, tile_cols(t % 4)]
                for g in range(G0):
                    pe.matmul(o, hid0[:, g, tile_cols(t)], w2_0[:, g, :], start=(g == 0), stop=False)
                ins = pe.matmul(o, mask_t[:, tile_cols(t)], b2_0[:, :], start=False, stop=True)
            ins.then_inc(f_pe, 1)

            turn(3, xn, 3)
            turned(3)
            pe.wait_ge(in_c, 80)

            def q_proj(half):
                ins = pe.matmul(ps[:, Q_BANKS[half], :], wq1[:, :], xn_t[:, cols(half)], start=True, stop=True)
                if half == 1:
                    ins.then_inc(c_qproj, 1)

            def k_proj(g, kb):
                pe.wait_ge(c_klo, kb)
                pe.matmul(ps[:, B_KP, 0:CK], wk1[:, :], ctx_f[:, bass.ds(g * CK, CK)], start=True, stop=True).then_inc(c_kp, 1)

            def max_scores(i, g, kn, both_kn, both_kb, banks):
                if i == 0:
                    pe.wait_ge(c_khi, kn)
                if i >= len(banks):
                    pe.wait_ge(max_reduced[i - len(banks)], both_kn)
                elif both_kb is not None:
                    last = [n for n in range(TT) if n % len(banks) == i][-1]
                    pe.wait_ge(max_reduced[last], both_kb)
                pe.matmul(ps[:, banks[i % len(banks)], 0:CK], q_max[:, tile_cols(i)],
                          keys_hl[:, bass.ds(g * CH, CH), 0, :], start=True, stop=True).then_inc(max_scored[i], 1)

            def scores1(jj, kv, kp, slot, shift_of=None):
                pe.wait_ge(slot_keys[jj], kv)
                for half in range(2):
                    u = 2 * jj + half
                    pe.wait_ge(exped[(u + 3) % 6], kv if u >= 3 else kp)
                    if shift_of is not None:
                        pe.wait_ge(shifted, 2 * shift_of + 2 + half)
                    s = ps[0:KT, u % 3, :]
                    pe.matmul(s, kslot[:, jj, 0, :], flat(q_all2[:, bass.ds(slot, 1), cols(half)]), start=True, stop=False)
                    pe.matmul(s, kslot[0:CD + 1, jj, 1, :], flat(q_shift2[0:CD + 1, bass.ds(slot, 1), cols(half)]), start=False,
                              stop=True).then_inc(scored[u], 1)

            def attend1(j, both1):
                for half in range(2):
                    pe.wait_ge(exped[2 * j + half], both1)
                pe.wait_ge(c_vslot[j], both1)
                for half in range(2):
                    ins = pe.matmul(ps[half * HD:(half + 1) * HD, B_ACC, :], vslot[:, j, 0:HD],
                                    probs[:, j, cols(half)], start=False, stop=False, skip_group_check=True)
                ins.then_inc(attended[j], 1)

            def sum_rows(h):
                pe.wait_ge(c_total, h)
                for t in range(TT):
                    ins = pe.matmul(ps[:, B_AUX, 2 * P + t:2 * P + t + 1], psum_pool[:, tile_cols(t)], ones[0:KT, 0:1],
                                    start=True, stop=True)
                ins.then_inc(c_sums, 1)

            def project_out(h, part, bank, bias):
                if part == 0:
                    pe.wait_ge(c_acc, h)
                    pe.wait_ge(c_wo, h)
                    pe.wait_ge(c_rden, h)
                elif not bias:
                    pe.wait_ge(c_x, 2 * h - 1)
                rows = slice(part * HD, (part + 1) * HD)
                for u in range(4):
                    ins = pe.matmul(ps[:, bank, tile_cols(u)], acc_raw[rows, tile_cols(u)], wo_slot[rows, :],
                                    start=True, stop=True)
                ins.then_inc(c_out, 1)

            def step(slot, g, k, nxt, last=False, start_of=None, output_of=None, x_added=None, banks=(3, 4, B_AUX), tail=True, next_q=None):
                both = pe.snap(k + CHUNKS)
                both1 = pe.snap(k + (CHUNKS + 1))
                if nxt:
                    both_kb = pe.snap(k + 2 * CHUNKS) if len(banks) > 2 else None
                    both_kn = pe.snap(k + (2 * CHUNKS + 1))
                    if start_of is None:
                        k_proj(g, both)

                def maxima(*which):
                    for i in which:
                        if nxt:
                            max_scores(i, g, both1, both_kn, both_kb, banks)

                scores1(1, both1, both, slot)
                if start_of is not None:
                    pe.wait_ge(c_acczero, start_of + 1)
                    if nxt:
                        pe.wait_ge(c_qlo, start_of + 2)
                        k_proj(g, both)
                attend1(0, both1)
                maxima(0, 1)
                if output_of is not None:
                    sum_rows(output_of)
                scores1(2, both1, both, slot)
                if x_added is not None and nxt:
                    pe.wait_ge(c_x, x_added)
                maxima(2, 3)
                attend1(1, both1)
                if output_of is not None:
                    project_out(output_of, 0, B_AUX, False)
                maxima(4)
                if not last:
                    scores1(0, pe.snap(k + (CHUNKS + 2)), both1, slot)
                maxima(5, 6)
                if tail:
                    attend1(2, both1)
                if output_of is not None:
                    project_out(output_of, 1, B_AUX, False)
                if next_q is not None:
                    pe.wait_ge(c_wq, 16 * next_q)
                    pe.wait_ge(c_klo, next_q * CHUNKS)
                    q_proj(0)
                maxima(7)

            def head(h, prev, nxt, second=False):
                if nxt:
                    if not prev:
                        pe.wait_ge(c_wq, 16)
                        pe.wait_ge(c_klo, CHUNKS)
                        q_proj(0)
                    pe.wait_ge(c_wk, 16 * h + 16)
                    pe.wait_ge(max_reduced[5 if prev else 7], (h + 2) * CHUNKS)
                    q_proj(1)
                pe.wait_ge(max_found, h + 2)
                pe.matmul(ps[HD:HD + TT, B_MX, 0:P], row_max[:, :], neg_ident[:, :], start=True, stop=True).then_inc(max_row, 1)
                k0 = pe.snap(h * CHUNKS)
                slot = 0
                if prev:
                    slot = pe.snap(h % 2)
                    attend1(CH - 1, pe.snap(k0 + CHUNKS))
                both, both1 = pe.snap(k0 + CHUNKS), pe.snap(k0 + (CHUNKS + 1))
                pe.wait_ge(c_qcopy, 2 * h + 2)
                scores1(0, both1, both, slot, shift_of=h)
                step(slot, 0, k0, nxt, start_of=h, output_of=h if prev else None, banks=(3, 4))
                x_added = pe.snap(2 * h) if prev else None
                with pe.Fori(0, TURNS) as n:
                    for u in range(UNROLL):
                        g = pe.snap(n * UNROLL + (u + 1))
                        step(slot, g, pe.snap(k0 + g), nxt, x_added=x_added)
                step(slot, CHUNKS - 1, pe.snap(k0 + (CHUNKS - 1)), nxt, last=True, tail=not nxt,
                     next_q=h + 2 if nxt and second else None)

            for half in range(2):
                q_proj(half)
            pe.wait_ge(c_qlo, 1)
            k_proj(0, 0)

            def first_maxima(g, k1, both0, both1, last):
                for i in range(TT):
                    max_scores(i, g, k1, both1, both0, (0, 1, 2, B_AUX))
                    if i == 3 and not last:
                        k_proj(g + 1, k1)

            with pe.Fori(0, CHUNKS - 1) as g:
                first_maxima(g, pe.snap(g + 1), pe.snap(g + CHUNKS), pe.snap(g + (CHUNKS + 1)), False)
            first_maxima(CHUNKS - 1, CHUNKS, 2 * CHUNKS - 1, 2 * CHUNKS, True)
            pe.wait_ge(c_rows, 4)
            head(0, False, True, second=True)
            with pe.Fori(1, HEADS - 2) as h:
                head(h, True, True, second=True)
            head(HEADS - 2, True, True)
            head(HEADS - 1, True, False)
            pe.wait_ge(c_x, 2 * HEADS - 2)
            sum_rows(HEADS)
            for part in range(2):
                project_out(HEADS, part, 3 + part, True)

            turn(4, xn, 4)
            turned(4)
            pe.wait_ge(in_f1, 16 * 5)
            for t in range(TT):
                o = ps[:, 0, t * E1:(t + 1) * E1]
                ins = pe.matmul(o, xn_t[:, tile_cols(t)], gw[:, :], start=True, stop=True)
            ins.then_inc(g_logits, 1)
            turn(5, x_tok)

            def up(m, s, half, m1, shared=False):
                pe.wait_ge(g_wlo, m1)
                if not shared:
                    pe.wait_ge(g_h[half], m)
                for w in range(2):
                    o = ps[:, 2 * w + half, :]
                    hi, lo = w_parts[:, s, 0, tile_cols(w)], w_parts[:, s, 1, tile_cols(w)]
                    pe.matmul(o, hi, x_hi[:, cols(half)], start=True, stop=False)
                    pe.matmul(o, hi, x_lo[:, cols(half)], start=False, stop=False)
                    ins = pe.matmul(o, lo, x_hi[:, cols(half)], start=False, stop=True)
                ins.then_inc(g_u[half], 1)

            def gate(pair, half):
                pe.wait_ge(g_hg[half], pair)
                pe.matmul(ps[:, 4 + half, :], spread1[:, bass.ds(pair, 1), :].rearrange("p a c -> p (a c)"),
                          cw_3[:, cols(half)], start=True, stop=True).then_inc(g_gate[half], 1)

            def down(s, half, ready, count, start=False, stop=False):
                pe.wait_ge(ready[half], count)
                pe.matmul(ps[:, 6 + half, :], pair_w[:, s, 2 * P:3 * P], hgate[:, half, :], start=start, stop=stop,
                          skip_group_check=True).then_inc(g_y[half], 1)

            pe.wait_ge(g_step, 1)
            pe.wait_ge(g_xs, 2)
            for half in range(2):
                up(0, 0, half, 1, shared=True)
            turned(5)
            for half in range(2):
                down(0, half, g_h, 1, start=True)
            up(1, 1, 0, 2)
            pe.wait_ge(g_cw, 1)
            for t in range(TT):
                ins = pe.transpose(ps[0:E1, 4 + t // 4, tile_cols(t % 4)], cw[:, t, :], ident[:, :])
            ins.then_inc(g_cwt, 1)
            pe.wait_ge(g_cwtsb, 1)
            for half in range(2):
                pe.matmul(ps[:, 6 + half, :], b2_1[:, :], cw_t[:, cols(half)], start=False, stop=False, skip_group_check=True)
            pe.wait_ge(g_spread_ready, 1)
            gate(0, 0)

            def two_pairs(i, last):
                m1, m2 = pe.snap(2 * i + 1), pe.snap(2 * i + 2)
                m3 = pe.snap(2 * i + 3)
                up(m1, 1, 1, m2)
                gate(m1 - 1, 1)
                down(1, 0, g_hg, m1)
                up(m2, 0, 0, m3)
                gate(m1, 0)
                down(1, 1, g_hg, m1)
                up(m2, 0, 1, m3)
                gate(m1, 1)
                down(0, 0, g_hg, m2, stop=last)
                if not last:
                    up(m3, 1, 0, pe.snap(2 * i + 4))
                    gate(m2, 0)
                down(0, 1, g_hg, m2, stop=last)

            with pe.Fori(0, G1 // 2 - 1) as i:
                two_pairs(i, False)
            two_pairs(G1 // 2 - 1, True)


def kernel(**inputs):
    import numpy as np
    import concourse.bacc as bacc
    import ml_dtypes
    from concourse.bass_utils import run_bass_kernel_spmd

    a = {n: np.asarray(v) for n, v in inputs.items()}
    c = np.ascontiguousarray
    context = a["ctx_768"][0]
    context = np.concatenate([context, context[KEYS - (PADDED - KEYS):]], 0)
    w1, w3, w2 = a["L1_ffn_w1"], a["L1_ffn_w3"], a["L1_ffn_w2"]
    pairs = [np.concatenate([w1[2 * i], w1[2 * i + 1], w3[2 * i], w3[2 * i + 1],
                             w2[2 * i:2 * i + 2].reshape(P, D),
                             a["L1_ffn_b1"][2 * i:2 * i + 2].reshape(P, 1),
                             a["L1_ffn_b3"][2 * i:2 * i + 2].reshape(P, 1)], 1) for i in range(G1)]
    pairs.append(np.concatenate([a["L1_ffn_sw1"], a["L1_ffn_sw3"], a["L1_ffn_sw2"],
                                 a["L1_ffn_sb1"].reshape(P, 1), a["L1_ffn_sb3"].reshape(P, 1)], 1))
    wq = a["L1_xattn_Wq"].reshape(D, HEADS, HD).transpose(1, 0, 2)
    wk = a["L1_xattn_Wk"].reshape(CD, HEADS, HD).transpose(1, 0, 2)
    wo = a["L1_xattn_Wo"].reshape(HEADS, HD, D).transpose(1, 0, 2)
    spread0 = np.zeros((E0, G0, P), np.float32)
    for e in range(E0):
        spread0[e, e // EG0, (e % EG0) * H0:(e % EG0 + 1) * H0] = 1.0
    spread1 = np.zeros((3 * E1, G1, P), ml_dtypes.bfloat16)
    for e in range(E1):
        for part in range(3):
            spread1[part * E1 + e, e // 2, (e % 2) * H1:(e % 2 + 1) * H1] = 1.0
    arrays = {
        "x": a["x"][0],
        "ctx_rows": context,
        "ctx_t": context.T,
        "a_wq": a["L0_xattn_Wq"],
        "a_bq": a["L0_xattn_bq"].reshape(D, 1),
        "a_wkt": a["L0_xattn_Wk"].T,
        "a_bk": a["L0_xattn_bk"].reshape(D, 1),
        "a_wv": a["L0_xattn_Wv"],
        "a_bv": a["L0_xattn_bv"].reshape(1, D),
        "f0_wgt": a["L0_ffn_Wg"].T,
        "f0_scale": a["L0_ffn_ln_scale"].T,
        "f0_bias": a["L0_ffn_ln_bias"].T,
        "f0_w1": a["L0_ffn_W1"].transpose(1, 0, 2).reshape(D, E0 * H0),
        "f0_b1": a["L0_ffn_b1"].reshape(G0, P).T,
        "f0_w2": a["L0_ffn_W2"].reshape(G0, P, D).transpose(1, 0, 2),
        "f0_b2": a["L0_ffn_b2"],
        "c_wq": np.concatenate([wq, wq], 2),
        "c_wk": np.concatenate([wk, wk], 2),
        "c_wv": a["L1_xattn_Wv"],
        "c_wo": np.concatenate([wo, wo], 0),
        "c_bo": np.tile(a["L1_xattn_bo"], (P, 1)),
        "f1_gw": a["L1_ffn_gw"],
        "f1_gb": np.tile(a["L1_ffn_gb"], (P, 1)),
        "f1_pairs": np.stack(pairs[-1:] + pairs[:-1]),
        "f1_b2": a["L1_ffn_b2"],
        "f1_sb2": a["L1_ffn_sb2"].reshape(D, 1),
        "ident": np.eye(P, dtype=np.float32),
        "iota": np.tile(np.arange(E1, dtype=np.float32), (P, 1)),
        "spread0": spread0,
        "spread1": spread1,
    }
    arrays = {f"in_{n}": c(v) for n, v in arrays.items()}
    nc = bacc.Bacc("TRN2", target_bir_lowering=False, num_devices=1)
    args = [nc.dram_tensor(n, v.shape, mybir.dt.from_np(v.dtype), kind="ExternalInput").ap() for n, v in arrays.items()]
    out_t = nc.dram_tensor("out_t", [D, TOK], F32, kind="ExternalOutput").ap()
    build_program(nc, *args, out_t)
    r = run_bass_kernel_spmd(nc, [arrays], core_ids=[0])
    return r.results[0]["out_t"].T.reshape(1, TOK, D)
```
